# Optimizing a Trainium2 kernel written in Bass

```python
import numpy as np
import jax
import jax.numpy as jnp

def _softmax(x, axis=-1):
    return jax.nn.softmax(x, axis=axis)

def _gelu(x):
    return jax.nn.gelu(x, approximate=True)

def _silu(x):
    return jax.nn.silu(x)

def _sigmoid(x):
    return jax.nn.sigmoid(x)

def _layernorm(x, axis=-1, eps=1e-05):
    m = jnp.mean(x, axis=axis, keepdims=True)
    v = jnp.var(x, axis=axis, keepdims=True)
    return (x - m) / jnp.sqrt(v + eps)

def _scatter_add(tgt, idx, src, axis=0):
    return tgt.at[idx].add(src)

def _segment_sum(src, seg, n):
    return jax.ops.segment_sum(src, seg, n)
kernel_name = 'mk_gnn_resnorm_d4_gnn_r32_a5bd3c'

def setup_inputs(seed: int=0):
    np.random.seed(seed)
    _w = jnp.asarray

    def _rec_inputs():
        import jax
        import jax.numpy as jnp
        _gk = jax.random.key(seed)
        x = -0.0009044 + 1 * jax.random.normal(jax.random.fold_in(_gk, 1), (50000, 160), jnp.float32)
        src = jax.random.randint(jax.random.fold_in(_gk, 2), (50000,), 0, 50000, jnp.int32)
        dst = jax.random.randint(jax.random.fold_in(_gk, 3), (50000,), 0, 50000, jnp.int32)
        _o = jnp.argsort(dst, stable=True)
        src = src[_o]
        dst = dst[_o]
        edge_attr_10 = jax.random.uniform(jax.random.fold_in(_gk, 12), (50000, 10), jnp.float32, 0.0, 1)
        edge_attr_16 = -0.000191324 + 0.999809 * jax.random.normal(jax.random.fold_in(_gk, 13), (50000, 16), jnp.float32)
        edge_attr_3 = 0.00047201 + 1.00023 * jax.random.normal(jax.random.fold_in(_gk, 14), (50000, 3), jnp.float32)
        edge_attr_4 = 0.000126197 + 0.999763 * jax.random.normal(jax.random.fold_in(_gk, 15), (50000, 4), jnp.float32)
        edge_attr_64 = 0.000279952 + 1.00013 * jax.random.normal(jax.random.fold_in(_gk, 16), (50000, 64), jnp.float32)
        node_vec1 = jax.random.uniform(jax.random.fold_in(_gk, 18), (50000, 1), jnp.float32, 0.0, 1)
        node_vec1_n2 = jax.random.uniform(jax.random.fold_in(_gk, 19), (50000, 1), jnp.float32, 0.0, 1)
        node_vec1_n3 = jax.random.uniform(jax.random.fold_in(_gk, 20), (50000, 1), jnp.float32, 0.0, 1)
        return (x, src, dst, edge_attr_10, edge_attr_16, edge_attr_3, edge_attr_4, edge_attr_64, node_vec1, node_vec1_n2, node_vec1_n3)
    x, src, dst, edge_attr_10, edge_attr_16, edge_attr_3, edge_attr_4, edge_attr_64, node_vec1, node_vec1_n2, node_vec1_n3 = _rec_inputs()

    def _L0_gnn_setup():
        import jax, jax.numpy as jnp
        import numpy as np
        N_NODES = 10000
        N_EDGES = 10000
        MUL0, MUL1 = (64, 32)
        EDGE_DIM = 64
        W_NUMEL = 224
        DENOM = 32.0
        SQRT3 = 3.0 ** 0.5
        INV_SQRT3 = 1.0 / SQRT3
        INV_SQRT2 = 2.0 ** (-0.5)

        def _forward(node_feature, edge_attr, edge_feature, W_skip0, W_skip1, W_nl0, W_nl1, W_fc1, W_fc2, W_out_s, W_out_v, edge_index):
            N = node_feature.shape[0]
            E = edge_attr.shape[0]
            s = node_feature[:, :MUL0]
            v = node_feature[:, MUL0:].reshape(N, MUL1, 3)
            skip_s = s @ W_skip0
            skip_v = jnp.einsum('nmi,mk->nki', v, W_skip1)
            s = s @ W_nl0
            v = jnp.einsum('nmi,mk->nki', v, W_nl1)
            rhat = edge_attr / jnp.linalg.norm(edge_attr, axis=-1, keepdims=True)
            sh1 = SQRT3 * rhat
            w = jax.nn.relu(edge_feature @ W_fc1) @ W_fc2
            w0, w1, w2, w3, w4 = jnp.split(w, [64, 128, 160, 192], axis=-1)
            src, dst = (edge_index[0], edge_index[1])
            xs = s[dst]
            xv = v[dst]
            out0a = w0 * xs
            out0b = w3 * (jnp.einsum('emi,ei->em', xv, sh1) * INV_SQRT3)
            out1a = (w1 * xs)[:, :, None] * sh1[:, None, :]
            out1b = w2[:, :, None] * xv
            out1c = w4[:, :, None] * (jnp.cross(xv, sh1[:, None, :]) * INV_SQRT2)
            tp = jnp.concatenate([out0a, out0b, out1a.reshape(E, -1), out1b.reshape(E, -1), out1c.reshape(E, -1)], axis=-1)
            agg = jax.ops.segment_sum(tp, src, num_segments=N) / DENOM
            agg_s = agg[:, :96]
            agg_v = agg[:, 96:].reshape(N, 128, 3)
            out_s = agg_s @ W_out_s + skip_s
            out_v = jnp.einsum('nmi,mk->nki', agg_v, W_out_v) + skip_v
            fs = jax.nn.silu(out_s[:, :MUL0])
            gate = jax.nn.sigmoid(out_s[:, MUL0:MUL0 + 32])
            gv = gate[:, :, None] * out_v
            return jnp.concatenate([fs, gv.reshape(N, -1)], axis=-1)
        key = jax.random.key(seed)
        ks = jax.random.split(key, 12)

        def lin(k, fi, fo):
            return jax.random.normal(k, (fi, fo), jnp.float32) / np.float32(np.sqrt(fi))
        return {'node_feature': jax.random.normal(ks[0], (N_NODES, MUL0 + 3 * MUL1), jnp.float32), 'edge_attr': jax.random.normal(ks[1], (N_EDGES, 3), jnp.float32), 'edge_feature': jax.random.normal(ks[2], (N_EDGES, EDGE_DIM), jnp.float32), 'W_skip0': lin(ks[3], MUL0, 96), 'W_skip1': lin(ks[4], MUL1, 32), 'W_nl0': lin(ks[5], MUL0, MUL0), 'W_nl1': lin(ks[6], MUL1, MUL1), 'W_fc1': lin(ks[7], EDGE_DIM, 64), 'W_fc2': lin(ks[8], 64, W_NUMEL), 'W_out_s': lin(ks[9], 96, 96), 'W_out_v': lin(ks[10], 128, 32), 'edge_index': jax.random.randint(ks[11], (2, N_EDGES), 0, N_NODES)}
    _L0_gnn_all = _L0_gnn_setup()
    _L0_gnn_in = {k: v for k, v in _L0_gnn_all.items() if k in ('W_skip0', 'W_skip1', 'W_nl0', 'W_nl1', 'W_fc1', 'W_fc2', 'W_out_s', 'W_out_v')}
    del _L0_gnn_all

    def _L1_gnn_setup():
        import jax, jax.numpy as jnp
        import numpy as np
        N = 625
        E = 10000
        MUL0 = 64
        MUL1 = 32
        FC_IN = 16
        FC_H = 64
        WNUM = 192
        key = jax.random.key(seed)
        ks = jax.random.split(key, 16)
        return {'x': jax.random.normal(ks[0], (N, MUL0 + 3 * MUL1), jnp.float32), 'node_attr': jnp.ones((N, 1), jnp.float32), 'edge_scalars': jax.random.normal(ks[1], (E, FC_IN), jnp.float32), 'edge_attr_sh': jax.random.normal(ks[2], (E, 4), jnp.float32), 'edge_src': jax.random.randint(ks[3], (E,), 0, N), 'edge_dst': jax.random.randint(ks[4], (E,), 0, N), 'Wfc1': jax.random.normal(ks[5], (FC_IN, FC_H), jnp.float32), 'Wfc2': jax.random.normal(ks[6], (FC_H, WNUM), jnp.float32), 'Wsc0': jax.random.normal(ks[7], (MUL0, MUL0), jnp.float32), 'Wsc1': jax.random.normal(ks[8], (MUL1, MUL1), jnp.float32), 'Wl1_0': jax.random.normal(ks[9], (MUL0, MUL0), jnp.float32), 'Wl1_1': jax.random.normal(ks[10], (MUL1, MUL1), jnp.float32), 'Wl2_s': jax.random.normal(ks[11], (MUL0 + MUL1, MUL0), jnp.float32), 'Wl2_v': jax.random.normal(ks[12], (MUL0 + MUL1, MUL1), jnp.float32), 'Wa': 0.1 * jax.random.normal(ks[13], (MUL0 + MUL1, 1), jnp.float32)}
    _L1_gnn_all = _L1_gnn_setup()
    _L1_gnn_in = {k: v for k, v in _L1_gnn_all.items() if k in ('Wfc1', 'Wfc2', 'Wsc0', 'Wsc1', 'Wl1_0', 'Wl1_1', 'Wl2_s', 'Wl2_v', 'Wa')}
    del _L1_gnn_all

    def _L2_gnn_setup():
        import jax, jax.numpy as jnp
        import numpy as np
        N = 25000
        E = 12500
        S = 64
        V = 32
        NB = 10
        H = 100
        WN = 192
        MID = 96
        NUM_NEIGHBORS = 16.0
        C_S = float(np.sin(np.pi / 8.0))
        C_X = float(np.cos(np.pi / 8.0))
        SQRT3 = float(np.sqrt(3.0))

        def fctp_scalar_attr(xs, xv, attr, Ws, Wv):
            s = xs * attr @ Ws
            v = jnp.einsum('nuc,uo->noc', xv * attr[:, :, None], Wv)
            return (s, v)
        key = jax.random.key(seed)
        k = jax.random.split(key, 24)

        def w(i, shape):
            return jax.random.normal(k[i], shape, jnp.float32) / np.sqrt(float(shape[0]))
        return {'node_input': jax.random.normal(k[0], (N, S + 3 * V), jnp.float32), 'node_attr': jax.random.normal(k[1], (N, 1), jnp.float32), 'node_crystal_attr': jax.random.normal(k[2], (N, 1), jnp.float32), 'sym_mask': jax.random.normal(k[3], (N, 1), jnp.float32), 'edge_attr': jax.random.normal(k[4], (E, 4), jnp.float32), 'edge_length_embedded': jax.random.uniform(k[5], (E, NB), dtype=jnp.float32), 'edge_src': jax.random.randint(k[6], (E,), 0, N), 'edge_dst': jax.random.randint(k[7], (E,), 0, N), 'Ws_sc_a': w(8, (S, S)), 'Wv_sc_a': w(9, (V, V)), 'Ws_sc_c': w(10, (S, S)), 'Wv_sc_c': w(11, (V, V)), 'Ws_l1_a': w(12, (S, S)), 'Wv_l1_a': w(13, (V, V)), 'Ws_l1_c': w(14, (S, S)), 'Wv_l1_c': w(15, (V, V)), 'W_fc1': w(16, (NB, H)), 'W_fc2': w(17, (H, WN)), 'Ws_l2_a': w(18, (MID, MID)), 'Wv_l2_a': w(19, (MID, MID)), 'Ws_l2_c': w(20, (MID, MID)), 'Wv_l2_c': w(21, (MID, MID)), 'Ws_l3': w(22, (MID, S)), 'Wv_l3': w(23, (MID, V))}
    _L2_gnn_all = _L2_gnn_setup()
    _L2_gnn_in = {k: v for k, v in _L2_gnn_all.items() if k in ('Ws_sc_a', 'Wv_sc_a', 'Ws_sc_c', 'Wv_sc_c', 'Ws_l1_a', 'Wv_l1_a', 'Ws_l1_c', 'Wv_l1_c', 'W_fc1', 'W_fc2', 'Ws_l2_a', 'Wv_l2_a', 'Ws_l2_c', 'Wv_l2_c', 'Ws_l3', 'Wv_l3')}
    del _L2_gnn_all

    def _L3_gnn_setup():
        import jax, jax.numpy as jnp
        import numpy as np
        N, E = (1250, 20000)
        S_IN, V_IN = (64, 32)
        S_MID, V_MID = (96, 128)
        S_OUT, V_OUT = (96, 32)
        R = 64
        FC_HID = 64
        W_NUMEL = 64 + 64 + 32 + 32 + 32
        NUM_NEIGHBORS = 16.0

        def _inv(d):
            return 1.0 / jnp.sqrt(jnp.float32(d))

        def _forward(node_features, node_attr, edge_attr, edge_scalars, lin1_ws, lin1_wv, fc_w1, fc_w2, sc_ws, sc_wv, lin2_ws, lin2_wv, edge_src, edge_dst):
            n = node_features.shape[0]
            s = node_features[:, :S_IN]
            v = node_features[:, S_IN:].reshape(n, V_IN, 3)
            a = node_attr
            sc_s = s @ sc_ws * a * _inv(S_IN)
            sc_v = jnp.einsum('nci,cd->ndi', v, sc_wv) * a[:, :, None] * _inv(V_IN)
            h_s = s @ lin1_ws * a * _inv(S_IN)
            h_v = jnp.einsum('nci,cd->ndi', v, lin1_wv) * a[:, :, None] * _inv(V_IN)
            hid = jax.nn.silu(edge_scalars @ fc_w1 * _inv(R))
            w = hid @ fc_w2 * _inv(FC_HID)
            w1, w2, w3, w4, w5 = jnp.split(w, [64, 128, 160, 192], axis=-1)
            es = h_s[edge_src]
            ev = h_v[edge_src]
            e0 = edge_attr[:, :1]
            e1 = edge_attr[:, 1:4]
            m_s1 = w1 * es * e0
            m_s2 = w4 * jnp.einsum('eci,ei->ec', ev, e1) * _inv(3)
            m_v1 = (w2 * es)[:, :, None] * e1[:, None, :]
            m_v2 = w3[:, :, None] * ev * e0[:, :, None]
            m_v3 = w5[:, :, None] * jnp.cross(ev, e1[:, None, :]) * _inv(2)
            mid_s = jnp.concatenate([m_s1, m_s2], axis=-1)
            mid_v = jnp.concatenate([m_v1, m_v2, m_v3], axis=1)
            inv_nn = 1.0 / jnp.sqrt(jnp.float32(NUM_NEIGHBORS))
            agg_s = jax.ops.segment_sum(mid_s, edge_dst, num_segments=n) * inv_nn
            agg_v = jax.ops.segment_sum(mid_v, edge_dst, num_segments=n) * inv_nn
            o_s = agg_s @ lin2_ws * a * _inv(S_MID)
            o_v = jnp.einsum('nci,cd->ndi', agg_v, lin2_wv) * a[:, :, None] * _inv(V_MID)
            pre_s = sc_s + o_s
            pre_v = sc_v + o_v
            scalars = jax.nn.silu(pre_s[:, :64])
            gates = jax.nn.sigmoid(pre_s[:, 64:96])
            gated = gates[:, :, None] * pre_v
            return jnp.concatenate([scalars, gated.reshape(n, 3 * V_OUT)], axis=-1)
        key = jax.random.key(seed)
        ks = jax.random.split(key, 13)
        return {'node_features': jax.random.normal(ks[0], (N, S_IN + 3 * V_IN), jnp.float32), 'node_attr': jnp.ones((N, 1), jnp.float32), 'edge_src': jax.random.randint(ks[1], (E,), 0, N), 'edge_dst': jax.random.randint(ks[2], (E,), 0, N), 'edge_attr': jax.random.normal(ks[3], (E, 4), jnp.float32), 'edge_scalars': jax.random.normal(ks[4], (E, R), jnp.float32), 'lin1_ws': jax.random.normal(ks[5], (S_IN, S_IN), jnp.float32), 'lin1_wv': jax.random.normal(ks[6], (V_IN, V_IN), jnp.float32), 'fc_w1': jax.random.normal(ks[7], (R, FC_HID), jnp.float32), 'fc_w2': jax.random.normal(ks[8], (FC_HID, W_NUMEL), jnp.float32), 'sc_ws': jax.random.normal(ks[9], (S_IN, S_OUT), jnp.float32), 'sc_wv': jax.random.normal(ks[10], (V_IN, V_OUT), jnp.float32), 'lin2_ws': jax.random.normal(ks[11], (S_MID, S_OUT), jnp.float32), 'lin2_wv': jax.random.normal(ks[12], (V_MID, V_OUT), jnp.float32)}
    _L3_gnn_all = _L3_gnn_setup()
    _L3_gnn_in = {k: v for k, v in _L3_gnn_all.items() if k in ('lin1_ws', 'lin1_wv', 'fc_w1', 'fc_w2', 'sc_ws', 'sc_wv', 'lin2_ws', 'lin2_wv')}
    del _L3_gnn_all
    return {'x': x, 'src': src, 'dst': dst, 'edge_attr_10': edge_attr_10, 'edge_attr_16': edge_attr_16, 'edge_attr_3': edge_attr_3, 'edge_attr_4': edge_attr_4, 'edge_attr_64': edge_attr_64, 'node_vec1': node_vec1, 'node_vec1_n2': node_vec1_n2, 'node_vec1_n3': node_vec1_n3, 'L0_gnn_W_skip0': _L0_gnn_in['W_skip0'], 'L0_gnn_W_skip1': _L0_gnn_in['W_skip1'], 'L0_gnn_W_nl0': _L0_gnn_in['W_nl0'], 'L0_gnn_W_nl1': _L0_gnn_in['W_nl1'], 'L0_gnn_W_fc1': _L0_gnn_in['W_fc1'], 'L0_gnn_W_fc2': _L0_gnn_in['W_fc2'], 'L0_gnn_W_out_s': _L0_gnn_in['W_out_s'], 'L0_gnn_W_out_v': _L0_gnn_in['W_out_v'], 'L1_gnn_Wfc1': _L1_gnn_in['Wfc1'], 'L1_gnn_Wfc2': _L1_gnn_in['Wfc2'], 'L1_gnn_Wsc0': _L1_gnn_in['Wsc0'], 'L1_gnn_Wsc1': _L1_gnn_in['Wsc1'], 'L1_gnn_Wl1_0': _L1_gnn_in['Wl1_0'], 'L1_gnn_Wl1_1': _L1_gnn_in['Wl1_1'], 'L1_gnn_Wl2_s': _L1_gnn_in['Wl2_s'], 'L1_gnn_Wl2_v': _L1_gnn_in['Wl2_v'], 'L1_gnn_Wa': _L1_gnn_in['Wa'], 'L2_gnn_Ws_sc_a': _L2_gnn_in['Ws_sc_a'], 'L2_gnn_Wv_sc_a': _L2_gnn_in['Wv_sc_a'], 'L2_gnn_Ws_sc_c': _L2_gnn_in['Ws_sc_c'], 'L2_gnn_Wv_sc_c': _L2_gnn_in['Wv_sc_c'], 'L2_gnn_Ws_l1_a': _L2_gnn_in['Ws_l1_a'], 'L2_gnn_Wv_l1_a': _L2_gnn_in['Wv_l1_a'], 'L2_gnn_Ws_l1_c': _L2_gnn_in['Ws_l1_c'], 'L2_gnn_Wv_l1_c': _L2_gnn_in['Wv_l1_c'], 'L2_gnn_W_fc1': _L2_gnn_in['W_fc1'], 'L2_gnn_W_fc2': _L2_gnn_in['W_fc2'], 'L2_gnn_Ws_l2_a': _L2_gnn_in['Ws_l2_a'], 'L2_gnn_Wv_l2_a': _L2_gnn_in['Wv_l2_a'], 'L2_gnn_Ws_l2_c': _L2_gnn_in['Ws_l2_c'], 'L2_gnn_Wv_l2_c': _L2_gnn_in['Wv_l2_c'], 'L2_gnn_Ws_l3': _L2_gnn_in['Ws_l3'], 'L2_gnn_Wv_l3': _L2_gnn_in['Wv_l3'], 'L3_gnn_lin1_ws': _L3_gnn_in['lin1_ws'], 'L3_gnn_lin1_wv': _L3_gnn_in['lin1_wv'], 'L3_gnn_fc_w1': _L3_gnn_in['fc_w1'], 'L3_gnn_fc_w2': _L3_gnn_in['fc_w2'], 'L3_gnn_sc_ws': _L3_gnn_in['sc_ws'], 'L3_gnn_sc_wv': _L3_gnn_in['sc_wv'], 'L3_gnn_lin2_ws': _L3_gnn_in['lin2_ws'], 'L3_gnn_lin2_wv': _L3_gnn_in['lin2_wv']}

def reference(x, src, dst, edge_attr_10, edge_attr_16, edge_attr_3, edge_attr_4, edge_attr_64, node_vec1, node_vec1_n2, node_vec1_n3, L0_gnn_W_skip0, L0_gnn_W_skip1, L0_gnn_W_nl0, L0_gnn_W_nl1, L0_gnn_W_fc1, L0_gnn_W_fc2, L0_gnn_W_out_s, L0_gnn_W_out_v, L1_gnn_Wfc1, L1_gnn_Wfc2, L1_gnn_Wsc0, L1_gnn_Wsc1, L1_gnn_Wl1_0, L1_gnn_Wl1_1, L1_gnn_Wl2_s, L1_gnn_Wl2_v, L1_gnn_Wa, L2_gnn_Ws_sc_a, L2_gnn_Wv_sc_a, L2_gnn_Ws_sc_c, L2_gnn_Wv_sc_c, L2_gnn_Ws_l1_a, L2_gnn_Wv_l1_a, L2_gnn_Ws_l1_c, L2_gnn_Wv_l1_c, L2_gnn_W_fc1, L2_gnn_W_fc2, L2_gnn_Ws_l2_a, L2_gnn_Wv_l2_a, L2_gnn_Ws_l2_c, L2_gnn_Wv_l2_c, L2_gnn_Ws_l3, L2_gnn_Wv_l3, L3_gnn_lin1_ws, L3_gnn_lin1_wv, L3_gnn_fc_w1, L3_gnn_fc_w2, L3_gnn_sc_ws, L3_gnn_sc_wv, L3_gnn_lin2_ws, L3_gnn_lin2_wv):
    import jax
    import jax.numpy as jnp

    def _L0_gnn_ref(node_feature, edge_attr, edge_feature, W_skip0, W_skip1, W_nl0, W_nl1, W_fc1, W_fc2, W_out_s, W_out_v, edge_index):
        import jax, jax.numpy as jnp
        import numpy as np
        N_NODES = 10000
        N_EDGES = 10000
        MUL0, MUL1 = (64, 32)
        EDGE_DIM = 64
        W_NUMEL = 224
        DENOM = 32.0
        SQRT3 = 3.0 ** 0.5
        INV_SQRT3 = 1.0 / SQRT3
        INV_SQRT2 = 2.0 ** (-0.5)

        def _forward(node_feature, edge_attr, edge_feature, W_skip0, W_skip1, W_nl0, W_nl1, W_fc1, W_fc2, W_out_s, W_out_v, edge_index):
            N = node_feature.shape[0]
            E = edge_attr.shape[0]
            s = node_feature[:, :MUL0]
            v = node_feature[:, MUL0:].reshape(N, MUL1, 3)
            skip_s = s @ W_skip0
            skip_v = jnp.einsum('nmi,mk->nki', v, W_skip1)
            s = s @ W_nl0
            v = jnp.einsum('nmi,mk->nki', v, W_nl1)
            rhat = edge_attr / jnp.linalg.norm(edge_attr, axis=-1, keepdims=True)
            sh1 = SQRT3 * rhat
            w = jax.nn.relu(edge_feature @ W_fc1) @ W_fc2
            w0, w1, w2, w3, w4 = jnp.split(w, [64, 128, 160, 192], axis=-1)
            src, dst = (edge_index[0], edge_index[1])
            xs = s[dst]
            xv = v[dst]
            out0a = w0 * xs
            out0b = w3 * (jnp.einsum('emi,ei->em', xv, sh1) * INV_SQRT3)
            out1a = (w1 * xs)[:, :, None] * sh1[:, None, :]
            out1b = w2[:, :, None] * xv
            out1c = w4[:, :, None] * (jnp.cross(xv, sh1[:, None, :]) * INV_SQRT2)
            tp = jnp.concatenate([out0a, out0b, out1a.reshape(E, -1), out1b.reshape(E, -1), out1c.reshape(E, -1)], axis=-1)
            agg = jax.ops.segment_sum(tp, src, num_segments=N) / DENOM
            agg_s = agg[:, :96]
            agg_v = agg[:, 96:].reshape(N, 128, 3)
            out_s = agg_s @ W_out_s + skip_s
            out_v = jnp.einsum('nmi,mk->nki', agg_v, W_out_v) + skip_v
            fs = jax.nn.silu(out_s[:, :MUL0])
            gate = jax.nn.sigmoid(out_s[:, MUL0:MUL0 + 32])
            gv = gate[:, :, None] * out_v
            return jnp.concatenate([fs, gv.reshape(N, -1)], axis=-1)
        return _forward(node_feature, edge_attr, edge_feature, W_skip0, W_skip1, W_nl0, W_nl1, W_fc1, W_fc2, W_out_s, W_out_v, edge_index)

    def _L1_gnn_ref(x, node_attr, edge_scalars, edge_attr_sh, edge_src, edge_dst, Wfc1, Wfc2, Wsc0, Wsc1, Wl1_0, Wl1_1, Wl2_s, Wl2_v, Wa):
        import jax, jax.numpy as jnp
        import numpy as np
        N = 625
        E = 10000
        MUL0 = 64
        MUL1 = 32
        FC_IN = 16
        FC_H = 64
        WNUM = 192
        n = x.shape[0]
        x0 = x[:, :MUL0]
        x1 = x[:, MUL0:].reshape(n, MUL1, 3)
        a = node_attr
        h = jax.nn.silu(edge_scalars @ (Wfc1 / jnp.sqrt(jnp.float32(FC_IN))))
        w = h @ (Wfc2 / jnp.sqrt(jnp.float32(FC_H)))
        w0 = w[:, :64]
        w1 = w[:, 64:128]
        w2 = w[:, 128:160]
        w3 = w[:, 160:192]
        inv8 = 1.0 / jnp.sqrt(jnp.float32(MUL0))
        inv32 = 1.0 / jnp.sqrt(jnp.float32(MUL1))
        sc = jnp.concatenate([x0 @ Wsc0 * a * inv8, (jnp.einsum('num,uv->nvm', x1, Wsc1) * a[..., None] * inv32).reshape(n, 3 * MUL1)], axis=1)
        f0 = x0 @ Wl1_0 * a * inv8
        f1 = jnp.einsum('num,uv->nvm', x1, Wl1_1) * a[..., None] * inv32
        e0 = f0[edge_src]
        e1 = f1[edge_src]
        sh0 = edge_attr_sh[:, :1]
        sh1 = edge_attr_sh[:, 1:4]
        mid0 = w0 * e0 * sh0
        mid1 = w3 * jnp.einsum('eum,em->eu', e1, sh1) / jnp.sqrt(3.0)
        mid2 = w1[:, :, None] * e0[:, :, None] * sh1[:, None, :]
        mid3 = w2[:, :, None] * e1 * sh0[:, :, None]
        cnt = jnp.clip(jax.ops.segment_sum(jnp.ones(edge_dst.shape, x.dtype), edge_dst, num_segments=n), 1.0)

        def smean(v):
            s = jax.ops.segment_sum(v, edge_dst, num_segments=n)
            return s / cnt.reshape((n,) + (1,) * (v.ndim - 1))
        n0, n1 = (smean(mid0), smean(mid1))
        n2, n3 = (smean(mid2), smean(mid3))
        scal = jnp.concatenate([n0, n1], axis=1)
        vec = jnp.concatenate([n2, n3], axis=1)
        inv96 = 1.0 / jnp.sqrt(jnp.float32(MUL0 + MUL1))
        alpha = scal @ Wa * a * inv96
        out_s = scal @ Wl2_s * a * inv96
        out_v = jnp.einsum('num,uv->nvm', vec, Wl2_v) * a[..., None] * inv96
        conv = jnp.concatenate([out_s, out_v.reshape(n, 3 * MUL1)], axis=1)
        return sc + alpha * conv

    def _L2_gnn_ref(node_input, node_attr, node_crystal_attr, sym_mask, edge_attr, edge_length_embedded, edge_src, edge_dst, Ws_sc_a, Wv_sc_a, Ws_sc_c, Wv_sc_c, Ws_l1_a, Wv_l1_a, Ws_l1_c, Wv_l1_c, W_fc1, W_fc2, Ws_l2_a, Wv_l2_a, Ws_l2_c, Wv_l2_c, Ws_l3, Wv_l3):
        import jax, jax.numpy as jnp
        import numpy as np
        N = 25000
        E = 12500
        S = 64
        V = 32
        NB = 10
        H = 100
        WN = 192
        MID = 96
        NUM_NEIGHBORS = 16.0
        C_S = float(np.sin(np.pi / 8.0))
        C_X = float(np.cos(np.pi / 8.0))
        SQRT3 = float(np.sqrt(3.0))

        def fctp_scalar_attr(xs, xv, attr, Ws, Wv):
            s = xs * attr @ Ws
            v = jnp.einsum('nuc,uo->noc', xv * attr[:, :, None], Wv)
            return (s, v)
        n = node_input.shape[0]
        xs = node_input[:, :S]
        xv = node_input[:, S:].reshape(n, V, 3)
        ssa, sva = fctp_scalar_attr(xs, xv, node_attr, Ws_sc_a, Wv_sc_a)
        ssc, svc = fctp_scalar_attr(xs, xv, node_crystal_attr, Ws_sc_c, Wv_sc_c)
        s_s, s_v = (ssa + ssc, sva + svc)
        l1a_s, l1a_v = fctp_scalar_attr(xs, xv, node_attr, Ws_l1_a, Wv_l1_a)
        l1c_s, l1c_v = fctp_scalar_attr(xs, xv, node_crystal_attr, Ws_l1_c, Wv_l1_c)
        x1s, x1v = (l1a_s + l1c_s, l1a_v + l1c_v)
        weight = jax.nn.silu(edge_length_embedded @ W_fc1) @ W_fc2
        w0 = weight[:, :S]
        w1 = weight[:, S:2 * S]
        w2 = weight[:, 2 * S:2 * S + V]
        w3 = weight[:, 2 * S + V:]
        gs = x1s[edge_src]
        gv = x1v[edge_src]
        e_s = edge_attr[:, :1]
        e_v = edge_attr[:, 1:]
        mid0a = w0 * gs * e_s
        mid0b = w3 * (jnp.einsum('euc,ec->eu', gv, e_v) / SQRT3)
        mid1a = w1[:, :, None] * gs[:, :, None] * e_v[:, None, :]
        mid1b = w2[:, :, None] * gv * e_s[:, :, None]
        edge_feat = jnp.concatenate([mid0a, mid0b, mid1a.reshape(-1, 3 * S), mid1b.reshape(-1, 3 * V)], axis=-1)
        agg = jax.ops.segment_sum(edge_feat, edge_dst, num_segments=n) / np.sqrt(NUM_NEIGHBORS)
        m_s = agg[:, :MID]
        m_v = agg[:, MID:].reshape(n, MID, 3)
        l2a_s, l2a_v = fctp_scalar_attr(m_s, m_v, node_attr, Ws_l2_a, Wv_l2_a)
        l2c_s, l2c_v = fctp_scalar_attr(m_s, m_v, node_crystal_attr, Ws_l2_c, Wv_l2_c)
        m_s, m_v = (l2a_s + l2c_s, l2a_v + l2c_v)
        o_s, o_v = fctp_scalar_attr(m_s, m_v, sym_mask, Ws_l3, Wv_l3)
        out_s = C_S * s_s + C_X * o_s
        out_v = C_S * s_v + C_X * o_v
        return jnp.concatenate([out_s, out_v.reshape(n, 3 * V)], axis=-1)

    def _L3_gnn_ref(node_features, node_attr, edge_src, edge_dst, edge_attr, edge_scalars, lin1_ws, lin1_wv, fc_w1, fc_w2, sc_ws, sc_wv, lin2_ws, lin2_wv):
        import jax, jax.numpy as jnp
        import numpy as np
        N, E = (1250, 20000)
        S_IN, V_IN = (64, 32)
        S_MID, V_MID = (96, 128)
        S_OUT, V_OUT = (96, 32)
        R = 64
        FC_HID = 64
        W_NUMEL = 64 + 64 + 32 + 32 + 32
        NUM_NEIGHBORS = 16.0

        def _inv(d):
            return 1.0 / jnp.sqrt(jnp.float32(d))

        def _forward(node_features, node_attr, edge_attr, edge_scalars, lin1_ws, lin1_wv, fc_w1, fc_w2, sc_ws, sc_wv, lin2_ws, lin2_wv, edge_src, edge_dst):
            n = node_features.shape[0]
            s = node_features[:, :S_IN]
            v = node_features[:, S_IN:].reshape(n, V_IN, 3)
            a = node_attr
            sc_s = s @ sc_ws * a * _inv(S_IN)
            sc_v = jnp.einsum('nci,cd->ndi', v, sc_wv) * a[:, :, None] * _inv(V_IN)
            h_s = s @ lin1_ws * a * _inv(S_IN)
            h_v = jnp.einsum('nci,cd->ndi', v, lin1_wv) * a[:, :, None] * _inv(V_IN)
            hid = jax.nn.silu(edge_scalars @ fc_w1 * _inv(R))
            w = hid @ fc_w2 * _inv(FC_HID)
            w1, w2, w3, w4, w5 = jnp.split(w, [64, 128, 160, 192], axis=-1)
            es = h_s[edge_src]
            ev = h_v[edge_src]
            e0 = edge_attr[:, :1]
            e1 = edge_attr[:, 1:4]
            m_s1 = w1 * es * e0
            m_s2 = w4 * jnp.einsum('eci,ei->ec', ev, e1) * _inv(3)
            m_v1 = (w2 * es)[:, :, None] * e1[:, None, :]
            m_v2 = w3[:, :, None] * ev * e0[:, :, None]
            m_v3 = w5[:, :, None] * jnp.cross(ev, e1[:, None, :]) * _inv(2)
            mid_s = jnp.concatenate([m_s1, m_s2], axis=-1)
            mid_v = jnp.concatenate([m_v1, m_v2, m_v3], axis=1)
            inv_nn = 1.0 / jnp.sqrt(jnp.float32(NUM_NEIGHBORS))
            agg_s = jax.ops.segment_sum(mid_s, edge_dst, num_segments=n) * inv_nn
            agg_v = jax.ops.segment_sum(mid_v, edge_dst, num_segments=n) * inv_nn
            o_s = agg_s @ lin2_ws * a * _inv(S_MID)
            o_v = jnp.einsum('nci,cd->ndi', agg_v, lin2_wv) * a[:, :, None] * _inv(V_MID)
            pre_s = sc_s + o_s
            pre_v = sc_v + o_v
            scalars = jax.nn.silu(pre_s[:, :64])
            gates = jax.nn.sigmoid(pre_s[:, 64:96])
            gated = gates[:, :, None] * pre_v
            return jnp.concatenate([scalars, gated.reshape(n, 3 * V_OUT)], axis=-1)
        return _forward(node_features, node_attr, edge_attr, edge_scalars, lin1_ws, lin1_wv, fc_w1, fc_w2, sc_ws, sc_wv, lin2_ws, lin2_wv, edge_src, edge_dst)
    edge_index = jnp.stack([src, dst])
    x = _layernorm(x + _L0_gnn_ref(x, edge_attr_3, edge_attr_64, L0_gnn_W_skip0, L0_gnn_W_skip1, L0_gnn_W_nl0, L0_gnn_W_nl1, L0_gnn_W_fc1, L0_gnn_W_fc2, L0_gnn_W_out_s, L0_gnn_W_out_v, edge_index), axis=-1)
    x = _layernorm(x + _L1_gnn_ref(x, node_vec1, edge_attr_16, edge_attr_4, src, dst, L1_gnn_Wfc1, L1_gnn_Wfc2, L1_gnn_Wsc0, L1_gnn_Wsc1, L1_gnn_Wl1_0, L1_gnn_Wl1_1, L1_gnn_Wl2_s, L1_gnn_Wl2_v, L1_gnn_Wa), axis=-1)
    x = _layernorm(x + _L2_gnn_ref(x, node_vec1, node_vec1_n2, node_vec1_n3, edge_attr_4, edge_attr_10, src, dst, L2_gnn_Ws_sc_a, L2_gnn_Wv_sc_a, L2_gnn_Ws_sc_c, L2_gnn_Wv_sc_c, L2_gnn_Ws_l1_a, L2_gnn_Wv_l1_a, L2_gnn_Ws_l1_c, L2_gnn_Wv_l1_c, L2_gnn_W_fc1, L2_gnn_W_fc2, L2_gnn_Ws_l2_a, L2_gnn_Wv_l2_a, L2_gnn_Ws_l2_c, L2_gnn_Wv_l2_c, L2_gnn_Ws_l3, L2_gnn_Wv_l3), axis=-1)
    x = _layernorm(x + _L3_gnn_ref(x, node_vec1, src, dst, edge_attr_4, edge_attr_64, L3_gnn_lin1_ws, L3_gnn_lin1_wv, L3_gnn_fc_w1, L3_gnn_fc_w2, L3_gnn_sc_ws, L3_gnn_sc_wv, L3_gnn_lin2_ws, L3_gnn_lin2_wv), axis=-1)
    return x

_drawn_inputs = setup_inputs


def setup_inputs(seed=0):
    import zlib

    import numpy as np

    out = dict(_drawn_inputs(seed))
    spreads = {}
    factors = {'edge_attr_10': 4.293,
     'edge_attr_16': 8.0,
     'edge_attr_3': 6.723,
     'node_vec1_n3': 3.982,
     'L0_gnn_W_nl0': 6.318,
     'L0_gnn_W_nl1': 7.616,
     'L0_gnn_W_fc1': 6.009,
     'L0_gnn_W_fc2': 4.988,
     'L0_gnn_W_out_s': 7.164,
     'L0_gnn_W_out_v': 6.82,
     'L1_gnn_Wfc1': 8.0,
     'L1_gnn_Wfc2': 8.0,
     'L1_gnn_Wl1_0': 8.0,
     'L1_gnn_Wl1_1': 8.0,
     'L1_gnn_Wl2_s': 8.0,
     'L1_gnn_Wl2_v': 8.0,
     'L1_gnn_Wa': 8.0,
     'L2_gnn_Ws_l1_a': 3.545,
     'L2_gnn_Wv_l1_a': 4.863,
     'L2_gnn_Ws_l1_c': 3.463,
     'L2_gnn_Wv_l1_c': 4.718,
     'L2_gnn_Ws_l2_a': 4.46,
     'L2_gnn_Wv_l2_a': 3.574,
     'L2_gnn_Ws_l2_c': 4.501,
     'L2_gnn_Wv_l2_c': 3.452,
     'L2_gnn_Ws_l3': 3.042,
     'L3_gnn_lin1_ws': 3.017,
     'L3_gnn_lin1_wv': 3.31,
     'L3_gnn_lin2_ws': 3.309,
     'L3_gnn_lin2_wv': 3.069}
    for name, (base, spread) in spreads.items():
        noise = np.random.default_rng([zlib.crc32(name.encode()), seed]).standard_normal(out[name].shape)
        drawn = base * np.exp(spread * noise) if base else spread * noise
        out[name] = jnp.asarray(drawn.astype(out[name].dtype))
    for name, factor in factors.items():
        out[name] = (out[name] * factor).astype(out[name].dtype)
    return out
```

```python
from contextlib import ExitStack

import numpy as np
import concourse.bass as bass
from concourse import mybir

F32 = mybir.dt.float32
I32 = mybir.dt.int32
ALU = mybir.AluOpType
ACT = mybir.ActivationFunctionType
AX_X = mybir.AxisListType.X

P = 128
TILES = 4
GROUP = P * TILES
N = 50000
GROUPS = -(-N // GROUP)
NPAD = GROUPS * GROUP
ROWS = NPAD + P
S, V = 64, 32
HROW = 3 * V + S
LAYERS = 4
NORM_EPS = 1e-5

FC_IN = [64, 16, 10, 64]
FC_HID = [64, 64, 100, 64]
OUT_S = [96, 66, 128, 96]
OUT_V = [32, 32, 64, 32]
CROSS = [True, False, False, True]
HAS_E0 = [False, True, True, True]
WIDTH = [3 * OUT_V[l] + OUT_S[l] for l in range(LAYERS)]
SKIP_S = [96, 64, 64, 96]

EXT = 6
REC_F = TILES + TILES * EXT
REC_B = 2 * TILES + TILES * EXT


def weight_regions():
    out, at = {}, 0

    def add(name, rows, cols):
        nonlocal at
        out[name] = (at, rows, cols)
        at += cols

    for l in range(LAYERS):
        add(f"fc1_{l}", FC_IN[l], FC_HID[l])
        add(f"w12_{l}", FC_HID[l], 2 * S)
        add(f"wv_{l}", FC_HID[l], 3 * V)
        add(f"wx_{l}", FC_HID[l], 4 * V if CROSS[l] else V)
        add(f"r12_{l}", 2 * S, OUT_S[l] + OUT_V[l])
        add(f"r3_{l}", 3 * V, 3 * OUT_V[l])
        add(f"rx_{l}", 4 * V if CROSS[l] else V + (l == 1), WIDTH[l] if CROSS[l] else OUT_S[l])
        for part in ("a", "c") if l == 2 else ("a",):
            add(f"nv{part}_{l}", 3 * V, 6 * V)
            add(f"ns{part}_{l}", S, SKIP_S[l] + S)
    for name in ("lsa", "lsc", "lva", "lvc"):
        add(name, S + V, S + V)
    add("l3s", S + V, S)
    add("l3v", S + V, V)
    return out, at


REGIONS, WCOLS = weight_regions()


class Tally:

    def __init__(self, sem, credit):
        self.sem, self.total, self.first = sem, credit, {}

    def phase(self, key, step, times):
        self.first[key] = (self.total, step)
        self.total += step * times

    def at(self, key, n):
        first, step = self.first[key]
        return max(n, 0) * step + first if isinstance(n, int) else n * step + first


class Group:

    def __init__(self, half, odd):
        self.half, self.odd = half, odd
        self.n = half * 2 + odd

    def back(self):
        return Group(self.half, 0) if self.odd else Group(self.half - 1, 1)

    def ahead(self):
        return Group(self.half + 1, 0) if self.odd else Group(self.half, 1)


def over_groups(eng, step):
    step(Group(0, 0), False, True, True)
    step(Group(0, 1), True, True, True)
    with eng.Fori(1, GROUPS // 2 - 1) as half:
        step(Group(half, 0), True, True, True)
        step(Group(half, 1), True, True, True)
    step(Group(GROUPS // 2 - 1, 0), True, True, True)
    step(Group(GROUPS // 2 - 1, 1), True, True, False)
    step(Group(GROUPS // 2, 0), True, False, False)


def build(nc, d):
    assert GROUPS % 2 == 0
    ctx = ExitStack()
    with ctx:
        def sb(name, shape, dt=F32):
            return ctx.enter_context(nc.sbuf_tensor(name, shape, dt))

        def sem(name):
            return ctx.enter_context(nc.semaphore(name))

        def dram(name, shape):
            return nc.dram_tensor(name, shape, F32).ap()

        h_table = [dram(f"h_table{l}", [NPAD, HROW]) for l in range(LAYERS)]
        totals = [dram(f"totals{l}", [ROWS, WIDTH[l]]) for l in range(LAYERS)]
        base = [d["x"]] + [dram(f"base{l}", [NPAD, HROW]) for l in range(1, LAYERS)]
        rec_f = [dram(f"rec_f{k}", [P, GROUPS * REC_F]) for k in range(2)]
        rec_b = [dram(f"rec_b{k}", [P, GROUPS * REC_B]) for k in range(2)]

        weights = sb("weights", [P, WCOLS])
        consts = sb("consts", [P, 2 * P + 1])
        ident, lower, spare = consts[:, 0:P], consts[:, P:2 * P], consts[:, 2 * P:2 * P + 1]
        ones_row = sb("ones_row", [P, GROUP])
        zeros = sb("zeros", [P, TILES * max(WIDTH)])
        power = sb("power", [P, TILES * GROUPS])

        def w(name, r0=0, r1=None, c0=0, c1=None):
            at, rows, cols = REGIONS[name]
            return weights[r0:rows if r1 is None else r1, at + c0:at + (cols if c1 is None else c1)]

        area = sb("area", [P, 30000])
        area_at = [0]

        def part(shape):
            size = int(np.prod(shape))
            a = area[:, area_at[0]:area_at[0] + size]
            area_at[0] += size
            if len(shape) == 2:
                a = a.rearrange("p (a b) -> p a b", b=shape[1])
            return a

        src_idx = part([GROUPS * TILES])
        dst_idx = part([GROUPS * TILES])
        vec3 = part([GROUPS * TILES, 3])
        vec4 = part([GROUPS * TILES, 4])
        square = part([GROUPS * TILES, 3])
        inv_len = part([GROUPS * TILES])
        sum_sq = part([GROUPS * TILES])
        seen = [part([GROUPS * TILES]) for _ in range(2)]
        moved = part([GROUPS * TILES])
        front_all = [part([GROUPS, REC_F]) for _ in range(2)]
        back_all = [part([GROUPS, REC_B]) for _ in range(2)]
        row_prep = [part([GROUP]) for _ in range(2)]
        same_prep = part([GROUP])
        low_prep = part([GROUP])
        comp = part([2 * S + 2 * V])
        assert area_at[0] <= 30000, area_at

        area_at[0] = 0
        front_rec = [part([REC_F]) for _ in range(2)]
        back_rec = [part([REC_B]) for _ in range(2)]
        target_row = [part([GROUP]) for _ in range(2)]
        edge_feat = [part([GROUP]) for _ in range(2)]
        gath = [part([TILES, HROW + S]) for _ in range(2)]
        v_e0 = [part([TILES, 3 * V]) for _ in range(2)]
        dot_cross = [part([TILES, 4 * V]) for _ in range(2)]
        prod_dot = part([TILES, 3 * V])
        prod_a = part([TILES, 3 * V])
        prod_b = part([TILES, 3 * V])
        hidden = [part([GROUP]) for _ in range(2)]
        w_sb = [part([GROUP]) for _ in range(2)]
        message = [[part([GROUP]) for _ in range(3)] for _ in range(2)]
        same = [part([TILES, P]) for _ in range(2)]
        edge_out = [part([TILES, 384]) for _ in range(2)]
        outer = part([TILES, 3 * max(OUT_V)])
        summed = [part([TILES, max(WIDTH)]) for _ in range(2)]
        assert area_at[0] <= 30000, area_at

        area_at[0] = 0
        base_in = [part([TILES, HROW]) for _ in range(2)]
        tot_in = [part([TILES, max(WIDTH)]) for _ in range(2)]
        attr_in = [part([3 * TILES]) for _ in range(2)]
        attr = [part([3 * TILES]) for _ in range(2)]
        gates = [part([TILES, S + V]) for _ in range(2)]
        factor = part([6 * TILES])
        y = part([TILES, HROW])
        stats = part([TILES, 6])
        moments = part([TILES, 2])
        var_eps = part([TILES])
        rstd = part([TILES])
        x_new = [part([TILES, HROW]) for _ in range(2)]
        v_cols = [part([GROUP]) for _ in range(2)]
        s_cols = [part([GROUP]) for _ in range(2)]
        h_out = [part([TILES, HROW]) for _ in range(2)]
        tot_out = [part([TILES, max(WIDTH)]) for _ in range(2)]
        base_out = [part([TILES, HROW]) for _ in range(2)]
        assert area_at[0] <= 30000, area_at

        psum = ctx.enter_context(nc.psum_tensor("psum", [P, 8, GROUP], F32))
        WIDE, TURN, MSG, SUM = (0, 1), (2, 3), (4, 5), (6, 7)

        credited = []

        def tally(name, plan, kind=""):
            t = Tally(sem(name), {"": 1, "dma": 0, "dma, credited": 16}[kind])
            for key, step, times in plan:
                t.phase(key, step, times)
            if not kind:
                credited.append(t)
            return t

        G, H = GROUPS, GROUPS // 2

        def edges(step, times):
            return [(("edge", l), step, times) for l in range(LAYERS)]

        def nodes(step, times, passes=range(LAYERS + 1)):
            return [(("node", l), step(l) if callable(step) else step, times) for l in passes]

        s_const = sem("s_const")
        s_edges_in = sem("s_edges_in")
        s_fill = sem("s_fill")
        s_scaled = sem("s_scaled")
        s_comp_mm = sem("s_comp_mm")
        s_comp = sem("s_comp")
        s_comp_put = sem("s_comp_put")
        s_sq = sem("s_sq")
        s_len = sem("s_len")
        s_vec = sem("s_vec")
        s_row_prep = [sem(f"s_row_prep{b}") for b in range(2)]
        s_seen_step = sem("s_seen_step")
        s_rec = sem("s_rec")
        s_rec_out = sem("s_rec_out")
        s_barrier = sem("s_barrier")
        s_settled = {e: sem(f"s_settled_{n}") for n, e in
                     (("sp", nc.sync.engine), ("pool", nc.gpsimd.engine), ("dve", nc.vector.engine),
                      ("pe", nc.tensor.engine))}

        front_in = [tally(f"front_in{b}", edges(32, H), kind="dma") for b in range(2)]
        back_in = [tally(f"back_in{b}", edges(32, H), kind="dma") for b in range(2)]
        gathered = [tally(f"gathered{b}", edges(64, H), kind="dma") for b in range(2)]
        scattered = tally("scattered", edges(16, TILES * G), kind="dma")
        landed = tally("landed", edges(1, G))
        multiplied = tally("multiplied", edges(1, G))
        prepared = tally("prepared", edges(1, G))
        wide_mm = tally("wide_mm", edges(1, 4 * G))
        wide_copied = tally("wide_copied", edges(1, 4 * G))
        turned = tally("turned", edges(1, 3 * G))
        message_made = tally("message_made", edges(1, 3 * G))
        msg_mm = tally("msg_mm", edges(1, TILES * G))
        msg_copied = tally("msg_copied", edges(1, TILES * G))
        outer_made = tally("outer_made", edges(1, G))
        outer_added = tally("outer_added", edges(1, G))
        same_made = tally("same_made", edges(1, G))
        sum_mm = tally("sum_mm", edges(1, TILES * G))
        sum_copied = tally("sum_copied", edges(1, TILES * G))

        inner = range(LAYERS)
        fin = range(1, LAYERS + 1)
        node_in = [tally(f"node_in{b}", nodes(lambda k: 16 if k == 0 else 48, H), kind="dma") for b in range(2)]
        combine_step = tally("combine_step", nodes(lambda k: {1: 1, 2: 6, 3: 2, 4: 2}[k], G, fin))
        gated = tally("gated", nodes(1, G, [1, 4]))
        combined = tally("combined", nodes(1, G, fin))
        stats_made = tally("stats_made", nodes(1, G, fin))
        moments_made = tally("moments_made", nodes(1, G, fin))
        var_made = tally("var_made", nodes(1, G, fin))
        rstd_made = tally("rstd_made", nodes(1, G, fin))
        normed = tally("normed", nodes(1, G, fin))
        x_turned = tally("x_turned", nodes(1, G, inner))
        x_copied = tally("x_copied", nodes(1, G, inner))
        lin_mm = tally("lin_mm", nodes(1, TILES * G, inner))
        lin_act = tally("lin_act", nodes(1, TILES * G, inner))
        lin_step = tally("lin_step", nodes(1, TILES * G, [2]))
        lin_dve = tally("lin_dve", nodes(1, TILES * G, inner))
        stored = [tally(f"stored{b}", nodes(lambda k: (32, 48, 48, 48, 16)[k], H), kind="dma, credited")
                  for b in range(2)]

        block = ctx.enter_context(nc.Block())

        def barrier(eng, count):
            eng.drain().then_inc(s_barrier, 1)
            eng.wait_ge(s_barrier, 5 * count)

        def is_last_ahead(g):
            return isinstance(g.half, int) and g.half == H - 1

        def settle(eng):
            eng.sem_inc(s_settled[eng.engine], 1)

        def linear_places(k, t):
            act_bank, dve_bank = psum[:, 2 + t % 2, :], psum[:, 4 + t % 2, :]
            a = (f"nva_{k}", f"nsa_{k}")
            c = (f"nvc_{k}", f"nsc_{k}")
            if k in (0, 3):
                return [(act_bank, *a, "skip"), (dve_bank, *a, "h")]
            if k == 1:
                return [(act_bank, *a, "h"), (dve_bank, *a, "skip")]
            return [(act_bank, *a, "h"), (dve_bank, *a, "skip"), (dve_bank[:, HROW:], *c, "skip"),
                    (dve_bank[:, 2 * HROW:], *c, "h")]

        r2, r3, r32, r96, r128 = 2 ** -0.5, 3 ** -0.5, 32 ** -0.5, 96 ** -0.5, 128 ** -0.5
        C_S, C_X = float(np.sin(np.pi / 8)), float(np.cos(np.pi / 8))
        scales = [("r12_0", 0, 64, 3 ** 0.5 / 32), ("r12_0", 64, 128, 1 / 32), ("r3_0", 0, 96, 1 / 32),
                  ("rx_0", 0, 32, 1 / 32)]
        scales += [("rx_0", 32 * i, 32 * i + 32, 3 ** 0.5 * r2 / 32) for i in (1, 2, 3)]
        scales += [("fc1_1", 0, 16, 1 / 4), ("w12_1", 0, 64, 1 / 8), ("wv_1", 0, 64, 1 / 8),
                   ("wx_1", 0, 64, 1 / 8), ("r12_1", 0, 128, r96), ("r3_1", 0, 96, r96),
                   ("rx_1", 0, 32, r96 * r3), ("nva_1", 0, 96, r32), ("nsa_1", 0, 64, 1 / 8)]
        scales += [("fc1_3", 0, 64, 1 / 8), ("w12_3", 0, 64, 1 / 8), ("wv_3", 0, 64, 1 / 8),
                   ("wx_3", 0, 64, 1 / 8), ("nva_3", 0, 96, r32), ("nsa_3", 0, 64, 1 / 8),
                   ("r12_3", 0, 64, r128 / 4), ("r12_3", 64, 128, r96 / 4), ("r3_3", 0, 96, r128 / 4),
                   ("rx_3", 0, 32, r96 * r3 / 4)]
        scales += [("rx_3", 32 * i, 32 * i + 32, r128 * r2 / 4) for i in (1, 2, 3)]
        skip_scales = [("nva_2", 96, 96, C_S), ("nvc_2", 96, 96, C_S), ("nsa_2", 64, 64, C_S),
                       ("nsc_2", 64, 64, C_S)]

        comp_parts = [("lsa", "l3s", S), ("lsc", "l3s", S), ("lva", "l3v", V), ("lvc", "l3v", V)]
        comp_at = [0, S, 2 * S, 2 * S + V]

        def comp_moves():
            us, vs, uv, vv = (lambda c0, r0, r1, a: comp[r0:r1, c0 + a:c0 + a + V] for _ in range(4))
            out = []
            for half in range(2):
                for which in range(2):
                    src = comp_at[which] + V * half
                    col = 2 * V * half + V * which
                    out.append((w("r12_2", S, 2 * S, col, col + V), comp[0:S, src:src + V]))
                    out.append((w("rx_2", 0, V, col, col + V), comp[S:S + V, src:src + V]))
            for which in range(2):
                src = comp_at[2 + which]
                col = OUT_S[2] + V * which
                out.append((w("r12_2", 0, S, col, col + V), comp[0:S, src:src + V]))
                for i in range(3):
                    col = 2 * V * i + V * which
                    out.append((w("r3_2", V * i, V * i + V, col, col + V), comp[S:S + V, src:src + V]))
            return out

        def edge_vec(rec, at, lo, hi):
            return rec[:, at:at + TILES * EXT].rearrange("p (t c) -> p t c", c=EXT)[:, :, lo:hi]

        def sp_edge(sp, l):
            key = ("edge", l)
            k = min(l, 1)

            def front(g):
                b = g.odd
                sp.wait_ge(gathered[b].sem, gathered[b].at(key, g.half))
                settle(sp)
                sp.wait_ge(prepared.sem, prepared.at(key, g.n - 1))
                settle(sp)
                sp.wait_ge(wide_mm.sem, wide_mm.at(key, (g.n - 2) * 4 + 1))
                settle(sp)
                sp.dma_start(front_rec[b], rec_f[k][:, bass.ds(g.n * REC_F, REC_F)]).then_inc(front_in[b].sem, 16)
                sp.dma_start(edge_feat[b][0:FC_IN[l], :], d[f"feat{l}"][:, bass.ds(g.n * GROUP, GROUP)])\
                  .then_inc(front_in[b].sem, 16)

            def back(g):
                b = g.odd
                rows = d["dst_rows"] if l else d["src_rows"]
                sp.wait_ge(outer_added.sem, outer_added.at(key, g.n - 1))
                settle(sp)
                sp.wait_ge(same_made.sem, same_made.at(key, g.n - 1))
                settle(sp)
                sp.wait_ge(scattered.sem, scattered.at(key, (g.n - 1) * TILES))
                settle(sp)
                sp.dma_start(back_rec[b], rec_b[k][:, bass.ds(g.n * REC_B, REC_B)]).then_inc(back_in[b].sem, 16)
                sp.dma_start(target_row[b].bitcast(I32), rows[bass.ds(g.n, 1), :].to_broadcast([P, GROUP]))\
                  .then_inc(back_in[b].sem, 16)

            def step(g, has_back, has_it, has_ahead):
                if has_ahead and not is_last_ahead(g):
                    front(g.ahead().ahead())
                if has_it:
                    back(g)

            front(Group(0, 0))
            front(Group(0, 1))
            over_groups(sp, step)
            barrier(sp, 3 + 2 * l)

        def sp_node(sp, k):
            key = ("node", k)

            def load(g):
                b = g.odd
                n = g.n * GROUP
                if k == 0:
                    sp.wait_ge(x_turned.sem, x_turned.at(key, g.n - 1))
                    settle(sp)
                    sp.dma_start(x_new[b].rearrange("p t c -> p (t c)"),
                                 d["x"][bass.ds(n, GROUP), :].rearrange("(p t) c -> p (t c)", t=TILES))\
                      .then_inc(node_in[b].sem, 16)
                    return
                sp.wait_ge(combined.sem, combined.at(key, g.n - 1))
                settle(sp)
                sp.dma_start(base_in[b].rearrange("p t c -> p (t c)"),
                             base[k - 1][bass.ds(n, GROUP), :].rearrange("(p t) c -> p (t c)", t=TILES))\
                  .then_inc(node_in[b].sem, 16)
                sp.dma_start(tot_in[b][:, :, 0:WIDTH[k - 1]],
                             totals[k - 1][bass.ds(n, GROUP), :].rearrange("(p t) c -> p t c", t=TILES))\
                  .then_inc(node_in[b].sem, 16)
                sp.dma_start(attr_in[b], d["attrs"][:, bass.ds(g.n * 3 * TILES, 3 * TILES)])\
                  .then_inc(node_in[b].sem, 16)

            def store(g):
                b = g.odd
                n = g.n * GROUP

                def put(table, tile):
                    sp.dma_start(table[bass.ds(n, GROUP), :].rearrange("(p t) c -> p t c", t=TILES), tile)\
                      .then_inc(stored[b].sem, 16)

                if k == LAYERS:
                    sp.wait_ge(normed.sem, normed.at(key, g.n + 1))
                    settle(sp)
                    put(d["out"], x_new[b])
                    return
                sp.wait_ge(lin_act.sem, lin_act.at(key, (g.n + 1) * TILES))
                settle(sp)
                sp.wait_ge(lin_dve.sem, lin_dve.at(key, (g.n + 1) * TILES))
                settle(sp)
                put(h_table[k], h_out[b])
                if k in (0, 3):
                    put(totals[k], tot_out[b][:, :, 0:WIDTH[k]])
                else:
                    put(totals[k], zeros[:, 0:TILES * WIDTH[k]].rearrange("p (t c) -> p t c", t=TILES))
                    put(base[k], base_out[b])
                if k == 3:
                    put(base[k], x_new[b])

            def step(g, has_back, has_it, has_ahead):
                if has_ahead and not is_last_ahead(g):
                    load(g.ahead().ahead())
                if has_back:
                    store(g.back())

            load(Group(0, 0))
            load(Group(0, 1))
            over_groups(sp, step)
            for b in range(2):
                sp.wait_ge(stored[b].sem, stored[b].at(key, H))
            barrier(sp, 2 + 2 * k)

        @block.sync
        def _(sp):
            for t in credited:
                sp.sem_inc(t.sem, 1)
            sp.dma_start(weights[:, :], d["weights"]).then_inc(s_const, 16)
            sp.dma_start(consts[:, :], d["consts"]).then_inc(s_const, 16)
            sp.dma_start(src_idx.bitcast(I32), d["src_lanes"]).then_inc(s_edges_in, 16)
            sp.dma_start(dst_idx.bitcast(I32), d["dst_lanes"]).then_inc(s_edges_in, 16)
            sp.dma_start(vec3.rearrange("p a b -> p (a b)"), d["vec3"]).then_inc(s_edges_in, 16)
            sp.dma_start(vec4.rearrange("p a b -> p (a b)"), d["vec4"]).then_inc(s_edges_in, 16)
            for which, rows in ((0, d["src_rows"]), (1, d["dst_rows"])):
                def row(n, b, u):
                    sp.dma_start(row_prep[b].bitcast(I32), rows[bass.ds(n, 1), :].to_broadcast([P, GROUP]))\
                      .then_inc(s_row_prep[b], 16)
                for b in range(2):
                    if which:
                        sp.wait_ge(s_seen_step, 3 * (G * which - 2 + b) + 1)
                    row(b, b, 0)
                with sp.Fori(1, H) as half:
                    for b in range(2):
                        sp.wait_ge(s_seen_step, half * 6 + (3 * (G * which + b - 2) + 1))
                        row(half * 2 + b, b, half)
            sp.wait_ge(s_comp, 4)
            sp.wait_ge(s_scaled, 1)
            moves = comp_moves()
            for dst, src in moves:
                sp.dma_start(dst, src).then_inc(s_comp_put, 16)
            sp.wait_ge(s_comp_put, 16 * len(moves))
            sp.wait_ge(s_rec, 1)
            sp.wait_ge(s_fill, 1)
            for k in range(2):
                sp.dma_start(rec_f[k], front_all[k].rearrange("p a b -> p (a b)")).then_inc(s_rec_out, 16)
                sp.dma_start(rec_b[k], back_all[k].rearrange("p a b -> p (a b)")).then_inc(s_rec_out, 16)
            spare_rows_in = (stored[0].sem, stored[1].sem, s_rec_out, s_rec_out)
            for l in range(LAYERS):
                sp.dma_start(totals[l][NPAD:ROWS, :], zeros[:, 0:WIDTH[l]]).then_inc(spare_rows_in[l], 16)
            for credit in spare_rows_in[0:2]:
                sp.wait_ge(credit, 16)
            sp.wait_ge(s_rec_out, 16 * 6)
            barrier(sp, 1)
            sp_node(sp, 0)
            for l in range(LAYERS):
                sp_edge(sp, l)
                sp_node(sp, l + 1)

        def pool_edge(pool, l):
            key = ("edge", l)

            def gather(g, t):
                b = g.odd
                if t == 0:
                    pool.wait_ge(front_in[b].sem, front_in[b].at(key, g.half + 1))
                    settle(pool)
                    pool.wait_ge(prepared.sem, prepared.at(key, g.n - 1))
                    settle(pool)
                    pool.wait_ge(turned.sem, turned.at(key, (g.n - 1) * 3))
                settle(pool)
                pool.indirect_dma_start(
                    gath[b][:, t, 0:HROW], None, h_table[l][:, :],
                    bass.IndirectOffsetOnAxis(front_rec[b][:, t:t + 1].bitcast(I32), 0)).then_inc(gathered[b].sem, 16)

            def scatter(g, t):
                b = g.odd
                if t == 0:
                    pool.wait_ge(back_in[b].sem, back_in[b].at(key, g.half + 1))
                    settle(pool)
                pool.wait_ge(sum_copied.sem, sum_copied.at(key, g.n * TILES + t + 1))
                settle(pool)
                pool.wait_ge(scattered.sem, scattered.at(key, g.n * TILES + t))
                pool.sem_inc(landed.sem if t == 0 else s_settled[nc.gpsimd.engine], 1)
                pool.indirect_dma_start(
                    totals[l][:, :], bass.IndirectOffsetOnAxis(back_rec[b][:, TILES + t:TILES + t + 1].bitcast(I32), 0),
                    summed[b][:, t, 0:WIDTH[l]], None, compute_op=ALU.add).then_inc(scattered.sem, 16)

            def step(g, has_back, has_it, has_ahead):
                for t in range(TILES):
                    if has_back:
                        scatter(g.back(), t)
                    if has_ahead and not is_last_ahead(g):
                        gather(g.ahead().ahead(), t)

            for g in (Group(0, 0), Group(0, 1)):
                for t in range(TILES):
                    gather(g, t)
            over_groups(pool, step)
            pool.wait_ge(scattered.sem, scattered.at(key, G * TILES))
            barrier(pool, 3 + 2 * l)

        def pool_node(pool, k):
            key = ("node", k)

            def step(g, has_back, has_it, has_ahead):
                if has_it:
                    pool.wait_ge(var_made.sem, var_made.at(key, g.n + 1))
                    settle(pool)
                    nc.gpsimd.tensor_tensor(rstd, var_eps, power[:, 0:TILES], ALU.pow).then_inc(rstd_made.sem, 1)

            over_groups(pool, step)
            barrier(pool, 2 + 2 * k)

        @block.gpsimd
        def _(pool):
            pool.wait_ge(s_sq, 2)
            pool.wait_ge(s_fill, 1)
            nc.gpsimd.tensor_tensor(inv_len, sum_sq, power[:, 0:GROUPS * TILES], ALU.pow).then_inc(s_len, 1)
            barrier(pool, 1)
            barrier(pool, 2)
            for l in range(LAYERS):
                pool_edge(pool, l)
                pool_node(pool, l + 1)

        def dve_edge(dve, l):
            key = ("edge", l)
            nk, ns, width = OUT_V[l], OUT_S[l], WIDTH[l]
            if l == 1:
                for b in range(2):
                    nc.vector.memset(message[b][2][V:2 * V, :], 1.0)

            def prepare(g):
                b = g.odd
                v3 = gath[b][:, :, 0:3 * V].rearrange("p t (i c) -> p t i c", c=V)
                dve.wait_ge(gathered[b].sem, gathered[b].at(key, g.half + 1))
                dve.wait_ge(front_in[b].sem, front_in[b].at(key, g.half + 1))
                dve.wait_ge(turned.sem, turned.at(key, (g.n - 1) * 3))

                def e(lo, hi, shape):
                    return edge_vec(front_rec[b], TILES, lo, hi).unsqueeze(3).to_broadcast([P, TILES, hi - lo, shape])

                def four(a):
                    return a.rearrange("p t (i c) -> p t i c", c=V)

                def e0(width):
                    return edge_vec(front_rec[b], TILES, 0, 1).to_broadcast([P, TILES, width])

                nc.vector.tensor_tensor(gath[b][:, :, HROW:HROW + S], gath[b][:, :, 3 * V:HROW], e0(S), ALU.mult)
                if HAS_E0[l]:
                    nc.vector.tensor_tensor(v_e0[b], gath[b][:, :, 0:3 * V], e0(3 * V), ALU.mult)
                if CROSS[l]:
                    nc.vector.tensor_tensor(four(prod_a)[:, :, 0:2, :], v3[:, :, 1:3, :], e(3, 5, V), ALU.mult)
                    nc.vector.tensor_tensor(four(prod_a)[:, :, 2, :], v3[:, :, 0, :],
                                            edge_vec(front_rec[b], TILES, 2, 3).to_broadcast([P, TILES, V]), ALU.mult)
                    nc.vector.tensor_tensor(four(prod_b)[:, :, 0, :], v3[:, :, 2, :],
                                            edge_vec(front_rec[b], TILES, 2, 3).to_broadcast([P, TILES, V]), ALU.mult)
                    nc.vector.tensor_tensor(four(prod_b)[:, :, 1:3, :], v3[:, :, 0:2, :], e(3, 5, V), ALU.mult)
                nc.vector.tensor_tensor(four(prod_dot), v3, e(1, 4, V), ALU.mult).then_inc(multiplied.sem, 1)
                dve.wait_ge(multiplied.sem, multiplied.at(key, g.n + 1))
                if CROSS[l]:
                    nc.vector.tensor_tensor(dot_cross[b][:, :, V:4 * V], prod_a, prod_b, ALU.subtract)
                nc.vector.tensor_reduce(dot_cross[b][:, :, 0:V], prod_dot.rearrange("p t (i c) -> p t c i", c=V),
                                        AX_X, ALU.add).then_inc(prepared.sem, 1)

            def make_message(g, s):
                b = g.odd
                n = g.n * 3 + s
                rows = (2 * S, 3 * V, 4 * V if CROSS[l] else V)[s]
                r = (g.n + s) % 2 if isinstance(g.n, int) else (g.odd + s) % 2
                dve.wait_ge(turned.sem, turned.at(key, n + 1))
                dve.wait_ge(wide_copied.sem, wide_copied.at(key, g.n * 4 + s + 2))
                dve.wait_ge(msg_mm.sem, msg_mm.at(key, (g.n - 1) * TILES))
                nc.vector.tensor_tensor(message[b][s][0:rows, :], psum[0:rows, TURN[r], :], w_sb[r][0:rows, :],
                                        ALU.mult).then_inc(message_made.sem, 1)

            def compare(g):
                b = g.odd
                dve.wait_ge(back_in[b].sem, back_in[b].at(key, g.half + 1))
                dve.wait_ge(sum_mm.sem, sum_mm.at(key, (g.n - 1) * TILES))
                nc.vector.tensor_tensor(
                    same[b], target_row[b].bitcast(I32).rearrange("p (t c) -> p t c", c=P),
                    back_rec[b][:, 0:TILES].bitcast(I32).unsqueeze(2).to_broadcast([P, TILES, P]),
                    ALU.is_equal).then_inc(same_made.sem, 1)

            def add_outer(g):
                b = g.odd
                dve.wait_ge(msg_copied.sem, msg_copied.at(key, (g.n + 1) * TILES))
                outer4 = outer[:, :, 0:3 * nk].rearrange("p t (i c) -> p t i c", c=nk)
                nc.vector.tensor_tensor(
                    outer4, edge_out[b][:, :, width:width + nk].unsqueeze(2).to_broadcast([P, TILES, 3, nk]),
                    edge_vec(back_rec[b], 2 * TILES, 1, 4).unsqueeze(3).to_broadcast([P, TILES, 3, nk]),
                    ALU.mult).then_inc(outer_made.sem, 1)
                dve.wait_ge(outer_made.sem, outer_made.at(key, g.n + 1))
                nc.vector.tensor_tensor(edge_out[b][:, :, 0:3 * nk], edge_out[b][:, :, 0:3 * nk],
                                        outer[:, :, 0:3 * nk], ALU.add).then_inc(outer_added.sem, 1)

            def step(g, has_back, has_it, has_ahead):
                if has_back:
                    compare(g.back())
                if has_it:
                    make_message(g, 0)
                if has_back:
                    add_outer(g.back())
                if has_it:
                    make_message(g, 1)
                    make_message(g, 2)
                if has_ahead:
                    prepare(g.ahead())

            prepare(Group(0, 0))
            over_groups(dve, step)
            barrier(dve, 3 + 2 * l)

        def dve_node(dve, k):
            key = ("node", k)
            f = k - 1

            def combine(g):
                b = g.odd
                dve.wait_ge(node_in[b].sem, node_in[b].at(key, g.half + 1))
                if k < LAYERS:
                    dve.wait_ge(lin_act.sem, lin_act.at(key, (g.n - 1) * TILES))
                    dve.wait_ge(lin_dve.sem, lin_dve.at(key, (g.n - 1) * TILES))
                nc.vector.tensor_copy(attr[b], attr_in[b])
                t_in = tot_in[b]
                a = attr_in[b][:, 0:TILES]
                done = [0]

                def link(ins):
                    ins.then_inc(combine_step.sem, 1)
                    done[0] += 1
                    first, step = combine_step.first[key]
                    dve.wait_ge(combine_step.sem, g.n * step + (first + done[0]))

                def wide(x, width):
                    return x.unsqueeze(2).to_broadcast([P, TILES, width])

                if f in (0, 3):
                    if f == 3:
                        link(nc.vector.tensor_tensor(t_in[:, :, 0:WIDTH[3]], t_in[:, :, 0:WIDTH[3]],
                                                     wide(a, WIDTH[3]), ALU.mult))
                    dve.wait_ge(gated.sem, gated.at(key, g.n + 1))
                    gate = gates[b]
                    nc.vector.tensor_tensor(y[:, :, 3 * V:HROW], t_in[:, :, 3 * V:HROW], gate[:, :, 0:S], ALU.mult)
                    link(nc.vector.tensor_tensor(
                        y[:, :, 0:3 * V].rearrange("p t (i c) -> p t i c", c=V),
                        t_in[:, :, 0:3 * V].rearrange("p t (i c) -> p t i c", c=V),
                        gate[:, :, S:S + V].unsqueeze(2).to_broadcast([P, TILES, 3, V]), ALU.mult))
                elif f == 1:
                    q = [factor[:, TILES * i:TILES * i + TILES] for i in range(6)]
                    count, alpha = t_in[:, :, HROW + 1:HROW + 2], t_in[:, :, HROW:HROW + 1]
                    link(nc.vector.tensor_scalar(q[0].unsqueeze(2), count, 1.0, None, ALU.max))
                    link(nc.vector.reciprocal(q[1], q[0]))
                    link(nc.vector.tensor_tensor(q[2], q[1], a, ALU.mult))
                    link(nc.vector.tensor_tensor(q[3], q[2], q[2], ALU.mult))
                    link(nc.vector.tensor_tensor(q[4].unsqueeze(2), q[3].unsqueeze(2), alpha, ALU.mult))
                    link(nc.vector.tensor_tensor(y, t_in[:, :, 0:HROW], wide(q[4], HROW), ALU.mult))
                else:
                    t5 = t_in[:, :, 0:WIDTH[2]].rearrange("p t (i u c) -> p t i u c", u=2, c=V)
                    fa, fc = factor[:, 0:TILES], factor[:, TILES:2 * TILES]
                    nc.vector.tensor_tensor(fa, a, attr_in[b][:, 2 * TILES:3 * TILES], ALU.mult)
                    link(nc.vector.tensor_tensor(fc, attr_in[b][:, TILES:2 * TILES], attr_in[b][:, 2 * TILES:3 * TILES],
                                                 ALU.mult))
                    y5 = y.rearrange("p t (i c) -> p t i c", c=V)
                    for t in range(TILES):
                        nc.vector.tensor_scalar(t5[:, t, :, 0, :], t5[:, t, :, 0, :], fa[:, t:t + 1], None, ALU.mult)
                        last = nc.vector.scalar_tensor_tensor(
                            y5[:, t], t5[:, t, :, 1, :], fc[:, t:t + 1], base_in[b].rearrange("p t (i c) -> p t i c", c=V)[:, t],
                            ALU.mult, ALU.add)
                    link(last)
                    nc.vector.tensor_tensor(y5, y5, t5[:, :, :, 0, :], ALU.add).then_inc(combined.sem, 1)
                if f != 2:
                    nc.vector.tensor_tensor(y, y, base_in[b], ALU.add).then_inc(combined.sem, 1)
                assert done[0] == combine_step.first[key][1]
                dve.wait_ge(combined.sem, combined.at(key, g.n + 1))
                for t in range(TILES):
                    last = nc.vector.bn_stats(stats[:, t, :], y[:, t, :])
                last.then_inc(stats_made.sem, 1)
                dve.wait_ge(stats_made.sem, stats_made.at(key, g.n + 1))
                settle(dve)
                for t in range(TILES):
                    last = nc.vector.bn_aggr(moments[:, t, :], stats[:, t, :])
                last.then_inc(moments_made.sem, 1)
                dve.wait_ge(moments_made.sem, moments_made.at(key, g.n + 1))
                nc.vector.tensor_scalar(var_eps.unsqueeze(2), moments[:, :, 1:2], NORM_EPS, None, ALU.add)\
                  .then_inc(var_made.sem, 1)

            def normalise(g):
                b = g.odd
                dve.wait_ge(rstd_made.sem, rstd_made.at(key, g.n + 1))
                if k >= 3:
                    dve.wait_ge(stored[b].sem, stored[b].at(key, g.half))
                if k < LAYERS:
                    dve.wait_ge(x_turned.sem, x_turned.at(key, g.n - 1))
                for t in range(TILES):
                    last = nc.vector.tensor_scalar(x_new[b][:, t, :], y[:, t, :], moments[:, t, 0:1], rstd[:, t:t + 1],
                                                   ALU.subtract, ALU.mult)
                last.then_inc(normed.sem, 1)

            def linear_out(g):
                b = g.odd
                for t in range(TILES):
                    n = g.n * TILES + t
                    acc = psum[:, 4 + t % 2, :]
                    a, c = attr[b][:, t:t + 1], attr[b][:, TILES + t:TILES + t + 1]
                    if t == 0:
                        dve.wait_ge(stored[b].sem, stored[b].at(key, g.half))
                    dve.wait_ge(lin_mm.sem, lin_mm.at(key, n + 1))
                    if k == 0:
                        last = nc.vector.tensor_copy(h_out[b][:, t, :], acc[:, 0:HROW])
                    elif k == 3:
                        last = nc.vector.tensor_scalar(h_out[b][:, t, :], acc[:, 0:HROW], a, None, ALU.mult)
                    else:
                        last = nc.vector.scalar_tensor_tensor(base_out[b][:, t, :], acc[:, 0:HROW], a,
                                                              x_new[b][:, t, :], ALU.mult, ALU.add)
                    if k == 2:
                        last.then_inc(lin_step.sem, 1)
                        dve.wait_ge(lin_act.sem, lin_act.at(key, n + 1))
                        nc.vector.scalar_tensor_tensor(h_out[b][:, t, :], acc[:, 2 * HROW:3 * HROW], c,
                                                       h_out[b][:, t, :], ALU.mult, ALU.add)
                        dve.wait_ge(lin_step.sem, lin_step.at(key, n + 1))
                        last = nc.vector.scalar_tensor_tensor(base_out[b][:, t, :], acc[:, HROW:2 * HROW], c,
                                                              base_out[b][:, t, :], ALU.mult, ALU.add)
                    last.then_inc(lin_dve.sem, 1)

            def step(g, has_back, has_it, has_ahead):
                if has_it and k:
                    combine(g)
                if has_back and k < LAYERS:
                    linear_out(g.back())
                if has_it and k:
                    normalise(g)

            over_groups(dve, step)
            barrier(dve, 2 + 2 * k)

        @block.vector
        def _(dve):
            nc.vector.memset(zeros[:, :], 0.0)
            nc.vector.memset(ones_row[:, :], 1.0)
            nc.vector.memset(power[:, :], -0.5).then_inc(s_fill, 1)
            dve.wait_ge(s_const, 32)
            for name, r0, r1, by in scales:
                nc.vector.tensor_scalar(w(name, r0, r1), w(name, r0, r1), by, None, ALU.mult)
            for name, rows, cols, by in skip_scales:
                last = nc.vector.tensor_scalar(w(name, 0, rows, 0, cols), w(name, 0, rows, 0, cols), by, None, ALU.mult)
            last.then_inc(s_scaled, 1)
            dve.wait_ge(s_edges_in, 64)
            nc.vector.tensor_tensor(square, vec3, vec3, ALU.mult).then_inc(s_sq, 1)
            dve.wait_ge(s_sq, 1)
            nc.vector.tensor_reduce(sum_sq, square, AX_X, ALU.add).then_inc(s_sq, 1)
            for which, idx in ((0, src_idx), (1, dst_idx)):
                def search(n, b, u):
                    first = n * 3 + 3 * G * which
                    dve.wait_ge(s_row_prep[b], u * 16 + 16 * (H * which + 1))
                    own = idx.bitcast(I32)[:, bass.ds(n * TILES, TILES)].unsqueeze(2).to_broadcast([P, TILES, P])
                    row = row_prep[b].bitcast(I32).rearrange("p (t c) -> p t c", c=P)
                    eq = same_prep.rearrange("p (t c) -> p t c", c=P)
                    lo = low_prep.rearrange("p (t c) -> p t c", c=P)
                    nc.vector.tensor_tensor(eq, row, own, ALU.is_equal).then_inc(s_seen_step, 1)
                    dve.wait_ge(s_seen_step, first + 1)
                    nc.vector.tensor_tensor(lo, eq, lower.unsqueeze(1).to_broadcast([P, TILES, P]), ALU.mult)\
                      .then_inc(s_seen_step, 1)
                    dve.wait_ge(s_seen_step, first + 2)
                    nc.vector.tensor_reduce(seen[which][:, bass.ds(n * TILES, TILES)], lo, AX_X, ALU.max)\
                      .then_inc(s_seen_step, 1)
                with dve.Fori(0, H) as half:
                    for b in range(2):
                        search(half * 2 + b, b, half)
            dve.wait_ge(s_seen_step, 3 * G * 2)
            step = [0]

            def link(ins):
                ins.then_inc(s_vec, 1)
                step[0] += 1
                dve.wait_ge(s_vec, step[0])

            dve.wait_ge(s_len, 1)
            link(nc.vector.tensor_tensor(square, vec3, inv_len.unsqueeze(2).to_broadcast([P, G * TILES, 3]), ALU.mult))
            for k in range(2):
                for rec, at in ((front_all[k], TILES), (back_all[k], 2 * TILES)):
                    e = rec[:, :, at:at + TILES * EXT].rearrange("p g (t c) -> p g t c", c=EXT)
                    if k == 0:
                        vec, lo = square.rearrange("p (g t) c -> p g t c", t=TILES), 0
                        for t in range(TILES):
                            nc.vector.memset(e[:, :, t, 0:1], 1.0)
                    else:
                        vec, lo = vec4.rearrange("p (g t) c -> p g t c", t=TILES), 1
                    for t in range(TILES):
                        if k:
                            nc.vector.tensor_copy(e[:, :, t, 0:1], vec[:, :, t, 0:1])
                        nc.vector.tensor_copy(e[:, :, t, 1:4], vec[:, :, t, lo:lo + 3])
                        nc.vector.tensor_copy(e[:, :, t, 4:6], vec[:, :, t, lo:lo + 2])
                source, target = ((dst_idx, src_idx), (src_idx, dst_idx))[k]

                def lanes(a):
                    return a.bitcast(I32).rearrange("p (g t) -> p g t", t=TILES)

                nc.vector.tensor_copy(front_all[k][:, :, 0:TILES].bitcast(I32), lanes(source))
                nc.vector.tensor_copy(back_all[k][:, :, 0:TILES].bitcast(I32), lanes(target))
                link(nc.vector.tensor_scalar(moved, target.bitcast(I32), -1.0, spare, ALU.mult, ALU.add))
                link(nc.vector.tensor_tensor(moved, moved, seen[k], ALU.mult))
                link(nc.vector.tensor_tensor(back_all[k][:, :, TILES:2 * TILES].bitcast(I32),
                                             moved.rearrange("p (g t) -> p g t", t=TILES), lanes(target), ALU.add))
            dve.drain().then_inc(s_rec, 1)
            barrier(dve, 1)
            dve_node(dve, 0)
            for l in range(LAYERS):
                dve_edge(dve, l)
                dve_node(dve, l + 1)

        def act_edge(act, l):
            key = ("edge", l)
            nk, width = OUT_V[l], WIDTH[l]

            def hide(g):
                b = g.odd
                act.wait_ge(wide_mm.sem, wide_mm.at(key, g.n * 4 + 1))
                act.wait_ge(wide_mm.sem, wide_mm.at(key, (g.n - 1) * 4))
                nc.scalar.activation(hidden[b][0:FC_HID[l], :], psum[0:FC_HID[l], WIDE[0], :],
                                     ACT.Relu if l == 0 else ACT.Silu).then_inc(wide_copied.sem, 1)

            def weight(g, s):
                rows = (2 * S, 3 * V, 4 * V if CROSS[l] else V)[s]
                r = (g.odd + s) % 2
                act.wait_ge(wide_mm.sem, wide_mm.at(key, g.n * 4 + s + 2))
                act.wait_ge(message_made.sem, message_made.at(key, g.n * 3 + s - 1))
                nc.scalar.copy(w_sb[r][0:rows, :], psum[0:rows, WIDE[(s + 1) % 2], :]).then_inc(wide_copied.sem, 1)

            def copy_message(g):
                b = g.odd
                for t in range(TILES):
                    n = g.n * TILES + t
                    act.wait_ge(msg_mm.sem, msg_mm.at(key, n + 1))
                    if t == 0:
                        act.wait_ge(sum_mm.sem, sum_mm.at(key, (g.n - 1) * TILES))
                    nc.scalar.copy(edge_out[b][:, t, 0:width + nk], psum[:, MSG[t % 2], 0:width + nk])\
                      .then_inc(msg_copied.sem, 1)

            def copy_sum(g):
                b = g.odd
                for t in range(TILES):
                    n = g.n * TILES + t
                    act.wait_ge(sum_mm.sem, sum_mm.at(key, n + 1))
                    if t == 0:
                        act.wait_ge(landed.sem, landed.at(key, g.n))
                    nc.scalar.copy(summed[b][:, t, 0:width], psum[:, SUM[t % 2], 0:width]).then_inc(sum_copied.sem, 1)

            def step(g, has_back, has_it, has_ahead):
                if has_back:
                    copy_message(g.back())
                if has_it:
                    for s in range(3):
                        weight(g, s)
                if has_ahead:
                    hide(g.ahead())
                if has_back:
                    copy_sum(g.back())

            hide(Group(0, 0))
            over_groups(act, step)
            barrier(act, 3 + 2 * l)

        def act_node(act, k):
            key = ("node", k)

            def gate(g):
                b = g.odd
                if k == 1:
                    act.wait_ge(node_in[b].sem, node_in[b].at(key, g.half + 1))
                else:
                    first, step = combine_step.first[key]
                    act.wait_ge(combine_step.sem, g.n * step + (first + 1))
                act.wait_ge(combined.sem, combined.at(key, g.n - 1))
                nc.scalar.activation(gates[b], tot_in[b][:, :, 3 * V:WIDTH[0]], ACT.Sigmoid).then_inc(gated.sem, 1)

            def copy_x(g):
                b = g.odd
                act.wait_ge(x_turned.sem, x_turned.at(key, g.n + 1))
                act.wait_ge(lin_mm.sem, lin_mm.at(key, (g.n - 1) * TILES))
                nc.scalar.copy(v_cols[b][0:3 * V, :], psum[0:3 * V, 6 * b, :])
                nc.scalar.copy(s_cols[b][0:S, :], psum[0:S, 6 * b + 1, :]).then_inc(x_copied.sem, 1)

            def linear_out(g):
                b = g.odd
                for t in range(TILES):
                    n = g.n * TILES + t
                    skip = 3 * V + SKIP_S[k]
                    acc = psum[:, 2 + t % 2, :]
                    if t == 0:
                        act.wait_ge(stored[b].sem, stored[b].at(key, g.half))
                    act.wait_ge(lin_mm.sem, lin_mm.at(key, n + 1))
                    if k in (0, 3):
                        last = nc.scalar.copy(tot_out[b][:, t, 0:skip], acc[:, 0:skip])
                    else:
                        last = nc.scalar.activation(h_out[b][:, t, :], acc[:, 0:HROW], ACT.Copy,
                                                    scale=attr[b][:, t:t + 1])
                    last.then_inc(lin_act.sem, 1)

            def step(g, has_back, has_it, has_ahead):
                if has_it and k in (1, 4):
                    gate(g)
                if has_back and k < LAYERS:
                    linear_out(g.back())
                if has_it and k < LAYERS:
                    copy_x(g)

            over_groups(act, step)
            barrier(act, 2 + 2 * k)

        @block.scalar
        def _(act):
            for i, (left, right, cols) in enumerate(comp_parts):
                act.wait_ge(s_comp_mm, i + 1)
                acc = psum[:, i, :]
                nc.scalar.mul(comp[0:S, comp_at[i]:comp_at[i] + cols], acc[0:S, 0:cols], C_X / 4)
                nc.scalar.mul(comp[S:S + V, comp_at[i]:comp_at[i] + cols], acc[S:S + V, 0:cols],
                              C_X / 4 * (r3 if cols == S else 1.0)).then_inc(s_comp, 1)
            barrier(act, 1)
            act_node(act, 0)
            for l in range(LAYERS):
                act_edge(act, l)
                act_node(act, l + 1)

        def pe_edge(pe, l):
            key = ("edge", l)
            nk, ns, width = OUT_V[l], OUT_S[l], WIDTH[l]
            x_rows = REGIONS[f"rx_{l}"][1]

            def hide(g):
                b = g.odd
                pe.wait_ge(front_in[b].sem, front_in[b].at(key, g.half + 1))
                pe.wait_ge(wide_copied.sem, wide_copied.at(key, g.n * 4 - 1))
                settle(pe)
                nc.tensor.matmul(psum[0:FC_HID[l], WIDE[0], :], w(f"fc1_{l}"), edge_feat[b][0:FC_IN[l], :],
                                 start=True, stop=True).then_inc(wide_mm.sem, 1)

            def weigh_and_turn(g, s):
                b = g.odd
                n = g.n * 3 + s
                r = (g.odd + s) % 2
                name, rows = ((f"w12_{l}", 2 * S), (f"wv_{l}", 3 * V), (f"wx_{l}", 4 * V if CROSS[l] else V))[s]
                pe.wait_ge(wide_copied.sem, wide_copied.at(key, g.n * 4 + 1 if s == 0 else g.n * 4 + s))
                settle(pe)
                nc.tensor.matmul(psum[0:rows, WIDE[(s + 1) % 2], :], w(name), hidden[b][0:FC_HID[l], :],
                                 start=True, stop=True).then_inc(wide_mm.sem, 1)
                pe.wait_ge(prepared.sem, prepared.at(key, g.n + 1))
                pe.wait_ge(message_made.sem, message_made.at(key, n - 1))
                for t in range(TILES):
                    src = (gath[b][:, t, 3 * V:3 * V + 2 * S],
                           (v_e0[b] if HAS_E0[l] else gath[b])[:, t, 0:3 * V],
                           dot_cross[b][:, t, 0:rows])[s]
                    last = nc.tensor.transpose(psum[0:rows, TURN[r], t * P:(t + 1) * P], src, ident)
                last.then_inc(turned.sem, 1)

            def output(g):
                b = g.odd
                for t in range(TILES):
                    n = g.n * TILES + t
                    if t == 0:
                        pe.wait_ge(message_made.sem, message_made.at(key, (g.n + 1) * 3))
                    pe.wait_ge(msg_copied.sem, msg_copied.at(key, n - 1))
                    acc = psum[:, MSG[t % 2], :]
                    cols = slice(t * P, (t + 1) * P)
                    m12, m3, mx = message[b]
                    nc.tensor.matmul(acc[:, 0:3 * nk], m3[0:3 * V, cols], w(f"r3_{l}"), start=True, stop=False,
                                     skip_group_check=True)
                    nc.tensor.matmul(acc[:, 3 * nk:width + nk], m12[:, cols], w(f"r12_{l}"), start=False, stop=False,
                                     skip_group_check=True)
                    to = acc[:, 0:width] if CROSS[l] else acc[:, 3 * nk:width]
                    nc.tensor.matmul(to, mx[0:x_rows, cols], w(f"rx_{l}"), start=False, stop=True,
                                     skip_group_check=True).then_inc(msg_mm.sem, 1)

            def sum_same(g):
                b = g.odd
                for t in range(TILES):
                    n = g.n * TILES + t
                    if t == 0:
                        pe.wait_ge(outer_added.sem, outer_added.at(key, g.n + 1))
                        pe.wait_ge(same_made.sem, same_made.at(key, g.n + 1))
                    pe.wait_ge(sum_copied.sem, sum_copied.at(key, n - 1))
                    nc.tensor.matmul(psum[:, SUM[t % 2], 0:width], same[b][:, t, :], edge_out[b][:, t, 0:width],
                                     start=True, stop=True).then_inc(sum_mm.sem, 1)

            def step(g, has_back, has_it, has_ahead):
                if has_back:
                    output(g.back())
                if has_it:
                    for s in range(3):
                        weigh_and_turn(g, s)
                if has_ahead:
                    hide(g.ahead())
                if has_back:
                    sum_same(g.back())

            hide(Group(0, 0))
            over_groups(pe, step)
            barrier(pe, 3 + 2 * l)

        def pe_node(pe, k):
            key = ("node", k)

            def turn(g):
                b = g.odd
                if k == 0:
                    pe.wait_ge(node_in[b].sem, node_in[b].at(key, g.half + 1))
                else:
                    pe.wait_ge(normed.sem, normed.at(key, g.n + 1))
                pe.wait_ge(x_copied.sem, x_copied.at(key, g.n - 1))
                for t in range(TILES):
                    cols = slice(t * P, (t + 1) * P)
                    nc.tensor.transpose(psum[0:3 * V, 6 * b, cols], x_new[b][:, t, 0:3 * V], ident)
                    last = nc.tensor.transpose(psum[0:S, 6 * b + 1, cols], x_new[b][:, t, 3 * V:HROW], ident)
                last.then_inc(x_turned.sem, 1)

            def linear(g):
                b = g.odd
                for t in range(TILES):
                    n = g.n * TILES + t
                    if t == 0:
                        pe.wait_ge(x_copied.sem, x_copied.at(key, g.n + 1))
                    pe.wait_ge(lin_act.sem, lin_act.at(key, n - 1))
                    pe.wait_ge(lin_dve.sem, lin_dve.at(key, n - 1))
                    cols = slice(t * P, (t + 1) * P)
                    vt, st = v_cols[b][0:3 * V, cols], s_cols[b][0:S, cols]
                    for to, name_v, name_s, c in linear_places(k, t):
                        v0, s0, v1, s1 = (0, 0, 3 * V, SKIP_S[k]) if c == "skip" else (3 * V, SKIP_S[k], 6 * V, None)
                        ns = (SKIP_S[k] if c == "skip" else S)
                        nc.tensor.matmul(to[:, 0:3 * V], vt, w(name_v, c0=v0, c1=v1), start=True, stop=True)
                        last = nc.tensor.matmul(to[:, 3 * V:3 * V + ns], st, w(name_s, c0=s0, c1=s1),
                                                start=True, stop=True)
                    last.then_inc(lin_mm.sem, 1)

            def step(g, has_back, has_it, has_ahead):
                if has_back and k < LAYERS:
                    linear(g.back())
                if has_it and k < LAYERS:
                    turn(g)

            over_groups(pe, step)
            barrier(pe, 2 + 2 * k)

        @block.tensor
        def _(pe):
            pe.wait_ge(s_const, 32)
            for i, (left, right, cols) in enumerate(comp_parts):
                nc.tensor.matmul(psum[0:S + V, i, 0:cols], w(left), w(right), start=True, stop=True)\
                  .then_inc(s_comp_mm, 1)
            barrier(pe, 1)
            pe_node(pe, 0)
            for l in range(LAYERS):
                pe_edge(pe, l)
                pe_node(pe, l + 1)


def pack_weights(i):
    def l_(layer, name):
        return np.asarray(i[f"L{layer}_gnn_{name}"])

    def diag(m):
        out = np.zeros((3 * m.shape[0], 3 * m.shape[1]), np.float32)
        for c in range(3):
            out[c * m.shape[0]:(c + 1) * m.shape[0], c * m.shape[1]:(c + 1) * m.shape[1]] = m
        return out

    fc1 = [l_(0, "W_fc1"), l_(1, "Wfc1"), l_(2, "W_fc1"), l_(3, "fc_w1")]
    fc2 = [l_(0, "W_fc2"), l_(1, "Wfc2"), l_(2, "W_fc2"), l_(3, "fc_w2")]
    out_s = [l_(0, "W_out_s"), np.concatenate([l_(1, "Wl2_s"), l_(1, "Wa"), np.zeros((S + V, 1), np.float32)], 1),
             None, l_(3, "lin2_ws")]
    out_v = [l_(0, "W_out_v"), l_(1, "Wl2_v"), None, l_(3, "lin2_wv")]
    skip = {"a_0": ("W_skip0", "W_skip1", "W_nl0", "W_nl1"), "a_1": ("Wsc0", "Wsc1", "Wl1_0", "Wl1_1"),
            "a_2": ("Ws_sc_a", "Wv_sc_a", "Ws_l1_a", "Wv_l1_a"), "c_2": ("Ws_sc_c", "Wv_sc_c", "Ws_l1_c", "Wv_l1_c"),
            "a_3": ("sc_ws", "sc_wv", "lin1_ws", "lin1_wv")}
    m = {}
    for l in range(LAYERS):
        f = fc2[l]
        m[f"fc1_{l}"] = fc1[l]
        m[f"w12_{l}"] = np.concatenate([f[:, S:2 * S], f[:, 0:S]], 1)
        m[f"wv_{l}"] = np.concatenate([f[:, 2 * S:2 * S + V]] * 3, 1)
        dot, cross = f[:, 2 * S + V:2 * S + 2 * V], f[:, 2 * S + 2 * V:]
        m[f"wx_{l}"] = np.concatenate([dot] + [cross] * 3, 1) if CROSS[l] else dot
        if l != 2:
            ns, nk = OUT_S[l], OUT_V[l]
            r12 = np.zeros((2 * S, ns + nk), np.float32)
            r12[S:, 0:ns] = out_s[l][0:S]
            r12[0:S, ns:] = out_v[l][0:S]
            m[f"r12_{l}"] = r12
            m[f"r3_{l}"] = diag(out_v[l][S:S + V])
            if CROSS[l]:
                rx = np.zeros((4 * V, 3 * nk + ns), np.float32)
                rx[0:V, 3 * nk:] = out_s[l][S:]
                rx[V:, 0:3 * nk] = diag(out_v[l][S + V:])
            else:
                rx = np.zeros((V + 1, ns), np.float32)
                rx[0:V] = out_s[l][S:]
                rx[V, ns - 1] = 1.0
            m[f"rx_{l}"] = rx
    for key, (ss, sv, hs, hv) in skip.items():
        layer = int(key[-1])
        m[f"nv{key}"] = np.concatenate([diag(l_(layer, sv)), diag(l_(layer, hv))], 1)
        m[f"ns{key}"] = np.concatenate([l_(layer, ss), l_(layer, hs)], 1)
    m["lsa"], m["lsc"] = l_(2, "Ws_l2_a").T, l_(2, "Ws_l2_c").T
    m["lva"], m["lvc"] = l_(2, "Wv_l2_a").T, l_(2, "Wv_l2_c").T
    m["l3s"], m["l3v"] = l_(2, "Ws_l3"), l_(2, "Wv_l3")
    packed = np.zeros((P, WCOLS), np.float32)
    for name, a in m.items():
        at, rows, cols = REGIONS[name]
        assert a.shape == (rows, cols), (name, a.shape, rows, cols)
        packed[0:rows, at:at + cols] = a
    return packed


def lay_out(i):
    def padded(a, fill):
        a = np.asarray(a)
        return np.concatenate([a, np.full((NPAD - N,) + a.shape[1:], fill, a.dtype)])

    def edge_lanes(a):
        a = a.reshape(GROUPS, TILES, P, -1)
        return np.ascontiguousarray(a.transpose(2, 0, 1, 3).reshape(P, -1))

    x = np.asarray(i["x"])
    vec = x[:, S:].reshape(N, V, 3).transpose(0, 2, 1).reshape(N, 3 * V)
    out = {"x": padded(np.concatenate([vec, x[:, 0:S]], 1), 0.0)}
    for name in ("src", "dst"):
        idx = padded(i[name], N)
        out[f"{name}_lanes"] = edge_lanes(idx)
        out[f"{name}_rows"] = idx.reshape(GROUPS, GROUP)
    out["vec3"] = edge_lanes(padded(i["edge_attr_3"], 1.0))
    out["vec4"] = edge_lanes(padded(i["edge_attr_4"], 0.0))
    for l, name in enumerate(("edge_attr_64", "edge_attr_16", "edge_attr_10", "edge_attr_64")):
        out[f"feat{l}"] = np.ascontiguousarray(padded(i[name], 0.0).T)
    attrs = np.stack([padded(i[n], 0.0)[:, 0] for n in ("node_vec1", "node_vec1_n2", "node_vec1_n3")])
    out["attrs"] = np.ascontiguousarray(attrs.reshape(3, GROUPS, P, TILES).transpose(2, 1, 0, 3).reshape(P, -1))
    out["weights"] = pack_weights(i)
    const = np.zeros((P, 2 * P + 1), np.float32)
    const[:, 0:P] = np.eye(P)
    const[:, P:2 * P] = np.tril(np.ones((P, P)), -1)
    const[:, 2 * P] = NPAD + np.arange(P)
    out["consts"] = const
    return out


def kernel(**inputs):
    import concourse.bacc as bacc
    from concourse.bass_utils import run_bass_kernel_spmd

    nc = bacc.Bacc("TRN2", target_bir_lowering=False, num_devices=1)
    arrays = {f"in_{k}": v for k, v in lay_out(inputs).items()}
    d = {k[3:]: nc.dram_tensor(k, v.shape, mybir.dt.from_np(v.dtype), kind="ExternalInput").ap()
         for k, v in arrays.items()}
    d["out"] = nc.dram_tensor("out", [NPAD, HROW], F32, kind="ExternalOutput").ap()
    build(nc, d)
    r = run_bass_kernel_spmd(nc, [arrays], core_ids=[0])
    got = r.results[0]["out"][0:N]
    vec = got[:, 0:3 * V].reshape(N, 3, V).transpose(0, 2, 1).reshape(N, 3 * V)
    return np.concatenate([got[:, 3 * V:], vec], 1)
```

```python
from contextlib import ExitStack

import numpy as np
import concourse.bass as bass
from concourse import mybir

F32 = mybir.dt.float32
I32 = mybir.dt.int32
ALU = mybir.AluOpType
ACT = mybir.ActivationFunctionType
AX_X = mybir.AxisListType.X

P = 128
TILES = 4
GROUP = P * TILES
N = 50000
GROUPS = -(-N // GROUP)
NPAD = GROUPS * GROUP
ROWS = NPAD + 2 * P
S, V = 64, 32
HROW = 3 * V + S
LAYERS = 4
NORM_EPS = 1e-5

FC_IN = [64, 16, 10, 64]
FC_HID = [64, 64, 100, 64]
OUT_S = [96, 66, 128, 96]
OUT_V = [32, 32, 64, 32]
CROSS = [True, False, False, True]
HAS_E0 = [False, True, True, True]
WIDTH = [3 * OUT_V[l] + OUT_S[l] for l in range(LAYERS)]
SKIP_S = [96, 64, 64, 96]
ACT_PAIRS = [1, 2, 2, 2]
DVE_PAIRS = [1, 2, 2, 0]

EXT = 6
REC_F = TILES + TILES * EXT
REC_B = 2 * TILES + TILES * EXT


def weight_regions():
    out, at = {}, 0

    def add(name, rows, cols):
        nonlocal at
        out[name] = (at, rows, cols)
        at += cols

    for l in range(LAYERS):
        add(f"fc1_{l}", FC_IN[l], FC_HID[l])
        add(f"w12_{l}", FC_HID[l], 2 * S)
        add(f"wv_{l}", FC_HID[l], 3 * V)
        add(f"wx_{l}", FC_HID[l], 4 * V if CROSS[l] else V)
        add(f"r12_{l}", 2 * S, OUT_S[l] + OUT_V[l])
        add(f"r3_{l}", 3 * V, 3 * OUT_V[l])
        add(f"rx_{l}", 4 * V if CROSS[l] else V + (l == 1), WIDTH[l] if CROSS[l] else OUT_S[l])
        for part in ("a", "c") if l == 2 else ("a",):
            add(f"nv{part}_{l}", 3 * V, 6 * V)
            add(f"ns{part}_{l}", S, SKIP_S[l] + S)
    for name in ("lsa", "lsc", "lva", "lvc"):
        add(name, S + V, S + V)
    add("l3s", S + V, S)
    add("l3v", S + V, V)
    return out, at


REGIONS, WCOLS = weight_regions()


class Tally:

    def __init__(self, sem, credit):
        self.sem, self.total, self.first = sem, credit, {}

    def phase(self, key, step, times):
        self.first[key] = (self.total, step)
        self.total += step * times

    def at(self, key, n):
        first, step = self.first[key]
        return max(n, 0) * step + first if isinstance(n, int) else n * step + first

    def at_pair(self, key, n, pair):
        return self.first[key][0] if isinstance(n, int) and n < 0 else self.at(key, n) + (pair + 1)


class Group:

    def __init__(self, half, odd):
        self.half, self.odd = half, odd
        self.n = half * 2 + odd

    def back(self):
        return Group(self.half, 0) if self.odd else Group(self.half - 1, 1)

    def ahead(self):
        return Group(self.half + 1, 0) if self.odd else Group(self.half, 1)


def over_groups(eng, step, peeled=1):
    step(Group(0, 0), False, True, True)
    step(Group(0, 1), True, True, True)
    with eng.Fori(1, GROUPS // 2 - peeled) as half:
        step(Group(half, 0), True, True, True)
        step(Group(half, 1), True, True, True)
    for half in range(GROUPS // 2 - peeled, GROUPS // 2 - 1):
        step(Group(half, 0), True, True, True)
        step(Group(half, 1), True, True, True)
    step(Group(GROUPS // 2 - 1, 0), True, True, True)
    step(Group(GROUPS // 2 - 1, 1), True, True, False)
    step(Group(GROUPS // 2, 0), True, False, False)


def build(nc, d):
    assert GROUPS % 2 == 0
    ctx = ExitStack()
    with ctx:
        def sb(name, shape, dt=F32):
            return ctx.enter_context(nc.sbuf_tensor(name, shape, dt))

        def sem(name):
            return ctx.enter_context(nc.semaphore(name))

        def dram(name, shape):
            return nc.dram_tensor(name, shape, F32).ap()

        h_table = [dram(f"h_table{l}", [NPAD, HROW]) for l in range(LAYERS)]
        totals = [dram(f"totals{l}", [ROWS, WIDTH[l]]) for l in range(LAYERS)]
        base = [d["x"]] + [dram(f"base{l}", [NPAD, HROW]) for l in range(1, LAYERS)]
        rec_f = [dram(f"rec_f{k}", [P, GROUPS * REC_F]) for k in range(2)]
        rec_b = [dram(f"rec_b{k}", [P, GROUPS * REC_B]) for k in range(2)]

        weights = sb("weights", [P, WCOLS])
        consts = sb("consts", [P, 3 * P + 2])
        ident = consts[:, 0:P]
        earlier = consts[:, P:3 * P]
        spare = consts[:, 3 * P:3 * P + 2]
        zeros = sb("zeros", [P, TILES * max(WIDTH)])
        power = sb("power", [P, TILES * GROUPS])

        def w(name, r0=0, r1=None, c0=0, c1=None):
            at, rows, cols = REGIONS[name]
            return weights[r0:rows if r1 is None else r1, at + c0:at + (cols if c1 is None else c1)]

        area = sb("area", [P, 30000])
        area_at = [0]

        def part(shape):
            size = int(np.prod(shape))
            a = area[:, area_at[0]:area_at[0] + size]
            area_at[0] += size
            if len(shape) == 2:
                a = a.rearrange("p (a b) -> p a b", b=shape[1])
            return a

        src_idx = part([GROUPS * TILES])
        dst_idx = part([GROUPS * TILES])
        vec3 = part([GROUPS * TILES, 3])
        vec4 = part([GROUPS * TILES, 4])
        square = part([GROUPS * TILES, 3])
        inv_len = part([GROUPS * TILES])
        sum_sq = part([GROUPS * TILES])
        seen = [part([GROUPS * TILES]) for _ in range(2)]
        moved = part([GROUPS * TILES])
        front_all = [part([GROUPS, REC_F]) for _ in range(2)]
        back_all = [part([GROUPS, REC_B]) for _ in range(2)]
        row_prep = [part([GROUP]) for _ in range(2)]
        matches = [part([2 * P]) for _ in range(TILES)]
        own_f = [part([GROUPS * TILES]) for _ in range(2)]
        comp = part([2 * S + 2 * V])
        assert area_at[0] <= 30000, area_at

        area_at[0] = 0
        front_rec = [part([REC_F]) for _ in range(2)]
        back_rec = [part([REC_B]) for _ in range(2)]
        target_row = [part([GROUP]) for _ in range(2)]
        edge_feat = [part([GROUP]) for _ in range(2)]
        gath = [part([TILES, HROW + S]) for _ in range(2)]
        v_e0 = [part([TILES, 3 * V]) for _ in range(2)]
        dot_cross = [part([TILES, 4 * V]) for _ in range(2)]
        prod_dot = part([TILES, 3 * V])
        prod_a = part([TILES, 3 * V])
        prod_b = part([TILES, 3 * V])
        hidden = [part([GROUP]) for _ in range(2)]
        w_sb = [part([GROUP]) for _ in range(2)]
        message = [[part([GROUP]) for _ in range(3)] for _ in range(2)]
        same = [part([TILES + TILES // 2, P]) for _ in range(2)]
        edge_out = [part([TILES, 384]) for _ in range(2)]
        outer = part([TILES, 3 * max(OUT_V)])
        summed = [part([TILES, max(WIDTH)]) for _ in range(2)]
        assert area_at[0] <= 30000, area_at

        area_at[0] = 0
        base_in = [part([TILES, HROW]) for _ in range(2)]
        tot_in = [part([TILES, max(WIDTH)]) for _ in range(2)]
        attr_in = [part([3 * TILES]) for _ in range(2)]
        attr = [part([3 * TILES]) for _ in range(2)]
        gates = [part([TILES, S + V]) for _ in range(2)]
        factor = part([6 * TILES])
        y = [part([TILES, HROW]) for _ in range(2)]
        stats = part([TILES, 6])
        moments = [part([TILES, 2]) for _ in range(2)]
        var_eps = [part([TILES]) for _ in range(2)]
        rstd = [part([TILES]) for _ in range(2)]
        x_new = [part([TILES, HROW]) for _ in range(2)]
        x_scaled = [[part([TILES, HROW]) for _ in range(2)] for _ in range(2)]
        v_cols = [[part([GROUP]) for _ in range(2)] for _ in range(2)]
        s_cols = [[part([GROUP]) for _ in range(2)] for _ in range(2)]
        h_out = [part([TILES, HROW]) for _ in range(2)]
        tot_out = [part([TILES, max(WIDTH)]) for _ in range(2)]
        base_out = [part([TILES, HROW]) for _ in range(2)]
        assert area_at[0] <= 30000, area_at

        psum = ctx.enter_context(nc.psum_tensor("psum", [P, 8, GROUP], F32))
        WIDE, TURN, MSG, SUM = (0, 1), (2, 3), (4, 5), (6, 7)

        credited = []

        def tally(name, plan, kind=""):
            t = Tally(sem(name), {"": 1, "dma": 0, "dma, credited": 16}[kind])
            for key, step, times in plan:
                t.phase(key, step, times)
            if not kind:
                credited.append(t)
            return t

        G, H = GROUPS, GROUPS // 2

        def edges(step, times):
            return [(("edge", l), step, times) for l in range(LAYERS)]

        def nodes(step, times, passes=range(LAYERS + 1)):
            return [(("node", l), step(l) if callable(step) else step, times) for l in passes]

        s_const = sem("s_const")
        s_edges_in = sem("s_edges_in")
        s_fill = sem("s_fill")
        s_scaled = sem("s_scaled")
        s_comp_mm = sem("s_comp_mm")
        s_comp = sem("s_comp")
        s_comp_put = sem("s_comp_put")
        s_sq = sem("s_sq")
        s_len = sem("s_len")
        s_vec = sem("s_vec")
        s_row_prep = [sem(f"s_row_prep{b}") for b in range(2)]
        s_seen_step = sem("s_seen_step")
        s_own = sem("s_own")
        s_rec = sem("s_rec")
        s_rec_out = sem("s_rec_out")
        s_barrier = sem("s_barrier")
        s_settled = {e: sem(f"s_settled_{n}") for n, e in
                     (("sp", nc.sync.engine), ("pool", nc.gpsimd.engine), ("dve", nc.vector.engine),
                      ("pe", nc.tensor.engine))}

        front_in = [tally(f"front_in{b}", edges(32, H), kind="dma") for b in range(2)]
        back_in = [tally(f"back_in{b}", edges(32, H), kind="dma") for b in range(2)]
        gathered = [tally(f"gathered{b}", edges(64, H), kind="dma") for b in range(2)]
        scattered = tally("scattered", edges(16, TILES * G), kind="dma")
        landed = tally("landed", edges(1, G))
        multiplied = tally("multiplied", edges(1, G))
        prepared = tally("prepared", edges(1, G))
        wide_mm = tally("wide_mm", edges(1, 4 * G))
        wide_copied = tally("wide_copied", edges(1, 4 * G))
        turned = tally("turned", edges(1, 3 * G))
        message_made = tally("message_made", edges(1, 3 * G))
        msg_mm = tally("msg_mm", edges(1, TILES * G))
        msg_copied = tally("msg_copied", edges(1, TILES * G))
        outer_made = tally("outer_made", edges(1, G))
        outer_added = tally("outer_added", edges(1, G))
        same_made = tally("same_made", edges(1, G))
        sum_mm = tally("sum_mm", edges(1, TILES * G))
        sum_copied = tally("sum_copied", edges(1, TILES * G))

        inner = range(LAYERS)
        fin = range(1, LAYERS + 1)
        node_in = [tally(f"node_in{b}", nodes(lambda k: 16 if k == 0 else 48, H), kind="dma") for b in range(2)]
        combine_step = tally("combine_step", nodes(lambda k: {1: 1, 2: 6, 3: 2, 4: 2}[k], G, fin))
        gated = tally("gated", nodes(1, G, [1, 4]))
        combined = tally("combined", nodes(1, G, fin))
        stats_made = tally("stats_made", nodes(1, G, fin))
        moments_made = tally("moments_made", nodes(1, G, fin))
        var_made = tally("var_made", nodes(1, G, fin))
        rstd_made = tally("rstd_made", nodes(1, G, fin))
        normed = tally("normed", nodes(1, G, fin))
        x_turned = tally("x_turned", nodes(1, G, inner))
        x_copied = tally("x_copied", nodes(1, G, inner))
        scaled = tally("scaled", nodes(1, G, [1, 2, 3]))
        lin_mm = tally("lin_mm", nodes(2, G, inner))
        lin_act = tally("lin_act", nodes(lambda k: ACT_PAIRS[k], G, inner))
        lin_dve = tally("lin_dve", nodes(lambda k: DVE_PAIRS[k], G, [0, 1, 2]))
        stored = [tally(f"stored{b}", nodes(lambda k: (32, 48, 48, 32)[k], H, inner), kind="dma, credited")
                  for b in range(2)]
        x_stored = [tally(f"x_stored{b}", nodes(16, H, [3, 4]), kind="dma") for b in range(2)]

        block = ctx.enter_context(nc.Block())

        def barrier(eng, count):
            eng.drain().then_inc(s_barrier, 1)
            eng.wait_ge(s_barrier, 5 * count)

        def is_last_ahead(g):
            return isinstance(g.half, int) and g.half == H - 1

        def is_third_last(g):
            return isinstance(g.half, int) and g.half == H - 2 and g.odd == 1

        def settle(eng):
            eng.sem_inc(s_settled[eng.engine], 1)

        def lin_banks(pair):
            return psum[:, 4 + 2 * pair:6 + 2 * pair, :]

        def lin_h(pair):
            return lin_banks(pair)[:, :, 3 * V:3 * V + HROW]

        def lin_skip_96(pair):
            return lin_banks(pair).rearrange("p t (u c) -> p t u c", u=2)[:, :, :, 0:3 * V]

        def pair_of(tile, pair, lo, hi):
            return tile[:, 2 * pair:2 * pair + 2, lo:hi]

        def paths(k):
            return 2 if k == 2 else 1

        r2, r3, r32, r96, r128 = 2 ** -0.5, 3 ** -0.5, 32 ** -0.5, 96 ** -0.5, 128 ** -0.5
        C_S, C_X = float(np.sin(np.pi / 8)), float(np.cos(np.pi / 8))
        scales = [("r12_0", 0, 64, 3 ** 0.5 / 32), ("r12_0", 64, 128, 1 / 32), ("r3_0", 0, 96, 1 / 32),
                  ("rx_0", 0, 32, 1 / 32)]
        scales += [("rx_0", 32 * i, 32 * i + 32, 3 ** 0.5 * r2 / 32) for i in (1, 2, 3)]
        scales += [("fc1_1", 0, 16, 1 / 4), ("w12_1", 0, 64, 1 / 8), ("wv_1", 0, 64, 1 / 8),
                   ("wx_1", 0, 64, 1 / 8), ("r12_1", 0, 128, r96), ("r3_1", 0, 96, r96),
                   ("rx_1", 0, 32, r96 * r3), ("nva_1", 0, 96, r32), ("nsa_1", 0, 64, 1 / 8)]
        scales += [("fc1_3", 0, 64, 1 / 8), ("w12_3", 0, 64, 1 / 8), ("wv_3", 0, 64, 1 / 8),
                   ("wx_3", 0, 64, 1 / 8), ("nva_3", 0, 96, r32), ("nsa_3", 0, 64, 1 / 8),
                   ("r12_3", 0, 64, r128 / 4), ("r12_3", 64, 128, r96 / 4), ("r3_3", 0, 96, r128 / 4),
                   ("rx_3", 0, 32, r96 * r3 / 4)]
        scales += [("rx_3", 32 * i, 32 * i + 32, r128 * r2 / 4) for i in (1, 2, 3)]
        skip_scales = [("nva_2", 96, 96, C_S), ("nvc_2", 96, 96, C_S), ("nsa_2", 64, 64, C_S),
                       ("nsc_2", 64, 64, C_S)]

        comp_parts = [("lsa", "l3s", S), ("lsc", "l3s", S), ("lva", "l3v", V), ("lvc", "l3v", V)]
        comp_at = [0, S, 2 * S, 2 * S + V]

        def comp_moves():
            out = []
            for half in range(2):
                for which in range(2):
                    src = comp_at[which] + V * half
                    col = 2 * V * half + V * which
                    out.append((w("r12_2", S, 2 * S, col, col + V), comp[0:S, src:src + V]))
                    out.append((w("rx_2", 0, V, col, col + V), comp[S:S + V, src:src + V]))
            for which in range(2):
                src = comp_at[2 + which]
                col = OUT_S[2] + V * which
                out.append((w("r12_2", 0, S, col, col + V), comp[0:S, src:src + V]))
                for i in range(3):
                    col = 2 * V * i + V * which
                    out.append((w("r3_2", V * i, V * i + V, col, col + V), comp[S:S + V, src:src + V]))
            return out

        def edge_vec(rec, at, lo, hi):
            return rec[:, at:at + TILES * EXT].rearrange("p (t c) -> p t c", c=EXT)[:, :, lo:hi]

        def sp_edge(sp, l):
            key = ("edge", l)
            k = min(l, 1)

            def front(g):
                b = g.odd
                sp.wait_ge(gathered[b].sem, gathered[b].at(key, g.half))
                settle(sp)
                sp.wait_ge(prepared.sem, prepared.at(key, g.n - 1))
                settle(sp)
                sp.wait_ge(wide_mm.sem, wide_mm.at(key, (g.n - 2) * 4 + 1))
                settle(sp)
                sp.dma_start(front_rec[b], rec_f[k][:, bass.ds(g.n * REC_F, REC_F)]).then_inc(front_in[b].sem, 16)
                sp.dma_start(edge_feat[b][0:FC_IN[l], :], d[f"feat{l}"][:, bass.ds(g.n * GROUP, GROUP)])\
                  .then_inc(front_in[b].sem, 16)

            def back(g):
                b = g.odd
                rows = d["dst_rows"] if l else d["src_rows"]
                sp.wait_ge(outer_added.sem, outer_added.at(key, g.n - 1))
                settle(sp)
                sp.wait_ge(same_made.sem, same_made.at(key, g.n - 1))
                settle(sp)
                sp.wait_ge(scattered.sem, scattered.at(key, (g.n - 1) * TILES))
                settle(sp)
                sp.dma_start(back_rec[b], rec_b[k][:, bass.ds(g.n * REC_B, REC_B)]).then_inc(back_in[b].sem, 16)
                sp.dma_start(target_row[b].bitcast(I32), rows[bass.ds(g.n, 1), :].to_broadcast([P, GROUP]))\
                  .then_inc(back_in[b].sem, 16)

            def step(g, has_back, has_it, has_ahead):
                if has_ahead and not is_last_ahead(g):
                    front(g.ahead().ahead())
                if has_it:
                    back(g)

            front(Group(0, 0))
            front(Group(0, 1))
            over_groups(sp, step)
            barrier(sp, 3 + 2 * l)

        def sp_node(sp, k):
            key = ("node", k)

            def load(g):
                b = g.odd
                n = g.n * GROUP
                if k == 0:
                    sp.wait_ge(x_turned.sem, x_turned.at(key, g.n - 1))
                    settle(sp)
                    sp.dma_start(x_new[b].rearrange("p t c -> p (t c)"),
                                 d["x"][bass.ds(n, GROUP), :].rearrange("(p t) c -> p (t c)", t=TILES))\
                      .then_inc(node_in[b].sem, 16)
                    return
                sp.wait_ge(combined.sem, combined.at(key, g.n - 1))
                settle(sp)
                sp.dma_start(tot_in[b][:, :, 0:WIDTH[k - 1]],
                             totals[k - 1][bass.ds(n, GROUP), :].rearrange("(p t) c -> p t c", t=TILES))\
                  .then_inc(node_in[b].sem, 16)
                sp.dma_start(base_in[b].rearrange("p t c -> p (t c)"),
                             base[k - 1][bass.ds(n, GROUP), :].rearrange("(p t) c -> p (t c)", t=TILES))\
                  .then_inc(node_in[b].sem, 16)
                if k < LAYERS:
                    sp.wait_ge(scaled.sem, scaled.at(key, g.n - 1))
                    settle(sp)
                sp.dma_start(attr_in[b], d["attrs"][:, bass.ds(g.n * 3 * TILES, 3 * TILES)])\
                  .then_inc(node_in[b].sem, 16)

            def put(g, table, tile, done):
                sp.dma_start(table[bass.ds(g.n * GROUP, GROUP), :].rearrange("(p t) c -> p t c", t=TILES), tile)\
                  .then_inc(done[g.odd].sem, 16)

            def store_x(g):
                sp.wait_ge(normed.sem, normed.at(key, g.n + 1))
                settle(sp)
                put(g, d["out"] if k == LAYERS else base[3], x_new[g.odd], x_stored)

            def store(g):
                b = g.odd
                sp.wait_ge(lin_act.sem, lin_act.at(key, g.n + 1))
                settle(sp)
                if k != 3:
                    sp.wait_ge(lin_dve.sem, lin_dve.at(key, g.n + 1))
                    settle(sp)
                put(g, h_table[k], h_out[b], stored)
                if k in (0, 3):
                    put(g, totals[k], tot_out[b][:, :, 0:WIDTH[k]], stored)
                else:
                    put(g, totals[k], zeros[:, 0:TILES * WIDTH[k]].rearrange("p (t c) -> p t c", t=TILES),
                        stored)
                    put(g, base[k], base_out[b], stored)

            def step(g, has_back, has_it, has_ahead):
                if k == 0:
                    if has_ahead and not is_last_ahead(g):
                        load(g.ahead().ahead())
                elif has_ahead and not is_last_ahead(g) and not is_third_last(g):
                    load(g.ahead().ahead().ahead())
                if has_back:
                    (store_x if k == LAYERS else store)(g.back())
                if k == 3 and has_ahead:
                    store_x(g.ahead())

            load(Group(0, 0))
            load(Group(0, 1))
            if k:
                load(Group(1, 0))
            if k == 3:
                store_x(Group(0, 0))
            over_groups(sp, step, peeled=2)
            for b in range(2):
                if k < LAYERS:
                    sp.wait_ge(stored[b].sem, stored[b].at(key, H))
                if k >= 3:
                    sp.wait_ge(x_stored[b].sem, x_stored[b].at(key, H))
            barrier(sp, 2 + 2 * k)

        @block.sync
        def _(sp):
            for t in credited:
                sp.sem_inc(t.sem, 1)
            sp.dma_start(weights[:, :], d["weights"]).then_inc(s_const, 16)
            sp.dma_start(consts[:, :], d["consts"]).then_inc(s_const, 16)
            sp.dma_start(src_idx.bitcast(I32), d["src_lanes"]).then_inc(s_edges_in, 16)
            sp.dma_start(dst_idx.bitcast(I32), d["dst_lanes"]).then_inc(s_edges_in, 16)
            sp.dma_start(vec3.rearrange("p a b -> p (a b)"), d["vec3"]).then_inc(s_edges_in, 16)
            sp.dma_start(vec4.rearrange("p a b -> p (a b)"), d["vec4"]).then_inc(s_edges_in, 16)
            for which, rows in ((0, d["src_rows"]), (1, d["dst_rows"])):
                def row(n, b, u):
                    sp.dma_start(row_prep[b].bitcast(I32), rows[bass.ds(n, 1), :].to_broadcast([P, GROUP]))\
                      .then_inc(s_row_prep[b], 16)
                for b in range(2):
                    if which:
                        sp.wait_ge(s_seen_step, G * which + b - 1)
                    row(b, b, 0)
                with sp.Fori(1, H) as half:
                    for b in range(2):
                        sp.wait_ge(s_seen_step, half * 2 + (G * which + b - 1))
                        row(half * 2 + b, b, half)
            sp.wait_ge(s_comp, 4)
            sp.wait_ge(s_scaled, 1)
            moves = comp_moves()
            for dst, src in moves:
                sp.dma_start(dst, src).then_inc(s_comp_put, 16)
            sp.wait_ge(s_comp_put, 16 * len(moves))
            sp.wait_ge(s_rec, 1)
            sp.wait_ge(s_fill, 1)
            for k in range(2):
                sp.dma_start(rec_f[k], front_all[k].rearrange("p a b -> p (a b)")).then_inc(s_rec_out, 16)
                sp.dma_start(rec_b[k], back_all[k].rearrange("p a b -> p (a b)")).then_inc(s_rec_out, 16)
            spare_rows_in = (stored[0].sem, stored[1].sem, s_rec_out, s_rec_out)
            for l in range(LAYERS):
                sp.dma_start(totals[l][NPAD:ROWS, :].rearrange("(a p) c -> p a c", p=P),
                             zeros[:, 0:2 * WIDTH[l]].rearrange("p (a c) -> p a c", a=2)).then_inc(spare_rows_in[l], 16)
            for credit in spare_rows_in[0:2]:
                sp.wait_ge(credit, 16)
            sp.wait_ge(s_rec_out, 16 * 6)
            barrier(sp, 1)
            sp_node(sp, 0)
            for l in range(LAYERS):
                sp_edge(sp, l)
                sp_node(sp, l + 1)

        def pool_edge(pool, l):
            key = ("edge", l)

            def gather(g, t):
                b = g.odd
                if t == 0:
                    pool.wait_ge(front_in[b].sem, front_in[b].at(key, g.half + 1))
                    settle(pool)
                    pool.wait_ge(prepared.sem, prepared.at(key, g.n - 1))
                    settle(pool)
                    pool.wait_ge(turned.sem, turned.at(key, (g.n - 1) * 3))
                settle(pool)
                pool.indirect_dma_start(
                    gath[b][:, t, 0:HROW], None, h_table[l][:, :],
                    bass.IndirectOffsetOnAxis(front_rec[b][:, t:t + 1].bitcast(I32), 0)).then_inc(gathered[b].sem, 16)

            def scatter(g, t):
                b = g.odd
                if t == 0:
                    pool.wait_ge(back_in[b].sem, back_in[b].at(key, g.half + 1))
                    settle(pool)
                pool.wait_ge(sum_copied.sem, sum_copied.at(key, g.n * TILES + t + 1))
                settle(pool)
                if t % 2 == 0:
                    pool.wait_ge(scattered.sem, scattered.at(key, g.n * TILES + t))
                    pool.sem_inc(landed.sem if t == 0 else s_settled[nc.gpsimd.engine], 1)
                pool.indirect_dma_start(
                    totals[l][:, :], bass.IndirectOffsetOnAxis(back_rec[b][:, TILES + t:TILES + t + 1].bitcast(I32), 0),
                    summed[b][:, t, 0:WIDTH[l]], None, compute_op=ALU.add).then_inc(scattered.sem, 16)

            def step(g, has_back, has_it, has_ahead):
                for pair in range(TILES // 2):
                    for t in (2 * pair, 2 * pair + 1):
                        if has_back:
                            scatter(g.back(), t)
                    for t in (2 * pair, 2 * pair + 1):
                        if has_ahead and not is_last_ahead(g):
                            gather(g.ahead().ahead(), t)

            for g in (Group(0, 0), Group(0, 1)):
                for t in range(TILES):
                    gather(g, t)
            over_groups(pool, step)
            pool.wait_ge(scattered.sem, scattered.at(key, G * TILES))
            barrier(pool, 3 + 2 * l)

        def pool_node(pool, k):
            key = ("node", k)

            def root(g):
                b = g.odd
                pool.wait_ge(var_made.sem, var_made.at(key, g.n + 1))
                settle(pool)
                nc.gpsimd.tensor_tensor(rstd[b], var_eps[b], power[:, 0:TILES], ALU.pow).then_inc(rstd_made.sem, 1)

            def step(g, has_back, has_it, has_ahead):
                if has_ahead:
                    root(g.ahead())

            root(Group(0, 0))
            over_groups(pool, step)
            barrier(pool, 2 + 2 * k)

        @block.gpsimd
        def _(pool):
            pool.wait_ge(s_sq, 2)
            pool.wait_ge(s_fill, 1)
            nc.gpsimd.tensor_tensor(inv_len, sum_sq, power[:, 0:GROUPS * TILES], ALU.pow).then_inc(s_len, 1)
            barrier(pool, 1)
            barrier(pool, 2)
            for l in range(LAYERS):
                pool_edge(pool, l)
                pool_node(pool, l + 1)

        def dve_edge(dve, l):
            key = ("edge", l)
            nk, ns, width = OUT_V[l], OUT_S[l], WIDTH[l]
            if l == 1:
                for b in range(2):
                    nc.vector.memset(message[b][2][V:2 * V, :], 1.0)

            def prepare(g):
                b = g.odd
                v3 = gath[b][:, :, 0:3 * V].rearrange("p t (i c) -> p t i c", c=V)
                dve.wait_ge(gathered[b].sem, gathered[b].at(key, g.half + 1))
                dve.wait_ge(front_in[b].sem, front_in[b].at(key, g.half + 1))
                dve.wait_ge(turned.sem, turned.at(key, (g.n - 1) * 3))

                def e(lo, hi, shape):
                    return edge_vec(front_rec[b], TILES, lo, hi).unsqueeze(3).to_broadcast([P, TILES, hi - lo, shape])

                def four(a):
                    return a.rearrange("p t (i c) -> p t i c", c=V)

                def e0(width):
                    return edge_vec(front_rec[b], TILES, 0, 1).to_broadcast([P, TILES, width])

                nc.vector.tensor_tensor(gath[b][:, :, HROW:HROW + S], gath[b][:, :, 3 * V:HROW], e0(S), ALU.mult)
                if HAS_E0[l]:
                    nc.vector.tensor_tensor(v_e0[b], gath[b][:, :, 0:3 * V], e0(3 * V), ALU.mult)
                if CROSS[l]:
                    nc.vector.tensor_tensor(four(prod_a)[:, :, 0:2, :], v3[:, :, 1:3, :], e(3, 5, V), ALU.mult)
                    nc.vector.tensor_tensor(four(prod_a)[:, :, 2, :], v3[:, :, 0, :],
                                            edge_vec(front_rec[b], TILES, 2, 3).to_broadcast([P, TILES, V]), ALU.mult)
                    nc.vector.tensor_tensor(four(prod_b)[:, :, 0, :], v3[:, :, 2, :],
                                            edge_vec(front_rec[b], TILES, 2, 3).to_broadcast([P, TILES, V]), ALU.mult)
                    nc.vector.tensor_tensor(four(prod_b)[:, :, 1:3, :], v3[:, :, 0:2, :], e(3, 5, V), ALU.mult)
                nc.vector.tensor_tensor(four(prod_dot), v3, e(1, 4, V), ALU.mult).then_inc(multiplied.sem, 1)
                dve.wait_ge(multiplied.sem, multiplied.at(key, g.n + 1))
                if CROSS[l]:
                    nc.vector.tensor_tensor(dot_cross[b][:, :, V:4 * V], prod_a, prod_b, ALU.subtract)
                nc.vector.tensor_reduce(dot_cross[b][:, :, 0:V], prod_dot.rearrange("p t (i c) -> p t c i", c=V),
                                        AX_X, ALU.add).then_inc(prepared.sem, 1)

            def make_message(g, s):
                b = g.odd
                n = g.n * 3 + s
                rows = (2 * S, 3 * V, 4 * V if CROSS[l] else V)[s]
                r = (g.n + s) % 2 if isinstance(g.n, int) else (g.odd + s) % 2
                dve.wait_ge(turned.sem, turned.at(key, n + 1))
                dve.wait_ge(wide_copied.sem, wide_copied.at(key, g.n * 4 + s + 2))
                dve.wait_ge(msg_mm.sem, msg_mm.at(key, (g.n - 1) * TILES))
                nc.vector.tensor_tensor(message[b][s][0:rows, :], psum[0:rows, TURN[r], :], w_sb[r][0:rows, :],
                                        ALU.mult).then_inc(message_made.sem, 1)

            def compare(g):
                b = g.odd
                dve.wait_ge(back_in[b].sem, back_in[b].at(key, g.half + 1))
                dve.wait_ge(sum_mm.sem, sum_mm.at(key, (g.n - 1) * TILES))
                nc.vector.tensor_tensor(
                    same[b][:, 0:TILES], target_row[b].bitcast(I32).rearrange("p (t c) -> p t c", c=P),
                    back_rec[b][:, 0:TILES].bitcast(I32).unsqueeze(2).to_broadcast([P, TILES, P]), ALU.is_equal)
                nc.vector.tensor_tensor(
                    same[b][:, TILES:], target_row[b].bitcast(I32).rearrange("p (h u c) -> p h u c", u=2, c=P)[:, :, 0, :],
                    back_rec[b][:, 0:TILES].bitcast(I32).rearrange("p (h u) -> p h u", u=2)[:, :, 1].unsqueeze(2)
                    .to_broadcast([P, TILES // 2, P]), ALU.is_equal).then_inc(same_made.sem, 1)

            def add_outer(g):
                b = g.odd
                dve.wait_ge(msg_copied.sem, msg_copied.at(key, (g.n + 1) * TILES))
                outer4 = outer[:, :, 0:3 * nk].rearrange("p t (i c) -> p t i c", c=nk)
                nc.vector.tensor_tensor(
                    outer4, edge_out[b][:, :, width:width + nk].unsqueeze(2).to_broadcast([P, TILES, 3, nk]),
                    edge_vec(back_rec[b], 2 * TILES, 1, 4).unsqueeze(3).to_broadcast([P, TILES, 3, nk]),
                    ALU.mult).then_inc(outer_made.sem, 1)
                dve.wait_ge(outer_made.sem, outer_made.at(key, g.n + 1))
                nc.vector.tensor_tensor(edge_out[b][:, :, 0:3 * nk], edge_out[b][:, :, 0:3 * nk],
                                        outer[:, :, 0:3 * nk], ALU.add).then_inc(outer_added.sem, 1)

            def step(g, has_back, has_it, has_ahead):
                if has_back:
                    compare(g.back())
                if has_it:
                    make_message(g, 0)
                if has_back:
                    add_outer(g.back())
                if has_it:
                    make_message(g, 1)
                    make_message(g, 2)
                if has_ahead:
                    prepare(g.ahead())

            prepare(Group(0, 0))
            over_groups(dve, step)
            barrier(dve, 3 + 2 * l)

        def dve_node(dve, k):
            key = ("node", k)
            f = k - 1

            def combine(g):
                b = g.odd
                dve.wait_ge(node_in[b].sem, node_in[b].at(key, g.half + 1))
                dve.wait_ge(normed.sem, normed.at(key, g.n - 1))
                t_in = tot_in[b]
                a = attr_in[b][:, 0:TILES]
                y5 = y[b].rearrange("p t (i c) -> p t i c", c=V)
                done = [0]

                def link(ins):
                    ins.then_inc(combine_step.sem, 1)
                    done[0] += 1
                    first, step = combine_step.first[key]
                    dve.wait_ge(combine_step.sem, g.n * step + (first + done[0]))

                def wide(x, width):
                    return x.unsqueeze(2).to_broadcast([P, TILES, width])

                if f in (0, 3):
                    dve.wait_ge(gated.sem, gated.at(key, g.n + 1))
                    gate = gates[b]
                    if f == 3:
                        link(nc.vector.tensor_tensor(gate, gate, wide(a, S + V), ALU.mult))
                    nc.vector.tensor_tensor(y[b][:, :, 3 * V:HROW], t_in[:, :, 3 * V:HROW], gate[:, :, 0:S], ALU.mult)
                    link(nc.vector.tensor_tensor(
                        y5[:, :, 0:3, :], t_in[:, :, 0:3 * V].rearrange("p t (i c) -> p t i c", c=V),
                        gate[:, :, S:S + V].unsqueeze(2).to_broadcast([P, TILES, 3, V]), ALU.mult))
                elif f == 1:
                    q = [factor[:, TILES * i:TILES * i + TILES] for i in range(6)]
                    count, alpha = t_in[:, :, HROW + 1:HROW + 2], t_in[:, :, HROW:HROW + 1]
                    link(nc.vector.tensor_scalar(q[0].unsqueeze(2), count, 1.0, None, ALU.max))
                    link(nc.vector.reciprocal(q[1], q[0]))
                    link(nc.vector.tensor_tensor(q[2], q[1], a, ALU.mult))
                    link(nc.vector.tensor_tensor(q[3], q[2], q[2], ALU.mult))
                    link(nc.vector.tensor_tensor(q[4].unsqueeze(2), q[3].unsqueeze(2), alpha, ALU.mult))
                    link(nc.vector.tensor_tensor(y[b], t_in[:, :, 0:HROW], wide(q[4], HROW), ALU.mult))
                else:
                    t5 = t_in[:, :, 0:WIDTH[2]].rearrange("p t (i u c) -> p t i u c", u=2, c=V)
                    fa, fc = factor[:, 0:TILES], factor[:, TILES:2 * TILES]
                    nc.vector.tensor_tensor(fa, a, attr_in[b][:, 2 * TILES:3 * TILES], ALU.mult)
                    link(nc.vector.tensor_tensor(fc, attr_in[b][:, TILES:2 * TILES], attr_in[b][:, 2 * TILES:3 * TILES],
                                                 ALU.mult))
                    base5 = base_in[b].rearrange("p t (i c) -> p t i c", c=V)
                    for t in range(TILES):
                        last = nc.vector.scalar_tensor_tensor(y5[:, t], t5[:, t, :, 1, :], fc[:, t:t + 1], base5[:, t],
                                                              ALU.mult, ALU.add)
                    link(last)
                    for t in range(TILES):
                        last = nc.vector.scalar_tensor_tensor(y5[:, t], t5[:, t, :, 0, :], fa[:, t:t + 1], y5[:, t],
                                                              ALU.mult, ALU.add)
                    last.then_inc(combined.sem, 1)
                if f != 2:
                    nc.vector.tensor_tensor(y[b], y[b], base_in[b], ALU.add).then_inc(combined.sem, 1)
                assert done[0] == combine_step.first[key][1]
                dve.wait_ge(combined.sem, combined.at(key, g.n + 1))
                for t in range(TILES):
                    last = nc.vector.bn_stats(stats[:, t, :], y[b][:, t, :])
                last.then_inc(stats_made.sem, 1)
                dve.wait_ge(stats_made.sem, stats_made.at(key, g.n + 1))
                settle(dve)
                for t in range(TILES):
                    last = nc.vector.bn_aggr(moments[b][:, t, :], stats[:, t, :])
                last.then_inc(moments_made.sem, 1)
                dve.wait_ge(moments_made.sem, moments_made.at(key, g.n + 1))
                nc.vector.tensor_scalar(var_eps[b].unsqueeze(2), moments[b][:, :, 1:2], NORM_EPS, None, ALU.add)\
                  .then_inc(var_made.sem, 1)

            def normalise(g):
                b = g.odd
                dve.wait_ge(rstd_made.sem, rstd_made.at(key, g.n + 1))
                if k >= 3:
                    dve.wait_ge(x_stored[b].sem, x_stored[b].at(key, g.half))
                if k == 3:
                    dve.wait_ge(x_turned.sem, x_turned.at(key, g.n - 1))
                if k in (1, 2):
                    dve.wait_ge(scaled.sem, scaled.at(key, g.n - 1))
                    dve.wait_ge(lin_dve.sem, lin_dve.at(key, g.n - 1))
                for t in range(TILES):
                    last = nc.vector.tensor_scalar(x_new[b][:, t, :], y[b][:, t, :], moments[b][:, t, 0:1],
                                                   rstd[b][:, t:t + 1], ALU.subtract, ALU.mult)
                last.then_inc(normed.sem, 1)

            def linear_out(g):
                b = g.odd
                dve.wait_ge(stored[b].sem, stored[b].at(key, g.half))
                for pair in ((1,), (0, 1), (0, 1))[k]:
                    dve.wait_ge(lin_mm.sem, lin_mm.at_pair(key, g.n, pair))
                    if k == 0:
                        nc.vector.tensor_copy(pair_of(h_out[b], pair, 0, HROW), lin_h(pair))
                        nc.vector.tensor_copy(
                            pair_of(tot_out[b], pair, 0, 6 * V).rearrange("p t (u c) -> p t u c", u=2),
                            lin_skip_96(pair)).then_inc(lin_dve.sem, 1)
                    else:
                        nc.vector.tensor_tensor(pair_of(base_out[b], pair, 0, 3 * V), lin_banks(pair)[:, :, 0:3 * V],
                                                pair_of(x_new[b], pair, 0, 3 * V), ALU.add)
                        nc.vector.tensor_tensor(pair_of(base_out[b], pair, 3 * V, HROW),
                                                lin_banks(pair)[:, :, 3 * V + HROW:3 * V + HROW + S],
                                                pair_of(x_new[b], pair, 3 * V, HROW), ALU.add).then_inc(lin_dve.sem, 1)

            def step(g, has_back, has_it, has_ahead):
                if has_ahead and k:
                    combine(g.ahead())
                if has_it and k == LAYERS:
                    normalise(g)
                if has_back and k < 3:
                    linear_out(g.back())
                if has_ahead and k in (1, 2, 3):
                    normalise(g.ahead())

            if k:
                combine(Group(0, 0))
            if k in (1, 2, 3):
                normalise(Group(0, 0))
            over_groups(dve, step)
            barrier(dve, 2 + 2 * k)

        @block.vector
        def _(dve):
            nc.vector.memset(zeros[:, :], 0.0)
            nc.vector.memset(power[:, :], -0.5).then_inc(s_fill, 1)
            dve.wait_ge(s_const, 32)
            for name, r0, r1, by in scales:
                nc.vector.tensor_scalar(w(name, r0, r1), w(name, r0, r1), by, None, ALU.mult)
            for name, rows, cols, by in skip_scales:
                at = S if rows == S else 0
                skip_cols = w(name, 0, rows, at, at + cols)
                last = nc.vector.tensor_scalar(skip_cols, skip_cols, by, None, ALU.mult)
            last.then_inc(s_scaled, 1)
            dve.wait_ge(s_edges_in, 64)
            nc.vector.tensor_tensor(square, vec3, vec3, ALU.mult).then_inc(s_sq, 1)
            dve.wait_ge(s_sq, 1)
            nc.vector.tensor_reduce(sum_sq, square, AX_X, ALU.add).then_inc(s_sq, 1)
            for which, idx in ((0, src_idx), (1, dst_idx)):
                nc.vector.tensor_copy(own_f[which], idx.bitcast(I32)).then_inc(s_own, 1)
            dve.wait_ge(s_own, 2)
            for which in range(2):
                def search(n, b, u):
                    dve.wait_ge(s_row_prep[b], u * 16 + 16 * (H * which + 1))
                    dve.wait_ge(s_seen_step, n + G * which)
                    for t in range(TILES):
                        first = t // 2 * 2 if t % 2 else t
                        width = (t + 1 - first) * P
                        last = nc.vector.scalar_tensor_tensor(
                            matches[t][:, 0:width], row_prep[b].bitcast(I32)[:, first * P:(t + 1) * P],
                            own_f[which][:, bass.ds(n * TILES + t, 1)], earlier[:, 2 * P - width:],
                            ALU.is_equal, ALU.mult, accum_out=seen[which][:, bass.ds(n * TILES + t, 1)])
                    last.then_inc(s_seen_step, 1)
                for b in range(2):
                    search(b, b, 0)
                with dve.Fori(1, H) as half:
                    for b in range(2):
                        search(half * 2 + b, b, half)
            dve.wait_ge(s_seen_step, G * 2)
            for which in range(2):
                nc.vector.tensor_scalar(seen[which], seen[which], 1.0, None, ALU.min)
            step = [0]

            def link(ins):
                ins.then_inc(s_vec, 1)
                step[0] += 1
                dve.wait_ge(s_vec, step[0])

            dve.wait_ge(s_len, 1)
            link(nc.vector.tensor_tensor(square, vec3, inv_len.unsqueeze(2).to_broadcast([P, G * TILES, 3]), ALU.mult))
            for k in range(2):
                for rec, at in ((front_all[k], TILES), (back_all[k], 2 * TILES)):
                    e = rec[:, :, at:at + TILES * EXT].rearrange("p g (t c) -> p g t c", c=EXT)
                    if k == 0:
                        vec, lo = square.rearrange("p (g t) c -> p g t c", t=TILES), 0
                        for t in range(TILES):
                            nc.vector.memset(e[:, :, t, 0:1], 1.0)
                    else:
                        vec, lo = vec4.rearrange("p (g t) c -> p g t c", t=TILES), 1
                    for t in range(TILES):
                        if k:
                            nc.vector.tensor_copy(e[:, :, t, 0:1], vec[:, :, t, 0:1])
                        nc.vector.tensor_copy(e[:, :, t, 1:4], vec[:, :, t, lo:lo + 3])
                        nc.vector.tensor_copy(e[:, :, t, 4:6], vec[:, :, t, lo:lo + 2])
                source, target = ((dst_idx, src_idx), (src_idx, dst_idx))[k]

                def lanes(a):
                    return a.bitcast(I32).rearrange("p (g t) -> p g t", t=TILES)

                nc.vector.tensor_copy(front_all[k][:, :, 0:TILES].bitcast(I32), lanes(source))
                nc.vector.tensor_copy(back_all[k][:, :, 0:TILES].bitcast(I32), lanes(target))
                for odd in range(2):
                    last = nc.vector.tensor_scalar(
                        moved.rearrange("p (n u) -> p n u", u=2)[:, :, odd],
                        target.bitcast(I32).rearrange("p (n u) -> p n u", u=2)[:, :, odd],
                        -1.0, spare[:, odd:odd + 1], ALU.mult, ALU.add)
                link(last)
                link(nc.vector.tensor_tensor(moved, moved, seen[k], ALU.mult))
                link(nc.vector.tensor_tensor(back_all[k][:, :, TILES:2 * TILES].bitcast(I32),
                                             moved.rearrange("p (g t) -> p g t", t=TILES), lanes(target), ALU.add))
            dve.drain().then_inc(s_rec, 1)
            barrier(dve, 1)
            dve_node(dve, 0)
            for l in range(LAYERS):
                dve_edge(dve, l)
                dve_node(dve, l + 1)

        def act_edge(act, l):
            key = ("edge", l)
            nk, width = OUT_V[l], WIDTH[l]

            def hide(g):
                b = g.odd
                act.wait_ge(wide_mm.sem, wide_mm.at(key, g.n * 4 + 1))
                act.wait_ge(wide_mm.sem, wide_mm.at(key, (g.n - 1) * 4))
                nc.scalar.activation(hidden[b][0:FC_HID[l], :], psum[0:FC_HID[l], WIDE[0], :],
                                     ACT.Relu if l == 0 else ACT.Silu).then_inc(wide_copied.sem, 1)

            def weight(g, s):
                rows = (2 * S, 3 * V, 4 * V if CROSS[l] else V)[s]
                r = (g.odd + s) % 2
                act.wait_ge(wide_mm.sem, wide_mm.at(key, g.n * 4 + s + 2))
                act.wait_ge(message_made.sem, message_made.at(key, g.n * 3 + s - 1))
                nc.scalar.copy(w_sb[r][0:rows, :], psum[0:rows, WIDE[(s + 1) % 2], :]).then_inc(wide_copied.sem, 1)

            def copy_message(g):
                b = g.odd
                for t in range(TILES):
                    n = g.n * TILES + t
                    act.wait_ge(msg_mm.sem, msg_mm.at(key, n + 1))
                    if t == 0:
                        act.wait_ge(sum_mm.sem, sum_mm.at(key, (g.n - 1) * TILES))
                    nc.scalar.copy(edge_out[b][:, t, 0:width + nk], psum[:, MSG[t % 2], 0:width + nk])\
                      .then_inc(msg_copied.sem, 1)

            def copy_sum(g):
                b = g.odd
                for t in range(TILES):
                    n = g.n * TILES + t
                    act.wait_ge(sum_mm.sem, sum_mm.at(key, n + 1))
                    if t == 0:
                        act.wait_ge(landed.sem, landed.at(key, g.n))
                    nc.scalar.copy(summed[b][:, t, 0:width], psum[:, SUM[t % 2], 0:width]).then_inc(sum_copied.sem, 1)

            def step(g, has_back, has_it, has_ahead):
                if has_back:
                    copy_message(g.back())
                if has_it:
                    for s in range(3):
                        weight(g, s)
                if has_ahead:
                    hide(g.ahead())
                if has_back:
                    copy_sum(g.back())

            hide(Group(0, 0))
            over_groups(act, step)
            barrier(act, 3 + 2 * l)

        def act_node(act, k):
            key = ("node", k)

            def gate(g):
                b = g.odd
                act.wait_ge(node_in[b].sem, node_in[b].at(key, g.half + 1))
                act.wait_ge(combined.sem, combined.at(key, g.n - 1))
                if k == 1:
                    nc.scalar.activation(gates[b], tot_in[b][:, :, 3 * V:WIDTH[0]], ACT.Sigmoid).then_inc(gated.sem, 1)
                else:
                    for t in range(TILES):
                        last = nc.scalar.activation(gates[b][:, t, :], tot_in[b][:, t, 3 * V:WIDTH[3]], ACT.Sigmoid,
                                                    scale=attr_in[b][:, t:t + 1])
                    last.then_inc(gated.sem, 1)

            def scale_x(g):
                b = g.odd
                act.wait_ge(node_in[b].sem, node_in[b].at(key, g.half + 1))
                if k == 3:
                    act.wait_ge(lin_act.sem, lin_act.at(key, g.n - 1))
                    nc.scalar.copy(attr[b], attr_in[b]).then_inc(scaled.sem, 1)
                    return
                act.wait_ge(normed.sem, normed.at(key, g.n + 1))
                act.wait_ge(x_turned.sem, x_turned.at(key, g.n - 1))
                for path in range(paths(k)):
                    for t in range(TILES):
                        col = path * TILES + t
                        last = nc.scalar.activation(x_scaled[path][b][:, t, :], x_new[b][:, t, :], ACT.Copy,
                                                    scale=attr_in[b][:, col:col + 1])
                last.then_inc(scaled.sem, 1)

            def copy_x(g):
                b = g.odd
                act.wait_ge(x_turned.sem, x_turned.at(key, g.n + 1))
                act.wait_ge(lin_mm.sem, lin_mm.at(key, g.n - 1))
                for path in range(paths(k)):
                    nc.scalar.copy(v_cols[path][b][0:3 * V, :], psum[0:3 * V, 2 * path, :])
                    last = nc.scalar.copy(s_cols[path][b][0:S, :], psum[0:S, 2 * path + 1, :])
                last.then_inc(x_copied.sem, 1)

            def linear_out(g):
                b = g.odd
                act.wait_ge(stored[b].sem, stored[b].at(key, g.half))
                if k == 3:
                    act.wait_ge(scaled.sem, scaled.at(key, g.n + 1))
                for pair in range(ACT_PAIRS[k]):
                    if k in (1, 2):
                        act.wait_ge(lin_dve.sem, lin_dve.at_pair(key, g.n, pair))
                    else:
                        act.wait_ge(lin_mm.sem, lin_mm.at_pair(key, g.n, pair))
                    if k == 3:
                        for t in (2 * pair, 2 * pair + 1):
                            nc.scalar.activation(h_out[b][:, t, :], lin_h(pair)[:, t % 2, :], ACT.Copy,
                                                 scale=attr[b][:, t:t + 1])
                    else:
                        last = nc.scalar.copy(pair_of(h_out[b], pair, 0, HROW), lin_h(pair))
                    if k in (0, 3):
                        last = nc.scalar.copy(pair_of(tot_out[b], pair, 0, 6 * V).rearrange("p t (u c) -> p t u c", u=2),
                                              lin_skip_96(pair))
                    last.then_inc(lin_act.sem, 1)

            def step(g, has_back, has_it, has_ahead):
                if has_it and k < LAYERS:
                    copy_x(g)
                if has_back and k < LAYERS:
                    linear_out(g.back())
                if has_ahead and k in (1, 4) and not is_last_ahead(g):
                    gate(g.ahead().ahead())
                if has_ahead and k in (1, 2, 3):
                    scale_x(g.ahead())

            if k in (1, 4):
                gate(Group(0, 0))
                gate(Group(0, 1))
            if k in (1, 2, 3):
                scale_x(Group(0, 0))
            over_groups(act, step)
            barrier(act, 2 + 2 * k)

        @block.scalar
        def _(act):
            for i, (left, right, cols) in enumerate(comp_parts):
                act.wait_ge(s_comp_mm, i + 1)
                acc = psum[:, i, :]
                nc.scalar.mul(comp[0:S, comp_at[i]:comp_at[i] + cols], acc[0:S, 0:cols], C_X / 4)
                nc.scalar.mul(comp[S:S + V, comp_at[i]:comp_at[i] + cols], acc[S:S + V, 0:cols],
                              C_X / 4 * (r3 if cols == S else 1.0)).then_inc(s_comp, 1)
            barrier(act, 1)
            act_node(act, 0)
            for l in range(LAYERS):
                act_edge(act, l)
                act_node(act, l + 1)

        def pe_edge(pe, l):
            key = ("edge", l)
            nk, ns, width = OUT_V[l], OUT_S[l], WIDTH[l]
            x_rows = REGIONS[f"rx_{l}"][1]

            def hide(g):
                b = g.odd
                pe.wait_ge(front_in[b].sem, front_in[b].at(key, g.half + 1))
                pe.wait_ge(wide_copied.sem, wide_copied.at(key, g.n * 4 - 1))
                settle(pe)
                nc.tensor.matmul(psum[0:FC_HID[l], WIDE[0], :], w(f"fc1_{l}"), edge_feat[b][0:FC_IN[l], :],
                                 start=True, stop=True).then_inc(wide_mm.sem, 1)

            def weigh_and_turn(g, s):
                b = g.odd
                n = g.n * 3 + s
                r = (g.odd + s) % 2
                name, rows = ((f"w12_{l}", 2 * S), (f"wv_{l}", 3 * V), (f"wx_{l}", 4 * V if CROSS[l] else V))[s]
                pe.wait_ge(wide_copied.sem, wide_copied.at(key, g.n * 4 + 1 if s == 0 else g.n * 4 + s))
                settle(pe)
                nc.tensor.matmul(psum[0:rows, WIDE[(s + 1) % 2], :], w(name), hidden[b][0:FC_HID[l], :],
                                 start=True, stop=True).then_inc(wide_mm.sem, 1)
                pe.wait_ge(prepared.sem, prepared.at(key, g.n + 1))
                pe.wait_ge(message_made.sem, message_made.at(key, n - 1))
                for t in range(TILES):
                    src = (gath[b][:, t, 3 * V:3 * V + 2 * S],
                           (v_e0[b] if HAS_E0[l] else gath[b])[:, t, 0:3 * V],
                           dot_cross[b][:, t, 0:rows])[s]
                    last = nc.tensor.transpose(psum[0:rows, TURN[r], t * P:(t + 1) * P], src, ident)
                last.then_inc(turned.sem, 1)

            def output(g):
                b = g.odd
                for t in range(TILES):
                    n = g.n * TILES + t
                    if t == 0:
                        pe.wait_ge(message_made.sem, message_made.at(key, (g.n + 1) * 3))
                    pe.wait_ge(msg_copied.sem, msg_copied.at(key, n - 1))
                    acc = psum[:, MSG[t % 2], :]
                    cols = slice(t * P, (t + 1) * P)
                    m12, m3, mx = message[b]
                    nc.tensor.matmul(acc[:, 0:3 * nk], m3[0:3 * V, cols], w(f"r3_{l}"), start=True, stop=False,
                                     skip_group_check=True)
                    nc.tensor.matmul(acc[:, 3 * nk:width + nk], m12[:, cols], w(f"r12_{l}"), start=False, stop=False,
                                     skip_group_check=True)
                    to = acc[:, 0:width] if CROSS[l] else acc[:, 3 * nk:width]
                    nc.tensor.matmul(to, mx[0:x_rows, cols], w(f"rx_{l}"), start=False, stop=True,
                                     skip_group_check=True).then_inc(msg_mm.sem, 1)

            def sum_same(g):
                b = g.odd
                for t in range(TILES):
                    n = g.n * TILES + t
                    if t == 0:
                        pe.wait_ge(outer_added.sem, outer_added.at(key, g.n + 1))
                        pe.wait_ge(same_made.sem, same_made.at(key, g.n + 1))
                    pe.wait_ge(sum_copied.sem, sum_copied.at(key, n - 1))
                    to = psum[:, SUM[t % 2], 0:width]
                    last = nc.tensor.matmul(to, same[b][:, t, :], edge_out[b][:, t, 0:width], start=True, stop=t % 2 == 1)
                    if t % 2 == 0:
                        last = nc.tensor.matmul(to, same[b][:, TILES + t // 2, :], edge_out[b][:, t + 1, 0:width],
                                                start=False, stop=True)
                    last.then_inc(sum_mm.sem, 1)

            def step(g, has_back, has_it, has_ahead):
                if has_back:
                    output(g.back())
                if has_it:
                    for s in range(3):
                        weigh_and_turn(g, s)
                if has_ahead:
                    hide(g.ahead())
                if has_back:
                    sum_same(g.back())

            hide(Group(0, 0))
            over_groups(pe, step)
            barrier(pe, 3 + 2 * l)

        def pe_node(pe, k):
            key = ("node", k)

            def turn(g):
                b = g.odd
                if k == 0:
                    pe.wait_ge(node_in[b].sem, node_in[b].at(key, g.half + 1))
                elif k == 3:
                    pe.wait_ge(normed.sem, normed.at(key, g.n + 1))
                else:
                    pe.wait_ge(scaled.sem, scaled.at(key, g.n + 1))
                pe.wait_ge(x_copied.sem, x_copied.at(key, g.n))
                for path in range(paths(k)):
                    x = x_scaled[path][b] if k in (1, 2) else x_new[b]
                    for t in range(TILES):
                        cols = slice(t * P, (t + 1) * P)
                        nc.tensor.transpose(psum[0:3 * V, 2 * path, cols], x[:, t, 0:3 * V], ident)
                        last = nc.tensor.transpose(psum[0:S, 2 * path + 1, cols], x[:, t, 3 * V:HROW], ident)
                last.then_inc(x_turned.sem, 1)

            def linear(g, pair):
                b = g.odd
                if pair == 0:
                    pe.wait_ge(x_copied.sem, x_copied.at(key, g.n + 1))
                if ACT_PAIRS[k] == 2:
                    pe.wait_ge(lin_act.sem, lin_act.at_pair(key, g.n - 1, pair))
                elif pair == 0:
                    pe.wait_ge(lin_act.sem, lin_act.at(key, g.n))
                else:
                    pe.wait_ge(lin_dve.sem, lin_dve.at(key, g.n))
                for t in (2 * pair, 2 * pair + 1):
                    cols = slice(t * P, (t + 1) * P)
                    to = psum[:, 4 + t, :]
                    for at, src, rows, kind, width in ((0, v_cols, 3 * V, "nv", 6 * V), (6 * V, s_cols, S, "ns", S + SKIP_S[k])):
                        for path in range(paths(k)):
                            last = nc.tensor.matmul(to[:, at:at + width], src[path][b][0:rows, cols],
                                                    w(f"{kind}{'ac'[path]}_{k}"), start=path == 0,
                                                    stop=path == paths(k) - 1, skip_group_check=True)
                last.then_inc(lin_mm.sem, 1)

            def step(g, has_back, has_it, has_ahead):
                if has_back and k < LAYERS:
                    linear(g.back(), 0)
                if has_it and k < LAYERS:
                    turn(g)
                if has_back and k < LAYERS:
                    linear(g.back(), 1)

            over_groups(pe, step)
            barrier(pe, 2 + 2 * k)

        @block.tensor
        def _(pe):
            pe.wait_ge(s_const, 32)
            for i, (left, right, cols) in enumerate(comp_parts):
                nc.tensor.matmul(psum[0:S + V, i, 0:cols], w(left), w(right), start=True, stop=True)\
                  .then_inc(s_comp_mm, 1)
            barrier(pe, 1)
            pe_node(pe, 0)
            for l in range(LAYERS):
                pe_edge(pe, l)
                pe_node(pe, l + 1)


def pack_weights(i):
    def l_(layer, name):
        return np.asarray(i[f"L{layer}_gnn_{name}"])

    def diag(m):
        out = np.zeros((3 * m.shape[0], 3 * m.shape[1]), np.float32)
        for c in range(3):
            out[c * m.shape[0]:(c + 1) * m.shape[0], c * m.shape[1]:(c + 1) * m.shape[1]] = m
        return out

    fc1 = [l_(0, "W_fc1"), l_(1, "Wfc1"), l_(2, "W_fc1"), l_(3, "fc_w1")]
    fc2 = [l_(0, "W_fc2"), l_(1, "Wfc2"), l_(2, "W_fc2"), l_(3, "fc_w2")]
    out_s = [l_(0, "W_out_s"), np.concatenate([l_(1, "Wl2_s"), l_(1, "Wa"), np.zeros((S + V, 1), np.float32)], 1),
             None, l_(3, "lin2_ws")]
    out_v = [l_(0, "W_out_v"), l_(1, "Wl2_v"), None, l_(3, "lin2_wv")]
    skip = {"a_0": ("W_skip0", "W_skip1", "W_nl0", "W_nl1"), "a_1": ("Wsc0", "Wsc1", "Wl1_0", "Wl1_1"),
            "a_2": ("Ws_sc_a", "Wv_sc_a", "Ws_l1_a", "Wv_l1_a"), "c_2": ("Ws_sc_c", "Wv_sc_c", "Ws_l1_c", "Wv_l1_c"),
            "a_3": ("sc_ws", "sc_wv", "lin1_ws", "lin1_wv")}
    m = {}
    for l in range(LAYERS):
        f = fc2[l]
        m[f"fc1_{l}"] = fc1[l]
        m[f"w12_{l}"] = np.concatenate([f[:, S:2 * S], f[:, 0:S]], 1)
        m[f"wv_{l}"] = np.concatenate([f[:, 2 * S:2 * S + V]] * 3, 1)
        dot, cross = f[:, 2 * S + V:2 * S + 2 * V], f[:, 2 * S + 2 * V:]
        m[f"wx_{l}"] = np.concatenate([dot] + [cross] * 3, 1) if CROSS[l] else dot
        if l != 2:
            ns, nk = OUT_S[l], OUT_V[l]
            r12 = np.zeros((2 * S, ns + nk), np.float32)
            r12[S:, 0:ns] = out_s[l][0:S]
            r12[0:S, ns:] = out_v[l][0:S]
            m[f"r12_{l}"] = r12
            m[f"r3_{l}"] = diag(out_v[l][S:S + V])
            if CROSS[l]:
                rx = np.zeros((4 * V, 3 * nk + ns), np.float32)
                rx[0:V, 3 * nk:] = out_s[l][S:]
                rx[V:, 0:3 * nk] = diag(out_v[l][S + V:])
            else:
                rx = np.zeros((V + 1, ns), np.float32)
                rx[0:V] = out_s[l][S:]
                rx[V, ns - 1] = 1.0
            m[f"rx_{l}"] = rx
    for key, (ss, sv, hs, hv) in skip.items():
        layer = int(key[-1])
        m[f"nv{key}"] = np.concatenate([diag(l_(layer, sv)), diag(l_(layer, hv))], 1)
        m[f"ns{key}"] = np.concatenate([l_(layer, hs), l_(layer, ss)], 1)
    m["lsa"], m["lsc"] = l_(2, "Ws_l2_a").T, l_(2, "Ws_l2_c").T
    m["lva"], m["lvc"] = l_(2, "Wv_l2_a").T, l_(2, "Wv_l2_c").T
    m["l3s"], m["l3v"] = l_(2, "Ws_l3"), l_(2, "Wv_l3")
    packed = np.zeros((P, WCOLS), np.float32)
    for name, a in m.items():
        at, rows, cols = REGIONS[name]
        assert a.shape == (rows, cols), (name, a.shape, rows, cols)
        packed[0:rows, at:at + cols] = a
    return packed


def lay_out(i):
    def padded(a, fill):
        a = np.asarray(a)
        return np.concatenate([a, np.full((NPAD - N,) + a.shape[1:], fill, a.dtype)])

    def edge_lanes(a):
        a = a.reshape(GROUPS, TILES, P, -1)
        return np.ascontiguousarray(a.transpose(2, 0, 1, 3).reshape(P, -1))

    x = np.asarray(i["x"])
    vec = x[:, S:].reshape(N, V, 3).transpose(0, 2, 1).reshape(N, 3 * V)
    out = {"x": padded(np.concatenate([vec, x[:, 0:S]], 1), 0.0)}
    for name in ("src", "dst"):
        idx = padded(i[name], N)
        out[f"{name}_lanes"] = edge_lanes(idx)
        out[f"{name}_rows"] = idx.reshape(GROUPS, GROUP)
    out["vec3"] = edge_lanes(padded(i["edge_attr_3"], 1.0))
    out["vec4"] = edge_lanes(padded(i["edge_attr_4"], 0.0))
    for l, name in enumerate(("edge_attr_64", "edge_attr_16", "edge_attr_10", "edge_attr_64")):
        out[f"feat{l}"] = np.ascontiguousarray(padded(i[name], 0.0).T)
    attrs = np.stack([padded(i[n], 0.0)[:, 0] for n in ("node_vec1", "node_vec1_n2", "node_vec1_n3")])
    out["attrs"] = np.ascontiguousarray(attrs.reshape(3, GROUPS, P, TILES).transpose(2, 1, 0, 3).reshape(P, -1))
    out["weights"] = pack_weights(i)
    const = np.zeros((P, 3 * P + 2), np.float32)
    const[:, 0:P] = np.eye(P)
    const[:, P:2 * P] = 1.0
    const[:, 2 * P:3 * P] = np.tril(np.ones((P, P)), -1)
    const[:, 3 * P] = NPAD + np.arange(P)
    const[:, 3 * P + 1] = NPAD + P + np.arange(P)
    out["consts"] = const
    return out


def kernel(**inputs):
    import concourse.bacc as bacc
    from concourse.bass_utils import run_bass_kernel_spmd

    nc = bacc.Bacc("TRN2", target_bir_lowering=False, num_devices=1)
    arrays = {f"in_{k}": v for k, v in lay_out(inputs).items()}
    d = {k[3:]: nc.dram_tensor(k, v.shape, mybir.dt.from_np(v.dtype), kind="ExternalInput").ap()
         for k, v in arrays.items()}
    d["out"] = nc.dram_tensor("out", [NPAD, HROW], F32, kind="ExternalOutput").ap()
    build(nc, d)
    r = run_bass_kernel_spmd(nc, [arrays], core_ids=[0])
    got = r.results[0]["out"][0:N]
    vec = got[:, 0:3 * V].reshape(N, 3, V).transpose(0, 2, 1).reshape(N, 3 * V)
    return np.concatenate([got[:, 3 * V:], vec], 1)
```

```python
from contextlib import ExitStack

import numpy as np
import concourse.bass as bass
from concourse import mybir

F32 = mybir.dt.float32
I32 = mybir.dt.int32
ALU = mybir.AluOpType
ACT = mybir.ActivationFunctionType
AX_X = mybir.AxisListType.X

P = 128
TILES = 4
GROUP = P * TILES
N = 50000
GROUPS = -(-N // GROUP)
NPAD = GROUPS * GROUP
ROWS = NPAD + 2 * P
S, V = 64, 32
HROW = 3 * V + S
LAYERS = 4
NORM_EPS = 1e-5

FC_IN = [64, 16, 10, 64]
FC_HID = [64, 64, 100, 64]
OUT_S = [96, 66, 128, 96]
OUT_V = [32, 32, 64, 32]
CROSS = [True, False, False, True]
HAS_E0 = [False, True, True, True]
WIDTH = [3 * OUT_V[l] + OUT_S[l] for l in range(LAYERS)]
BLOCKS = [[128, 128, 96], [128, 128], [128, 128], [128, 128, 96]]
V_AT = [OUT_V[l] if CROSS[l] else 0 for l in range(LAYERS)]
K_AT = [0 if CROSS[l] else WIDTH[l] for l in range(LAYERS)]
TURNS = [len(b) + 1 for b in BLOCKS]
SKIP_S = [96, 64, 64, 96]
ACT_PAIRS = [1, 2, 2, 2]
DVE_PAIRS = [1, 2, 2, 0]
PATHS = [1, 1, 2, 1]

ROW_GROUPS = 7
EXT = 6
REC_F = TILES + TILES * EXT
REC_B = 2 * TILES + TILES * EXT


def weight_regions():
    out, at = {}, 0

    def add(name, rows, cols):
        nonlocal at
        out[name] = (at, rows, cols)
        at += cols

    for l in range(LAYERS):
        add(f"fc1_{l}", FC_IN[l], FC_HID[l])
        add(f"w_{l}", FC_HID[l], 2 * S + (3 if CROSS[l] else 2) * V)
        if CROSS[l]:
            add(f"out0_{l}", P, 3 * OUT_V[l])
            add(f"out1_{l}", P, OUT_V[l] + OUT_S[l])
            add(f"out2_{l}", 3 * V, 3 * OUT_V[l])
        else:
            add(f"out0_{l}", P, OUT_S[l] + OUT_V[l])
            add(f"out1_{l}", P, 3 * OUT_V[l] + OUT_S[l])
        for part in ("a", "c") if l == 2 else ("a",):
            add(f"nv{part}_{l}", 3 * V, 6 * V)
            add(f"ns{part}_{l}", S, SKIP_S[l] + S)
    for name in ("lsa", "lsc", "lva", "lvc"):
        add(name, S + V, S + V)
    add("l3s", S + V, S)
    add("l3v", S + V, V)
    return out, at


REGIONS, WCOLS = weight_regions()


class Tally:

    def __init__(self, sem, credit):
        self.sem, self.total, self.first = sem, credit, {}

    def phase(self, key, step, times):
        self.first[key] = (self.total, step)
        self.total += step * times

    def at(self, key, n):
        first, step = self.first[key]
        return max(n, 0) * step + first if isinstance(n, int) else n * step + first

    def at_pair(self, key, n, pair):
        return self.first[key][0] if isinstance(n, int) and n < 0 else self.at(key, n) + (pair + 1)


class Group:

    def __init__(self, half, odd):
        self.half, self.odd = half, odd
        self.n = half * 2 + odd

    def back(self):
        return Group(self.half, 0) if self.odd else Group(self.half - 1, 1)

    def ahead(self):
        return Group(self.half + 1, 0) if self.odd else Group(self.half, 1)


def over_groups(eng, step, peeled=1, start=1):
    step(Group(0, 0), False, True, True)
    step(Group(0, 1), True, True, True)
    for half in range(1, start):
        step(Group(half, 0), True, True, True)
        step(Group(half, 1), True, True, True)
    with eng.Fori(start, GROUPS // 2 - peeled) as half:
        step(Group(half, 0), True, True, True)
        step(Group(half, 1), True, True, True)
    for half in range(GROUPS // 2 - peeled, GROUPS // 2 - 1):
        step(Group(half, 0), True, True, True)
        step(Group(half, 1), True, True, True)
    step(Group(GROUPS // 2 - 1, 0), True, True, True)
    step(Group(GROUPS // 2 - 1, 1), True, True, False)
    step(Group(GROUPS // 2, 0), True, False, False)


def build(nc, d):
    assert GROUPS % 2 == 0
    ctx = ExitStack()
    with ctx:
        def sb(name, shape, dt=F32):
            return ctx.enter_context(nc.sbuf_tensor(name, shape, dt))

        def sem(name):
            return ctx.enter_context(nc.semaphore(name))

        def dram(name, shape):
            return nc.dram_tensor(name, shape, F32).ap()

        h_table = [dram(f"h_table{l}", [NPAD, HROW]) for l in range(LAYERS)]
        totals = [dram(f"totals{l}", [ROWS, WIDTH[l]]) for l in range(LAYERS)]
        base = [d["x"]] + [dram(f"base{l}", [NPAD, HROW]) for l in range(1, LAYERS)]
        rec_f = [dram(f"rec_f{k}", [P, GROUPS * REC_F]) for k in range(2)]
        rec_b = [dram(f"rec_b{k}", [P, GROUPS * REC_B]) for k in range(2)]

        weights = sb("weights", [P, WCOLS])
        consts = sb("consts", [P, 3 * P + 2])
        ident = consts[:, 0:P]
        earlier = consts[:, P:3 * P]
        spare = consts[:, 3 * P:3 * P + 2]
        zeros = sb("zeros", [P, TILES * max(WIDTH)])
        power = sb("power", [P, TILES * GROUPS])

        def w(name, r0=0, r1=None, c0=0, c1=None):
            at, rows, cols = REGIONS[name]
            return weights[r0:rows if r1 is None else r1, at + c0:at + (cols if c1 is None else c1)]

        area = sb("area", [P, 30000])
        area_at = [0]

        def part(shape):
            size = int(np.prod(shape))
            a = area[:, area_at[0]:area_at[0] + size]
            area_at[0] += size
            if len(shape) == 2:
                a = a.rearrange("p (a b) -> p a b", b=shape[1])
            return a

        src_idx = part([GROUPS * TILES])
        dst_idx = part([GROUPS * TILES])
        vec3 = part([GROUPS * TILES, 3])
        vec4 = part([GROUPS * TILES, 4])
        square = part([GROUPS * TILES, 3])
        inv_len = part([GROUPS * TILES])
        sum_sq = part([GROUPS * TILES])
        seen = [part([GROUPS * TILES]) for _ in range(2)]
        moved = part([GROUPS * TILES])
        front_all = [part([GROUPS, REC_F]) for _ in range(2)]
        back_all = [part([GROUPS, REC_B]) for _ in range(2)]
        row_prep = [part([ROW_GROUPS * GROUP]) for _ in range(2)]
        matches = [part([2 * P]) for _ in range(TILES)]
        own_f = [part([GROUPS * TILES]) for _ in range(2)]
        comp = part([2 * S + 2 * V])
        assert area_at[0] <= 30000, area_at

        area_at[0] = 0
        front_rec = [part([REC_F]) for _ in range(2)]
        back_rec = [part([REC_B]) for _ in range(2)]
        target_row = [part([GROUP]) for _ in range(2)]
        edge_feat = [part([GROUP]) for _ in range(2)]
        gath = [part([TILES, HROW + S]) for _ in range(2)]
        v_e0 = [part([TILES, 3 * V]) for _ in range(2)]
        cross_dot = [part([TILES, 4 * V]) for _ in range(2)]
        prod_dot = part([TILES, 3 * V])
        prod_a = part([TILES, 3 * V])
        prod_b = part([TILES, 3 * V])
        hidden = [part([GROUP]) for _ in range(2)]
        weighted = [part([TILES, 3 * P]) for _ in range(2)]
        message = [[part([GROUP]) for _ in range(3)] for _ in range(2)]
        row_to = [part([TILES]) for _ in range(2)]
        same = [part([TILES + TILES // 2, P]) for _ in range(2)]
        edge_out = [part([TILES, 384]) for _ in range(2)]
        outer = part([TILES, 3 * max(OUT_V)])
        summed = [part([TILES, max(WIDTH)]) for _ in range(2)]
        assert area_at[0] <= 30000, area_at

        area_at[0] = 0
        base_in = [part([TILES, HROW]) for _ in range(2)]
        tot_in = [part([TILES, max(WIDTH)]) for _ in range(2)]
        attr_in = [part([3 * TILES]) for _ in range(2)]
        attr = [part([3 * TILES]) for _ in range(2)]
        gates = [part([TILES, S + V]) for _ in range(2)]
        factor = part([6 * TILES])
        y = [part([TILES, HROW]) for _ in range(2)]
        stats = part([TILES, 6])
        moments = [part([TILES, 2]) for _ in range(2)]
        var_eps = [part([TILES]) for _ in range(2)]
        rstd = [part([TILES]) for _ in range(2)]
        x_new = [part([TILES, HROW]) for _ in range(2)]
        x_scaled = [[part([TILES, HROW]) for _ in range(2)] for _ in range(2)]
        v_cols = [[part([GROUP]) for _ in range(2)] for _ in range(2)]
        s_cols = [[part([GROUP]) for _ in range(2)] for _ in range(2)]
        h_out = [part([TILES, HROW]) for _ in range(2)]
        tot_out = [part([TILES, max(WIDTH)]) for _ in range(2)]
        base_out = [part([TILES, HROW]) for _ in range(2)]
        assert area_at[0] <= 30000, area_at

        psum = ctx.enter_context(nc.psum_tensor("psum", [P, 8, GROUP], F32))
        WIDE, WEIGHT, MSG, SUM = (0, 1), (2, 3), (4, 5), (6, 7)

        credited = []

        def tally(name, plan, kind=""):
            t = Tally(sem(name), {"": 1, "dma": 0, "dma, credited": 16}[kind])
            for key, step, times in plan:
                t.phase(key, step, times)
            if not kind:
                credited.append(t)
            return t

        G, H = GROUPS, GROUPS // 2
        LOADS = G // (2 * ROW_GROUPS)
        assert LOADS * 2 * ROW_GROUPS == G

        def edges(step, times):
            return [(("edge", l), step, times) for l in range(LAYERS)]

        def nodes(step, times, passes=range(LAYERS + 1)):
            return [(("node", l), step(l) if callable(step) else step, times) for l in passes]

        s_const = sem("s_const")
        s_edges_in = sem("s_edges_in")
        s_fill = sem("s_fill")
        s_scaled = sem("s_scaled")
        s_comp_mm = sem("s_comp_mm")
        s_comp = sem("s_comp")
        s_comp_put = sem("s_comp_put")
        s_sq = sem("s_sq")
        s_len = sem("s_len")
        s_vec = sem("s_vec")
        s_row_prep = [sem(f"s_row_prep{b}") for b in range(2)]
        s_seen_step = sem("s_seen_step")
        s_own = sem("s_own")
        s_rec = sem("s_rec")
        s_rec_out = sem("s_rec_out")
        s_barrier = sem("s_barrier")
        s_settled = {e: sem(f"s_settled_{n}") for n, e in
                     (("sp", nc.sync.engine), ("pool", nc.gpsimd.engine), ("dve", nc.vector.engine),
                      ("pe", nc.tensor.engine))}

        front_in = [tally(f"front_in{b}", edges(32, H), kind="dma") for b in range(2)]
        back_in = [tally(f"back_in{b}", edges(32, H), kind="dma") for b in range(2)]
        gathered = [tally(f"gathered{b}", edges(64, H), kind="dma") for b in range(2)]
        scattered = tally("scattered", edges(16, TILES * G), kind="dma")
        landed = tally("landed", edges(1, G))
        multiplied = tally("multiplied", edges(1, G))
        prepared = tally("prepared", edges(1, G))
        wide_mm = tally("wide_mm", [(("edge", l), 1, TURNS[l] * G) for l in range(LAYERS)])
        wide_copied = tally("wide_copied", [(("edge", l), 1, TURNS[l] * G) for l in range(LAYERS)])
        weighed = tally("weighed", edges(1, G))
        message_made = tally("message_made", edges(1, G))
        msg_mm = tally("msg_mm", edges(1, TILES * G))
        msg_copied = tally("msg_copied", edges(1, TILES * G))
        outer_made = tally("outer_made", edges(1, G))
        outer_added = tally("outer_added", edges(1, G))
        same_made = tally("same_made", edges(1, G))
        sum_mm = tally("sum_mm", edges(1, TILES * G))
        sum_copied = tally("sum_copied", edges(1, TILES * G))

        inner = range(LAYERS)
        fin = range(1, LAYERS + 1)
        node_in = [tally(f"node_in{b}", nodes(lambda k: 16 if k == 0 else 48, H), kind="dma") for b in range(2)]
        combine_step = tally("combine_step", nodes(lambda k: {1: 1, 2: 6, 3: 2, 4: 2}[k], G, fin))
        gated = tally("gated", nodes(1, G, [1, 4]))
        combined = tally("combined", nodes(1, G, fin))
        stats_made = tally("stats_made", nodes(1, G, fin))
        moments_made = tally("moments_made", nodes(1, G, fin))
        var_made = tally("var_made", nodes(1, G, fin))
        rstd_made = tally("rstd_made", nodes(1, G, fin))
        normed = tally("normed", nodes(1, G, fin))
        x_turned = tally("x_turned", nodes(1, G, inner))
        x_copied = tally("x_copied", nodes(1, G, inner))
        scaled = tally("scaled", nodes(1, G, [1, 2, 3]))
        lin_mm = tally("lin_mm", nodes(2, G, inner))
        lin_act = tally("lin_act", nodes(lambda k: ACT_PAIRS[k], G, inner))
        lin_dve = tally("lin_dve", nodes(lambda k: DVE_PAIRS[k], G, [0, 1, 2]))
        stored = [tally(f"stored{b}", nodes(lambda k: (32, 48, 48, 32)[k], H, inner), kind="dma, credited")
                  for b in range(2)]
        x_stored = [tally(f"x_stored{b}", nodes(16, H, [3, 4]), kind="dma") for b in range(2)]

        block = ctx.enter_context(nc.Block())

        def barrier(eng, count):
            eng.drain().then_inc(s_barrier, 1)
            eng.wait_ge(s_barrier, 5 * count)

        def is_last_ahead(g):
            return isinstance(g.half, int) and g.half == H - 1

        def is_last(g):
            return isinstance(g.half, int) and g.half == H - 1 and g.odd == 1

        def is_third_last(g):
            return isinstance(g.half, int) and g.half == H - 2 and g.odd == 1

        def settle(eng):
            eng.sem_inc(s_settled[eng.engine], 1)

        def lin_banks(pair):
            return psum[:, 4 + 2 * pair:6 + 2 * pair, :]

        def lin_h(pair):
            return lin_banks(pair)[:, :, 3 * V:3 * V + HROW]

        def lin_skip_96(pair):
            return lin_banks(pair).rearrange("p t (u c) -> p t u c", u=2)[:, :, :, 0:3 * V]

        def pair_of(tile, pair, lo, hi):
            return tile[:, 2 * pair:2 * pair + 2, lo:hi]

        r2, r3, r32, r96, r128 = 2 ** -0.5, 3 ** -0.5, 32 ** -0.5, 96 ** -0.5, 128 ** -0.5
        C_S, C_X = float(np.sin(np.pi / 8)), float(np.cos(np.pi / 8))
        scales = [("out0_0", 0, 64, 3 ** 0.5 / 32), ("out0_0", 64, 128, 3 ** 0.5 * r2 / 32), ("out1_0", 0, 64, 1 / 32),
                  ("out1_0", 64, 96, 3 ** 0.5 * r2 / 32), ("out1_0", 96, 128, 1 / 32), ("out2_0", 0, 96, 1 / 32)]
        scales += [("fc1_1", 0, 16, 1 / 4), ("w_1", 0, 64, 1 / 8), ("out0_1", 0, 128, r96), ("out1_1", 0, 96, r96),
                   ("out1_1", 96, 128, r96 * r3), ("nva_1", 0, 96, r32), ("nsa_1", 0, 64, 1 / 8)]
        scales += [("fc1_3", 0, 64, 1 / 8), ("w_3", 0, 64, 1 / 8), ("nva_3", 0, 96, r32), ("nsa_3", 0, 64, 1 / 8),
                   ("out0_3", 0, 64, r128 / 4), ("out0_3", 64, 128, r128 * r2 / 4), ("out1_3", 0, 64, r96 / 4),
                   ("out1_3", 64, 96, r128 * r2 / 4), ("out1_3", 96, 128, r96 * r3 / 4), ("out2_3", 0, 96, r128 / 4)]
        skip_scales = [("nva_2", 96, 96, C_S), ("nvc_2", 96, 96, C_S), ("nsa_2", 64, 64, C_S),
                       ("nsc_2", 64, 64, C_S)]

        comp_parts = [("lsa", "l3s", S), ("lsc", "l3s", S), ("lva", "l3v", V), ("lvc", "l3v", V)]
        comp_at = [0, S, 2 * S, 2 * S + V]

        def comp_moves():
            out = []
            for half in range(2):
                for which in range(2):
                    src = comp_at[which] + V * half
                    col = 2 * V * half + V * which
                    out.append((w("out0_2", S, 2 * S, col, col + V), comp[0:S, src:src + V]))
                    out.append((w("out1_2", 3 * V, 4 * V, 3 * OUT_V[2] + col, 3 * OUT_V[2] + col + V), comp[S:S + V, src:src + V]))
            for which in range(2):
                src = comp_at[2 + which]
                col = OUT_S[2] + V * which
                out.append((w("out0_2", 0, S, col, col + V), comp[0:S, src:src + V]))
                for i in range(3):
                    col = 2 * V * i + V * which
                    out.append((w("out1_2", V * i, V * i + V, col, col + V), comp[S:S + V, src:src + V]))
            return out

        def edge_vec(rec, at, lo, hi):
            return rec[:, at:at + TILES * EXT].rearrange("p (t c) -> p t c", c=EXT)[:, :, lo:hi]

        def hide_use(l, n):
            return 0 if isinstance(n, int) and n == 0 else (n - 1) * TURNS[l] + 1

        def hide_bank(l, g):
            return WIDE[0 if isinstance(g.n, int) and g.n == 0 else ((g.odd - 1) * TURNS[l] + 1) % 2]

        def block_use(l, g, i):
            return g.n * TURNS[l] + (i + 2 - is_last(g))

        def block_bank(l, g, i):
            return WIDE[(g.odd * TURNS[l] + i - is_last(g)) % 2]

        def sp_edge(sp, l):
            key = ("edge", l)
            k = min(l, 1)

            def front(g):
                b = g.odd
                sp.wait_ge(gathered[b].sem, gathered[b].at(key, g.half))
                settle(sp)
                sp.wait_ge(prepared.sem, prepared.at(key, g.n - 1))
                settle(sp)
                sp.wait_ge(wide_mm.sem, wide_mm.at(key, hide_use(l, g.n - 2) + 1))
                settle(sp)
                sp.dma_start(front_rec[b], rec_f[k][:, bass.ds(g.n * REC_F, REC_F)]).then_inc(front_in[b].sem, 16)
                sp.dma_start(edge_feat[b][0:FC_IN[l], :], d[f"feat{l}"][:, bass.ds(g.n * GROUP, GROUP)])\
                  .then_inc(front_in[b].sem, 16)

            def back(g):
                b = g.odd
                rows = d["dst_rows"] if l else d["src_rows"]
                sp.wait_ge(outer_added.sem, outer_added.at(key, g.n - 1))
                settle(sp)
                sp.wait_ge(same_made.sem, same_made.at(key, g.n - 1))
                settle(sp)
                sp.dma_start(back_rec[b], rec_b[k][:, bass.ds(g.n * REC_B, REC_B)]).then_inc(back_in[b].sem, 16)
                sp.dma_start(target_row[b].bitcast(I32), rows[bass.ds(g.n, 1), :].to_broadcast([P, GROUP]))\
                  .then_inc(back_in[b].sem, 16)

            def step(g, has_back, has_it, has_ahead):
                if has_ahead and not is_last_ahead(g):
                    front(g.ahead().ahead())
                if has_it:
                    back(g)

            front(Group(0, 0))
            front(Group(0, 1))
            over_groups(sp, step)
            barrier(sp, 3 + 2 * l)

        def sp_node(sp, k):
            key = ("node", k)

            def load(g):
                b = g.odd
                n = g.n * GROUP
                if k == 0:
                    sp.wait_ge(x_turned.sem, x_turned.at(key, g.n - 1))
                    settle(sp)
                    sp.dma_start(x_new[b].rearrange("p t c -> p (t c)"),
                                 d["x"][bass.ds(n, GROUP), :].rearrange("(p t) c -> p (t c)", t=TILES))\
                      .then_inc(node_in[b].sem, 16)
                    return
                sp.wait_ge(combined.sem, combined.at(key, g.n - 1))
                settle(sp)
                sp.dma_start(tot_in[b][:, :, 0:WIDTH[k - 1]],
                             totals[k - 1][bass.ds(n, GROUP), :].rearrange("(p t) c -> p t c", t=TILES))\
                  .then_inc(node_in[b].sem, 16)
                sp.dma_start(base_in[b].rearrange("p t c -> p (t c)"),
                             base[k - 1][bass.ds(n, GROUP), :].rearrange("(p t) c -> p (t c)", t=TILES))\
                  .then_inc(node_in[b].sem, 16)
                if k < LAYERS:
                    sp.wait_ge(scaled.sem, scaled.at(key, g.n - 1))
                    settle(sp)
                sp.dma_start(attr_in[b], d["attrs"][:, bass.ds(g.n * 3 * TILES, 3 * TILES)])\
                  .then_inc(node_in[b].sem, 16)

            def put(g, table, tile, done):
                sp.dma_start(table[bass.ds(g.n * GROUP, GROUP), :].rearrange("(p t) c -> p t c", t=TILES), tile)\
                  .then_inc(done[g.odd].sem, 16)

            def store_x(g):
                sp.wait_ge(normed.sem, normed.at(key, g.n + 1))
                settle(sp)
                put(g, d["out"] if k == LAYERS else base[3], x_new[g.odd], x_stored)

            def store(g):
                b = g.odd
                sp.wait_ge(lin_act.sem, lin_act.at(key, g.n + 1))
                settle(sp)
                if k != 3:
                    sp.wait_ge(lin_dve.sem, lin_dve.at(key, g.n + 1))
                    settle(sp)
                put(g, h_table[k], h_out[b], stored)
                if k in (0, 3):
                    put(g, totals[k], tot_out[b][:, :, 0:WIDTH[k]], stored)
                else:
                    put(g, totals[k], zeros[:, 0:TILES * WIDTH[k]].rearrange("p (t c) -> p t c", t=TILES),
                        stored)
                    put(g, base[k], base_out[b], stored)

            def step(g, has_back, has_it, has_ahead):
                if k == 0:
                    if has_ahead and not is_last_ahead(g):
                        load(g.ahead().ahead())
                elif has_ahead and not is_last_ahead(g) and not is_third_last(g):
                    load(g.ahead().ahead().ahead())
                if has_back:
                    (store_x if k == LAYERS else store)(g.back())
                if k == 3 and has_ahead:
                    store_x(g.ahead())

            load(Group(0, 0))
            load(Group(0, 1))
            if k:
                load(Group(1, 0))
            if k == 3:
                store_x(Group(0, 0))
            over_groups(sp, step, peeled=2)
            for b in range(2):
                if k < LAYERS:
                    sp.wait_ge(stored[b].sem, stored[b].at(key, H))
                if k >= 3:
                    sp.wait_ge(x_stored[b].sem, x_stored[b].at(key, H))
            barrier(sp, 2 + 2 * k)

        @block.sync
        def _(sp):
            for t in credited:
                sp.sem_inc(t.sem, 1)
            sp.dma_start(weights[:, :], d["weights"]).then_inc(s_const, 16)
            sp.dma_start(consts[:, :], d["consts"]).then_inc(s_const, 16)
            sp.dma_start(src_idx.bitcast(I32), d["src_lanes"]).then_inc(s_edges_in, 16)
            sp.dma_start(dst_idx.bitcast(I32), d["dst_lanes"]).then_inc(s_edges_in, 16)
            sp.dma_start(vec3.rearrange("p a b -> p (a b)"), d["vec3"]).then_inc(s_edges_in, 16)
            sp.dma_start(vec4.rearrange("p a b -> p (a b)"), d["vec4"]).then_inc(s_edges_in, 16)
            for which, rows in ((0, d["src_loads"]), (1, d["dst_loads"])):
                def row(n, b):
                    sp.dma_start(row_prep[b].bitcast(I32),
                                 rows[bass.ds(n, 1), :].to_broadcast([P, ROW_GROUPS * GROUP]))\
                      .then_inc(s_row_prep[b], 16)
                for b in range(2):
                    if which:
                        sp.wait_ge(s_seen_step, G - ROW_GROUPS * (1 - b))
                    row(b, b)
                with sp.Fori(1, LOADS) as turn:
                    for b in range(2):
                        sp.wait_ge(s_seen_step, turn * (2 * ROW_GROUPS) + (G * which + ROW_GROUPS * (b - 1)))
                        row(turn * 2 + b, b)
            sp.wait_ge(s_comp, 4)
            sp.wait_ge(s_scaled, 1)
            moves = comp_moves()
            for dst, src in moves:
                sp.dma_start(dst, src).then_inc(s_comp_put, 16)
            sp.wait_ge(s_comp_put, 16 * len(moves))
            sp.wait_ge(s_rec, 1)
            sp.wait_ge(s_fill, 1)
            for k in range(2):
                sp.dma_start(rec_f[k], front_all[k].rearrange("p a b -> p (a b)")).then_inc(s_rec_out, 16)
                sp.dma_start(rec_b[k], back_all[k].rearrange("p a b -> p (a b)")).then_inc(s_rec_out, 16)
            spare_rows_in = (stored[0].sem, stored[1].sem, s_rec_out, s_rec_out)
            for l in range(LAYERS):
                sp.dma_start(totals[l][NPAD:ROWS, :].rearrange("(a p) c -> p a c", p=P),
                             zeros[:, 0:2 * WIDTH[l]].rearrange("p (a c) -> p a c", a=2)).then_inc(spare_rows_in[l], 16)
            for credit in spare_rows_in[0:2]:
                sp.wait_ge(credit, 16)
            sp.wait_ge(s_rec_out, 16 * 6)
            barrier(sp, 1)
            sp_node(sp, 0)
            for l in range(LAYERS):
                sp_edge(sp, l)
                sp_node(sp, l + 1)

        def pool_edge(pool, l):
            key = ("edge", l)

            def gather(g, t):
                b = g.odd
                if t == 0:
                    pool.wait_ge(front_in[b].sem, front_in[b].at(key, g.half + 1))
                    settle(pool)
                    pool.wait_ge(message_made.sem, message_made.at(key, g.n - 1))
                settle(pool)
                pool.indirect_dma_start(
                    gath[b][:, t, 0:HROW], None, h_table[l][:, :],
                    bass.IndirectOffsetOnAxis(front_rec[b][:, t:t + 1].bitcast(I32), 0)).then_inc(gathered[b].sem, 16)

            def scatter(g, t):
                b = g.odd
                if t == 0:
                    pool.wait_ge(same_made.sem, same_made.at(key, g.n + 1))
                    settle(pool)
                pool.wait_ge(sum_copied.sem, sum_copied.at(key, g.n * TILES + t + 1))
                settle(pool)
                if t % 2 == 0:
                    pool.wait_ge(scattered.sem, scattered.at(key, g.n * TILES + t))
                    pool.sem_inc(landed.sem if t == 0 else s_settled[nc.gpsimd.engine], 1)
                pool.indirect_dma_start(
                    totals[l][:, :], bass.IndirectOffsetOnAxis(row_to[b][:, t:t + 1].bitcast(I32), 0),
                    summed[b][:, t, 0:WIDTH[l]], None, compute_op=ALU.add).then_inc(scattered.sem, 16)

            def step(g, has_back, has_it, has_ahead):
                for pair in range(TILES // 2):
                    for t in (2 * pair, 2 * pair + 1):
                        if has_ahead and not is_last_ahead(g):
                            gather(g.ahead().ahead(), t)
                    for t in (2 * pair, 2 * pair + 1):
                        if has_back and not (isinstance(g.half, int) and g.half == 0):
                            scatter(g.back().back(), t)

            for g in (Group(0, 0), Group(0, 1)):
                for t in range(TILES):
                    gather(g, t)
            over_groups(pool, step, start=2)
            for t in range(TILES):
                scatter(Group(H - 1, 1), t)
            pool.wait_ge(scattered.sem, scattered.at(key, G * TILES))
            barrier(pool, 3 + 2 * l)

        def pool_node(pool, k):
            key = ("node", k)

            def root(g):
                b = g.odd
                pool.wait_ge(var_made.sem, var_made.at(key, g.n + 1))
                settle(pool)
                nc.gpsimd.tensor_tensor(rstd[b], var_eps[b], power[:, 0:TILES], ALU.pow).then_inc(rstd_made.sem, 1)

            def step(g, has_back, has_it, has_ahead):
                if has_ahead:
                    root(g.ahead())

            root(Group(0, 0))
            over_groups(pool, step)
            barrier(pool, 2 + 2 * k)

        @block.gpsimd
        def _(pool):
            pool.wait_ge(s_sq, 2)
            pool.wait_ge(s_fill, 1)
            nc.gpsimd.tensor_tensor(inv_len, sum_sq, power[:, 0:GROUPS * TILES], ALU.pow).then_inc(s_len, 1)
            barrier(pool, 1)
            barrier(pool, 2)
            for l in range(LAYERS):
                pool_edge(pool, l)
                pool_node(pool, l + 1)

        def dve_edge(dve, l):
            key = ("edge", l)
            nk, ns, width = OUT_V[l], OUT_S[l], WIDTH[l]
            if l == 1:
                for b in range(2):
                    nc.vector.memset(edge_out[b][:, :, width - 1:width], 1.0)

            def prepare(g):
                b = g.odd
                v3 = gath[b][:, :, 0:3 * V].rearrange("p t (i c) -> p t i c", c=V)
                dve.wait_ge(gathered[b].sem, gathered[b].at(key, g.half + 1))
                dve.wait_ge(front_in[b].sem, front_in[b].at(key, g.half + 1))
                dve.wait_ge(message_made.sem, message_made.at(key, g.n - 1))

                def e(lo, hi, shape):
                    return edge_vec(front_rec[b], TILES, lo, hi).unsqueeze(3).to_broadcast([P, TILES, hi - lo, shape])

                def four(a):
                    return a.rearrange("p t (i c) -> p t i c", c=V)

                def e0(width):
                    return edge_vec(front_rec[b], TILES, 0, 1).to_broadcast([P, TILES, width])

                if HAS_E0[l]:
                    nc.vector.tensor_tensor(gath[b][:, :, HROW:HROW + S], gath[b][:, :, 3 * V:HROW], e0(S), ALU.mult)
                    nc.vector.tensor_tensor(v_e0[b], gath[b][:, :, 0:3 * V], e0(3 * V), ALU.mult)
                if CROSS[l]:
                    nc.vector.tensor_tensor(four(prod_a)[:, :, 0:2, :], v3[:, :, 1:3, :], e(3, 5, V), ALU.mult)
                    nc.vector.tensor_tensor(four(prod_a)[:, :, 2, :], v3[:, :, 0, :],
                                            edge_vec(front_rec[b], TILES, 2, 3).to_broadcast([P, TILES, V]), ALU.mult)
                    nc.vector.tensor_tensor(four(prod_b)[:, :, 0, :], v3[:, :, 2, :],
                                            edge_vec(front_rec[b], TILES, 2, 3).to_broadcast([P, TILES, V]), ALU.mult)
                    nc.vector.tensor_tensor(four(prod_b)[:, :, 1:3, :], v3[:, :, 0:2, :], e(3, 5, V), ALU.mult)
                nc.vector.tensor_tensor(four(prod_dot), v3, e(1, 4, V), ALU.mult).then_inc(multiplied.sem, 1)
                dve.wait_ge(multiplied.sem, multiplied.at(key, g.n + 1))
                if CROSS[l]:
                    nc.vector.tensor_tensor(cross_dot[b][:, :, 0:3 * V], prod_a, prod_b, ALU.subtract)
                nc.vector.tensor_reduce(cross_dot[b][:, :, 3 * V:4 * V], prod_dot.rearrange("p t (i c) -> p t c i", c=V),
                                        AX_X, ALU.add).then_inc(prepared.sem, 1)

            def make_message(g):
                b = g.odd
                wt = psum[:, WEIGHT[0]:WEIGHT[1] + 1, :].rearrange("p b (u c) -> p (b u) c", u=2)
                out = weighted[b]

                def parts(a, c):
                    return a.rearrange("p t (i c) -> p t i c", c=c)

                dve.wait_ge(weighed.sem, weighed.at(key, g.n + 1))
                dve.wait_ge(prepared.sem, prepared.at(key, g.n + 1))
                dve.wait_ge(wide_mm.sem, wide_mm.at(key, (g.n - 1) * TURNS[l] + 1))
                if HAS_E0[l]:
                    s_pair = parts(gath[b][:, :, 3 * V:HROW + S], S)
                else:
                    s_pair = gath[b][:, :, 3 * V:HROW].unsqueeze(2).to_broadcast([P, TILES, 2, S])
                s_to = parts(out[:, :, 0:2 * P], P)[:, :, :, 0:S] if CROSS[l] else parts(out[:, :, 0:2 * S], S)
                nc.vector.tensor_tensor(s_to, parts(wt[:, :, 0:2 * S], S), s_pair, ALU.mult)
                v_in = v_e0[b] if HAS_E0[l] else gath[b][:, :, 0:3 * V]
                v_at = 2 * P if CROSS[l] else P
                if CROSS[l]:
                    nc.vector.tensor_tensor(
                        parts(out[:, :, S:P], V), wt[:, :, 2 * S + V:2 * S + 2 * V].unsqueeze(2).to_broadcast([P, TILES, 2, V]),
                        parts(cross_dot[b][:, :, 0:2 * V], V), ALU.mult)
                    nc.vector.tensor_tensor(out[:, :, P + S:2 * P], wt[:, :, 2 * S + V:2 * S + 3 * V],
                                            cross_dot[b][:, :, 2 * V:4 * V], ALU.mult)
                else:
                    nc.vector.tensor_tensor(out[:, :, P + 3 * V:2 * P], wt[:, :, 2 * S + V:2 * S + 2 * V],
                                            cross_dot[b][:, :, 3 * V:4 * V], ALU.mult)
                nc.vector.tensor_tensor(
                    parts(out[:, :, v_at:v_at + 3 * V], V), wt[:, :, 2 * S:2 * S + V].unsqueeze(2).to_broadcast([P, TILES, 3, V]),
                    parts(v_in, V), ALU.mult).then_inc(message_made.sem, 1)

            def compare(g):
                b = g.odd
                dve.wait_ge(back_in[b].sem, back_in[b].at(key, g.half + 1))
                dve.wait_ge(sum_mm.sem, sum_mm.at(key, (g.n - 1) * TILES))
                dve.wait_ge(landed.sem, landed.at(key, g.n))
                nc.vector.tensor_copy(row_to[b].bitcast(I32), back_rec[b][:, TILES:2 * TILES].bitcast(I32))
                nc.vector.tensor_tensor(
                    same[b][:, 0:TILES], target_row[b].bitcast(I32).rearrange("p (t c) -> p t c", c=P),
                    back_rec[b][:, 0:TILES].bitcast(I32).unsqueeze(2).to_broadcast([P, TILES, P]), ALU.is_equal)
                nc.vector.tensor_tensor(
                    same[b][:, TILES:], target_row[b].bitcast(I32).rearrange("p (h u c) -> p h u c", u=2, c=P)[:, :, 0, :],
                    back_rec[b][:, 0:TILES].bitcast(I32).rearrange("p (h u) -> p h u", u=2)[:, :, 1].unsqueeze(2)
                    .to_broadcast([P, TILES // 2, P]), ALU.is_equal).then_inc(same_made.sem, 1)

            def add_outer(g):
                b = g.odd
                dve.wait_ge(msg_copied.sem, msg_copied.at(key, (g.n + 1) * TILES))
                outer4 = outer[:, :, 0:3 * nk].rearrange("p t (i c) -> p t i c", c=nk)
                nc.vector.tensor_tensor(
                    outer4, edge_out[b][:, :, K_AT[l]:K_AT[l] + nk].unsqueeze(2).to_broadcast([P, TILES, 3, nk]),
                    edge_vec(back_rec[b], 2 * TILES, 1, 4).unsqueeze(3).to_broadcast([P, TILES, 3, nk]),
                    ALU.mult).then_inc(outer_made.sem, 1)
                dve.wait_ge(outer_made.sem, outer_made.at(key, g.n + 1))
                v_out = edge_out[b][:, :, V_AT[l]:V_AT[l] + 3 * nk]
                nc.vector.tensor_tensor(v_out, v_out, outer[:, :, 0:3 * nk], ALU.add).then_inc(outer_added.sem, 1)

            def step(g, has_back, has_it, has_ahead):
                if has_ahead:
                    prepare(g.ahead())
                if has_back:
                    compare(g.back())
                    add_outer(g.back())
                if has_ahead:
                    make_message(g.ahead())

            prepare(Group(0, 0))
            make_message(Group(0, 0))
            over_groups(dve, step)
            barrier(dve, 3 + 2 * l)

        def dve_node(dve, k):
            key = ("node", k)
            f = k - 1

            def combine(g):
                b = g.odd
                dve.wait_ge(node_in[b].sem, node_in[b].at(key, g.half + 1))
                dve.wait_ge(normed.sem, normed.at(key, g.n - 1))
                t_in = tot_in[b]
                a = attr_in[b][:, 0:TILES]
                y5 = y[b].rearrange("p t (i c) -> p t i c", c=V)
                done = [0]

                def link(ins):
                    ins.then_inc(combine_step.sem, 1)
                    done[0] += 1
                    first, step = combine_step.first[key]
                    dve.wait_ge(combine_step.sem, g.n * step + (first + done[0]))

                def wide(x, width):
                    return x.unsqueeze(2).to_broadcast([P, TILES, width])

                if f in (0, 3):
                    dve.wait_ge(gated.sem, gated.at(key, g.n + 1))
                    gate = gates[b]
                    if f == 3:
                        link(nc.vector.tensor_tensor(gate, gate, wide(a, S + V), ALU.mult))
                    nc.vector.tensor_tensor(y[b][:, :, 3 * V:HROW], t_in[:, :, 3 * V:HROW], gate[:, :, 0:S], ALU.mult)
                    link(nc.vector.tensor_tensor(
                        y5[:, :, 0:3, :], t_in[:, :, 0:3 * V].rearrange("p t (i c) -> p t i c", c=V),
                        gate[:, :, S:S + V].unsqueeze(2).to_broadcast([P, TILES, 3, V]), ALU.mult))
                elif f == 1:
                    q = [factor[:, TILES * i:TILES * i + TILES] for i in range(6)]
                    count, alpha = t_in[:, :, HROW + 1:HROW + 2], t_in[:, :, HROW:HROW + 1]
                    link(nc.vector.tensor_scalar(q[0].unsqueeze(2), count, 1.0, None, ALU.max))
                    link(nc.vector.reciprocal(q[1], q[0]))
                    link(nc.vector.tensor_tensor(q[2], q[1], a, ALU.mult))
                    link(nc.vector.tensor_tensor(q[3], q[2], q[2], ALU.mult))
                    link(nc.vector.tensor_tensor(q[4].unsqueeze(2), q[3].unsqueeze(2), alpha, ALU.mult))
                    link(nc.vector.tensor_tensor(y[b], t_in[:, :, 0:HROW], wide(q[4], HROW), ALU.mult))
                else:
                    t5 = t_in[:, :, 0:WIDTH[2]].rearrange("p t (i u c) -> p t i u c", u=2, c=V)
                    fa, fc = factor[:, 0:TILES], factor[:, TILES:2 * TILES]
                    nc.vector.tensor_tensor(fa, a, attr_in[b][:, 2 * TILES:3 * TILES], ALU.mult)
                    link(nc.vector.tensor_tensor(fc, attr_in[b][:, TILES:2 * TILES], attr_in[b][:, 2 * TILES:3 * TILES],
                                                 ALU.mult))
                    base5 = base_in[b].rearrange("p t (i c) -> p t i c", c=V)
                    for t in range(TILES):
                        last = nc.vector.scalar_tensor_tensor(y5[:, t], t5[:, t, :, 1, :], fc[:, t:t + 1], base5[:, t],
                                                              ALU.mult, ALU.add)
                    link(last)
                    for t in range(TILES):
                        last = nc.vector.scalar_tensor_tensor(y5[:, t], t5[:, t, :, 0, :], fa[:, t:t + 1], y5[:, t],
                                                              ALU.mult, ALU.add)
                    last.then_inc(combined.sem, 1)
                if f != 2:
                    nc.vector.tensor_tensor(y[b], y[b], base_in[b], ALU.add).then_inc(combined.sem, 1)
                assert done[0] == combine_step.first[key][1]
                dve.wait_ge(combined.sem, combined.at(key, g.n + 1))
                for t in range(TILES):
                    last = nc.vector.bn_stats(stats[:, t, :], y[b][:, t, :])
                last.then_inc(stats_made.sem, 1)
                dve.wait_ge(stats_made.sem, stats_made.at(key, g.n + 1))
                settle(dve)
                for t in range(TILES):
                    last = nc.vector.bn_aggr(moments[b][:, t, :], stats[:, t, :])
                last.then_inc(moments_made.sem, 1)
                dve.wait_ge(moments_made.sem, moments_made.at(key, g.n + 1))
                nc.vector.tensor_scalar(var_eps[b].unsqueeze(2), moments[b][:, :, 1:2], NORM_EPS, None, ALU.add)\
                  .then_inc(var_made.sem, 1)

            def normalise(g):
                b = g.odd
                dve.wait_ge(rstd_made.sem, rstd_made.at(key, g.n + 1))
                if k >= 3:
                    dve.wait_ge(x_stored[b].sem, x_stored[b].at(key, g.half))
                if k == 3:
                    dve.wait_ge(x_turned.sem, x_turned.at(key, g.n - 1))
                if k in (1, 2):
                    dve.wait_ge(scaled.sem, scaled.at(key, g.n - 1))
                    dve.wait_ge(lin_dve.sem, lin_dve.at(key, g.n - 1))
                for t in range(TILES):
                    last = nc.vector.tensor_scalar(x_new[b][:, t, :], y[b][:, t, :], moments[b][:, t, 0:1],
                                                   rstd[b][:, t:t + 1], ALU.subtract, ALU.mult)
                last.then_inc(normed.sem, 1)

            def linear_out(g):
                b = g.odd
                dve.wait_ge(stored[b].sem, stored[b].at(key, g.half))
                for pair in ((1,), (0, 1), (0, 1))[k]:
                    dve.wait_ge(lin_mm.sem, lin_mm.at_pair(key, g.n, pair))
                    if k == 0:
                        nc.vector.tensor_copy(pair_of(h_out[b], pair, 0, HROW), lin_h(pair))
                        nc.vector.tensor_copy(
                            pair_of(tot_out[b], pair, 0, 6 * V).rearrange("p t (u c) -> p t u c", u=2),
                            lin_skip_96(pair)).then_inc(lin_dve.sem, 1)
                    else:
                        nc.vector.tensor_tensor(pair_of(base_out[b], pair, 0, 3 * V), lin_banks(pair)[:, :, 0:3 * V],
                                                pair_of(x_new[b], pair, 0, 3 * V), ALU.add)
                        nc.vector.tensor_tensor(pair_of(base_out[b], pair, 3 * V, HROW),
                                                lin_banks(pair)[:, :, 3 * V + HROW:3 * V + HROW + S],
                                                pair_of(x_new[b], pair, 3 * V, HROW), ALU.add).then_inc(lin_dve.sem, 1)

            def step(g, has_back, has_it, has_ahead):
                if has_ahead and k:
                    combine(g.ahead())
                if has_it and k == LAYERS:
                    normalise(g)
                if has_back and k < 3:
                    linear_out(g.back())
                if has_ahead and k in (1, 2, 3):
                    normalise(g.ahead())

            if k:
                combine(Group(0, 0))
            if k in (1, 2, 3):
                normalise(Group(0, 0))
            over_groups(dve, step)
            barrier(dve, 2 + 2 * k)

        @block.vector
        def _(dve):
            nc.vector.memset(zeros[:, :], 0.0)
            nc.vector.memset(power[:, :], -0.5).then_inc(s_fill, 1)
            dve.wait_ge(s_const, 32)
            for name, r0, r1, by in scales:
                nc.vector.tensor_scalar(w(name, r0, r1), w(name, r0, r1), by, None, ALU.mult)
            for name, rows, cols, by in skip_scales:
                at = S if rows == S else 0
                skip_cols = w(name, 0, rows, at, at + cols)
                last = nc.vector.tensor_scalar(skip_cols, skip_cols, by, None, ALU.mult)
            last.then_inc(s_scaled, 1)
            dve.wait_ge(s_edges_in, 64)
            nc.vector.tensor_tensor(square, vec3, vec3, ALU.mult).then_inc(s_sq, 1)
            dve.wait_ge(s_sq, 1)
            nc.vector.tensor_reduce(sum_sq, square, AX_X, ALU.add).then_inc(s_sq, 1)
            for which, idx in ((0, src_idx), (1, dst_idx)):
                nc.vector.tensor_copy(own_f[which], idx.bitcast(I32)).then_inc(s_own, 1)
            dve.wait_ge(s_own, 2)
            for which in range(2):
                def search(n, u, i):
                    row = row_prep[i // ROW_GROUPS].bitcast(I32)
                    at = i % ROW_GROUPS * GROUP
                    if i % ROW_GROUPS == 0:
                        dve.wait_ge(s_row_prep[i // ROW_GROUPS], u * 16 + 16 * (LOADS * which + 1))
                    if which or i or not isinstance(u, int):
                        dve.wait_ge(s_seen_step, n + G * which)
                    for t in range(TILES):
                        first = t // 2 * 2 if t % 2 else t
                        width = (t + 1 - first) * P
                        last = nc.vector.scalar_tensor_tensor(
                            matches[t][:, 0:width], row[:, at + first * P:at + (t + 1) * P],
                            own_f[which][:, bass.ds(n * TILES + t, 1)], earlier[:, 2 * P - width:],
                            ALU.is_equal, ALU.mult, accum_out=seen[which][:, bass.ds(n * TILES + t, 1)])
                    last.then_inc(s_seen_step, 1)
                for i in range(2 * ROW_GROUPS):
                    search(i, 0, i)
                with dve.Fori(1, LOADS) as u:
                    for i in range(2 * ROW_GROUPS):
                        search(u * (2 * ROW_GROUPS) + i, u, i)
            dve.wait_ge(s_seen_step, G * 2)
            for which in range(2):
                nc.vector.tensor_scalar(seen[which], seen[which], 1.0, None, ALU.min)
            step = [0]

            def link(ins):
                ins.then_inc(s_vec, 1)
                step[0] += 1
                dve.wait_ge(s_vec, step[0])

            dve.wait_ge(s_len, 1)
            link(nc.vector.tensor_tensor(square, vec3, inv_len.unsqueeze(2).to_broadcast([P, G * TILES, 3]), ALU.mult))
            for k in range(2):
                for rec, at in ((front_all[k], TILES), (back_all[k], 2 * TILES)):
                    e = rec[:, :, at:at + TILES * EXT].rearrange("p g (t c) -> p g t c", c=EXT)
                    if k == 0:
                        vec, lo = square.rearrange("p (g t) c -> p g t c", t=TILES), 0
                        for t in range(TILES):
                            nc.vector.memset(e[:, :, t, 0:1], 1.0)
                    else:
                        vec, lo = vec4.rearrange("p (g t) c -> p g t c", t=TILES), 1
                    for t in range(TILES):
                        if k:
                            nc.vector.tensor_copy(e[:, :, t, 0:1], vec[:, :, t, 0:1])
                        nc.vector.tensor_copy(e[:, :, t, 1:4], vec[:, :, t, lo:lo + 3])
                        nc.vector.tensor_copy(e[:, :, t, 4:6], vec[:, :, t, lo:lo + 2])
                source, target = ((dst_idx, src_idx), (src_idx, dst_idx))[k]

                def lanes(a):
                    return a.bitcast(I32).rearrange("p (g t) -> p g t", t=TILES)

                nc.vector.tensor_copy(front_all[k][:, :, 0:TILES].bitcast(I32), lanes(source))
                nc.vector.tensor_copy(back_all[k][:, :, 0:TILES].bitcast(I32), lanes(target))
                for odd in range(2):
                    last = nc.vector.tensor_scalar(
                        moved.rearrange("p (n u) -> p n u", u=2)[:, :, odd],
                        target.bitcast(I32).rearrange("p (n u) -> p n u", u=2)[:, :, odd],
                        -1.0, spare[:, odd:odd + 1], ALU.mult, ALU.add)
                link(last)
                link(nc.vector.tensor_tensor(moved, moved, seen[k], ALU.mult))
                link(nc.vector.tensor_tensor(back_all[k][:, :, TILES:2 * TILES].bitcast(I32),
                                             moved.rearrange("p (g t) -> p g t", t=TILES), lanes(target), ALU.add))
            dve.drain().then_inc(s_rec, 1)
            barrier(dve, 1)
            dve_node(dve, 0)
            for l in range(LAYERS):
                dve_edge(dve, l)
                dve_node(dve, l + 1)

        def act_edge(act, l):
            key = ("edge", l)
            nk, width = OUT_V[l], WIDTH[l]

            def hide(g):
                b = g.odd
                act.wait_ge(wide_mm.sem, wide_mm.at(key, hide_use(l, g.n) + 1))
                act.wait_ge(weighed.sem, weighed.at(key, g.n - 1))
                nc.scalar.activation(hidden[b][0:FC_HID[l], :], psum[0:FC_HID[l], hide_bank(l, g), :],
                                     ACT.Relu if l == 0 else ACT.Silu).then_inc(wide_copied.sem, 1)

            def copy_block(g, i):
                b, rows = g.odd, BLOCKS[l][i]
                act.wait_ge(wide_mm.sem, wide_mm.at(key, block_use(l, g, i) + 1))
                act.wait_ge(msg_mm.sem, msg_mm.at(key, (g.n - 1) * TILES))
                nc.scalar.copy(message[b][i][0:rows, :], psum[0:rows, block_bank(l, g, i), :])\
                  .then_inc(wide_copied.sem, 1)

            def copy_message(g):
                b = g.odd
                for t in range(TILES):
                    n = g.n * TILES + t
                    acc = psum[:, MSG[t % 2], :]
                    act.wait_ge(msg_mm.sem, msg_mm.at(key, n + 1))
                    if t == 0:
                        act.wait_ge(sum_mm.sem, sum_mm.at(key, (g.n - 1) * TILES))
                    if l == 1:
                        nc.scalar.copy(edge_out[b][:, t, 0:width - 1], acc[:, 0:width - 1])
                        last = nc.scalar.copy(edge_out[b][:, t, width:width + nk], acc[:, width:width + nk])
                    else:
                        last = nc.scalar.copy(edge_out[b][:, t, 0:width + nk], acc[:, 0:width + nk])
                    last.then_inc(msg_copied.sem, 1)

            def copy_sum(g):
                b = g.odd
                for t in range(TILES):
                    n = g.n * TILES + t
                    act.wait_ge(sum_mm.sem, sum_mm.at(key, n + 1))
                    if t == 0:
                        act.wait_ge(landed.sem, landed.at(key, g.n))
                    nc.scalar.copy(summed[b][:, t, 0:width], psum[:, SUM[t % 2], 0:width]).then_inc(sum_copied.sem, 1)

            def step(g, has_back, has_it, has_ahead):
                if has_ahead:
                    hide(g.ahead())
                if has_back:
                    copy_message(g.back())
                if has_it:
                    for i in range(len(BLOCKS[l])):
                        copy_block(g, i)
                if has_back:
                    copy_sum(g.back())

            hide(Group(0, 0))
            over_groups(act, step)
            barrier(act, 3 + 2 * l)

        def act_node(act, k):
            key = ("node", k)

            def gate(g):
                b = g.odd
                act.wait_ge(node_in[b].sem, node_in[b].at(key, g.half + 1))
                act.wait_ge(combined.sem, combined.at(key, g.n - 1))
                if k == 1:
                    nc.scalar.activation(gates[b], tot_in[b][:, :, 3 * V:WIDTH[0]], ACT.Sigmoid).then_inc(gated.sem, 1)
                else:
                    for t in range(TILES):
                        last = nc.scalar.activation(gates[b][:, t, :], tot_in[b][:, t, 3 * V:WIDTH[3]], ACT.Sigmoid,
                                                    scale=attr_in[b][:, t:t + 1])
                    last.then_inc(gated.sem, 1)

            def scale_x(g):
                b = g.odd
                act.wait_ge(node_in[b].sem, node_in[b].at(key, g.half + 1))
                if k == 3:
                    act.wait_ge(lin_act.sem, lin_act.at(key, g.n - 1))
                    nc.scalar.copy(attr[b], attr_in[b]).then_inc(scaled.sem, 1)
                    return
                act.wait_ge(normed.sem, normed.at(key, g.n + 1))
                act.wait_ge(x_turned.sem, x_turned.at(key, g.n - 1))
                for path in range(PATHS[k]):
                    for t in range(TILES):
                        col = path * TILES + t
                        last = nc.scalar.activation(x_scaled[path][b][:, t, :], x_new[b][:, t, :], ACT.Copy,
                                                    scale=attr_in[b][:, col:col + 1])
                last.then_inc(scaled.sem, 1)

            def copy_x(g):
                b = g.odd
                act.wait_ge(x_turned.sem, x_turned.at(key, g.n + 1))
                act.wait_ge(lin_mm.sem, lin_mm.at(key, g.n - 1))
                for path in range(PATHS[k]):
                    nc.scalar.copy(v_cols[path][b][0:3 * V, :], psum[0:3 * V, 2 * path, :])
                    last = nc.scalar.copy(s_cols[path][b][0:S, :], psum[0:S, 2 * path + 1, :])
                last.then_inc(x_copied.sem, 1)

            def linear_out(g):
                b = g.odd
                act.wait_ge(stored[b].sem, stored[b].at(key, g.half))
                if k == 3:
                    act.wait_ge(scaled.sem, scaled.at(key, g.n + 1))
                for pair in range(ACT_PAIRS[k]):
                    if k in (1, 2):
                        act.wait_ge(lin_dve.sem, lin_dve.at_pair(key, g.n, pair))
                    else:
                        act.wait_ge(lin_mm.sem, lin_mm.at_pair(key, g.n, pair))
                    if k == 3:
                        for t in (2 * pair, 2 * pair + 1):
                            nc.scalar.activation(h_out[b][:, t, :], lin_h(pair)[:, t % 2, :], ACT.Copy,
                                                 scale=attr[b][:, t:t + 1])
                    else:
                        last = nc.scalar.copy(pair_of(h_out[b], pair, 0, HROW), lin_h(pair))
                    if k in (0, 3):
                        last = nc.scalar.copy(pair_of(tot_out[b], pair, 0, 6 * V).rearrange("p t (u c) -> p t u c", u=2),
                                              lin_skip_96(pair))
                    last.then_inc(lin_act.sem, 1)

            def step(g, has_back, has_it, has_ahead):
                if has_it and k < LAYERS:
                    copy_x(g)
                if has_back and k < LAYERS:
                    linear_out(g.back())
                if has_ahead and k in (1, 4) and not is_last_ahead(g):
                    gate(g.ahead().ahead())
                if has_ahead and k in (1, 2, 3):
                    scale_x(g.ahead())

            if k in (1, 4):
                gate(Group(0, 0))
                gate(Group(0, 1))
            if k in (1, 2, 3):
                scale_x(Group(0, 0))
            over_groups(act, step)
            barrier(act, 2 + 2 * k)

        @block.scalar
        def _(act):
            for i, (left, right, cols) in enumerate(comp_parts):
                act.wait_ge(s_comp_mm, i + 1)
                acc = psum[:, i, :]
                nc.scalar.mul(comp[0:S, comp_at[i]:comp_at[i] + cols], acc[0:S, 0:cols], C_X / 4)
                nc.scalar.mul(comp[S:S + V, comp_at[i]:comp_at[i] + cols], acc[S:S + V, 0:cols],
                              C_X / 4 * (r3 if cols == S else 1.0)).then_inc(s_comp, 1)
            barrier(act, 1)
            act_node(act, 0)
            for l in range(LAYERS):
                act_edge(act, l)
                act_node(act, l + 1)

        def pe_edge(pe, l):
            key = ("edge", l)
            nk, ns, width = OUT_V[l], OUT_S[l], WIDTH[l]

            def hide(g):
                b = g.odd
                pe.wait_ge(front_in[b].sem, front_in[b].at(key, g.half + 1))
                pe.wait_ge(wide_copied.sem, wide_copied.at(key, hide_use(l, g.n) - 1))
                settle(pe)
                nc.tensor.matmul(psum[0:FC_HID[l], hide_bank(l, g), :], w(f"fc1_{l}"), edge_feat[b][0:FC_IN[l], :],
                                 start=True, stop=True).then_inc(wide_mm.sem, 1)

            def weigh(g):
                b = g.odd
                pe.wait_ge(wide_copied.sem, wide_copied.at(key, hide_use(l, g.n) + 1))
                pe.wait_ge(message_made.sem, message_made.at(key, g.n))
                settle(pe)
                cols = REGIONS[f"w_{l}"][2]
                for t in range(TILES):
                    at = t % 2 * (GROUP // 2)
                    last = nc.tensor.matmul(psum[:, WEIGHT[t // 2], at:at + cols], hidden[b][0:FC_HID[l], t * P:(t + 1) * P],
                                            w(f"w_{l}"), start=True, stop=True, skip_group_check=True)
                last.then_inc(weighed.sem, 1)

            def turn(g):
                b = g.odd
                for i, rows in enumerate(BLOCKS[l]):
                    if i == 0:
                        pe.wait_ge(message_made.sem, message_made.at(key, g.n + 1))
                    pe.wait_ge(wide_copied.sem, wide_copied.at(key, block_use(l, g, i) - 1))
                    for t in range(TILES):
                        last = nc.tensor.transpose(psum[0:rows, block_bank(l, g, i), t * P:(t + 1) * P],
                                                   weighted[b][:, t, i * P:i * P + rows], ident)
                    last.then_inc(wide_mm.sem, 1)

            def output(g):
                b = g.odd
                if CROSS[l]:
                    pieces = ((0, 0, 3 * nk), (1, 3 * nk, nk + ns), (2, nk, 3 * nk))
                else:
                    pieces = ((1, 0, width - (l == 1)), (0, 3 * nk, ns + nk))
                for t in range(TILES):
                    n = g.n * TILES + t
                    if t == 0:
                        pe.wait_ge(wide_copied.sem, wide_copied.at(key, block_use(l, g, len(BLOCKS[l]) - 1) + 1))
                    pe.wait_ge(msg_copied.sem, msg_copied.at(key, n - 1))
                    for j, (i, at, number) in enumerate(pieces):
                        last = nc.tensor.matmul(psum[:, MSG[t % 2], at:at + number],
                                                message[b][i][0:BLOCKS[l][i], t * P:(t + 1) * P],
                                                w(f"out{i}_{l}", c1=number), start=j == 0, stop=j == len(pieces) - 1,
                                                skip_group_check=True)
                    last.then_inc(msg_mm.sem, 1)

            def sum_same(g):
                b = g.odd
                for t in range(TILES):
                    n = g.n * TILES + t
                    if t == 0:
                        pe.wait_ge(outer_added.sem, outer_added.at(key, g.n + 1))
                        pe.wait_ge(same_made.sem, same_made.at(key, g.n + 1))
                    pe.wait_ge(sum_copied.sem, sum_copied.at(key, n - 1))
                    to = psum[:, SUM[t % 2], 0:width]
                    last = nc.tensor.matmul(to, same[b][:, t, :], edge_out[b][:, t, V_AT[l]:V_AT[l] + width],
                                            start=True, stop=t % 2 == 1)
                    if t % 2 == 0:
                        last = nc.tensor.matmul(to, same[b][:, TILES + t // 2, :], edge_out[b][:, t + 1, V_AT[l]:V_AT[l] + width],
                                                start=False, stop=True)
                    last.then_inc(sum_mm.sem, 1)

            def step(g, has_back, has_it, has_ahead):
                if has_ahead:
                    hide(g.ahead())
                if has_back:
                    output(g.back())
                if has_ahead:
                    weigh(g.ahead())
                if has_it:
                    turn(g)
                if has_back:
                    sum_same(g.back())

            hide(Group(0, 0))
            weigh(Group(0, 0))
            over_groups(pe, step)
            barrier(pe, 3 + 2 * l)

        def pe_node(pe, k):
            key = ("node", k)

            def turn(g):
                b = g.odd
                if k == 0:
                    pe.wait_ge(node_in[b].sem, node_in[b].at(key, g.half + 1))
                elif k == 3:
                    pe.wait_ge(normed.sem, normed.at(key, g.n + 1))
                else:
                    pe.wait_ge(scaled.sem, scaled.at(key, g.n + 1))
                pe.wait_ge(x_copied.sem, x_copied.at(key, g.n))
                for path in range(PATHS[k]):
                    x = x_scaled[path][b] if k in (1, 2) else x_new[b]
                    for t in range(TILES):
                        cols = slice(t * P, (t + 1) * P)
                        nc.tensor.transpose(psum[0:3 * V, 2 * path, cols], x[:, t, 0:3 * V], ident)
                        last = nc.tensor.transpose(psum[0:S, 2 * path + 1, cols], x[:, t, 3 * V:HROW], ident)
                last.then_inc(x_turned.sem, 1)

            def linear(g, pairs):
                b = g.odd
                if 0 in pairs:
                    pe.wait_ge(x_copied.sem, x_copied.at(key, g.n + 1))
                for pair in pairs:
                    if ACT_PAIRS[k] == 2:
                        pe.wait_ge(lin_act.sem, lin_act.at_pair(key, g.n - 1, pair))
                    elif pair == 0:
                        pe.wait_ge(lin_act.sem, lin_act.at(key, g.n))
                    else:
                        pe.wait_ge(lin_dve.sem, lin_dve.at(key, g.n))
                    for t in (2 * pair, 2 * pair + 1):
                        cols = slice(t * P, (t + 1) * P)
                        for at, src, rows, kind, width in ((0, v_cols, 3 * V, "nv", 6 * V),
                                                           (6 * V, s_cols, S, "ns", S + SKIP_S[k])):
                            for path in range(PATHS[k]):
                                last = nc.tensor.matmul(psum[:, 4 + t, at:at + width], src[path][b][0:rows, cols],
                                                        w(f"{kind}{'ac'[path]}_{k}"), start=path == 0,
                                                        stop=path == PATHS[k] - 1, skip_group_check=True)
                    last.then_inc(lin_mm.sem, 1)

            def step(g, has_back, has_it, has_ahead):
                if k == LAYERS:
                    return
                if k == 1:
                    if has_back:
                        linear(g.back(), (0, 1))
                    if has_it:
                        turn(g)
                else:
                    if has_back:
                        linear(g.back(), (0,))
                    if has_it:
                        turn(g)
                    if has_back:
                        linear(g.back(), (1,))

            over_groups(pe, step)
            barrier(pe, 2 + 2 * k)

        @block.tensor
        def _(pe):
            pe.wait_ge(s_const, 32)
            for i, (left, right, cols) in enumerate(comp_parts):
                nc.tensor.matmul(psum[0:S + V, i, 0:cols], w(left), w(right), start=True, stop=True)\
                  .then_inc(s_comp_mm, 1)
            barrier(pe, 1)
            pe_node(pe, 0)
            for l in range(LAYERS):
                pe_edge(pe, l)
                pe_node(pe, l + 1)


def pack_weights(i):
    def l_(layer, name):
        return np.asarray(i[f"L{layer}_gnn_{name}"])

    def diag(m):
        out = np.zeros((3 * m.shape[0], 3 * m.shape[1]), np.float32)
        for c in range(3):
            out[c * m.shape[0]:(c + 1) * m.shape[0], c * m.shape[1]:(c + 1) * m.shape[1]] = m
        return out

    fc1 = [l_(0, "W_fc1"), l_(1, "Wfc1"), l_(2, "W_fc1"), l_(3, "fc_w1")]
    fc2 = [l_(0, "W_fc2"), l_(1, "Wfc2"), l_(2, "W_fc2"), l_(3, "fc_w2")]
    out_s = [l_(0, "W_out_s"), np.concatenate([l_(1, "Wl2_s"), l_(1, "Wa"), np.zeros((S + V, 1), np.float32)], 1),
             None, l_(3, "lin2_ws")]
    out_v = [l_(0, "W_out_v"), l_(1, "Wl2_v"), None, l_(3, "lin2_wv")]
    skip = {"a_0": ("W_skip0", "W_skip1", "W_nl0", "W_nl1"), "a_1": ("Wsc0", "Wsc1", "Wl1_0", "Wl1_1"),
            "a_2": ("Ws_sc_a", "Wv_sc_a", "Ws_l1_a", "Wv_l1_a"), "c_2": ("Ws_sc_c", "Wv_sc_c", "Ws_l1_c", "Wv_l1_c"),
            "a_3": ("sc_ws", "sc_wv", "lin1_ws", "lin1_wv")}
    m = {}
    for l in range(LAYERS):
        f = fc2[l]
        m[f"fc1_{l}"] = fc1[l]
        dot, cross = f[:, 2 * S + V:2 * S + 2 * V], f[:, 2 * S + 2 * V:]
        m[f"w_{l}"] = np.concatenate([f[:, S:2 * S], f[:, 0:S], f[:, 2 * S:2 * S + V], cross, dot], 1)
        ns, nk = OUT_S[l], OUT_V[l]
        if CROSS[l]:
            m[f"out0_{l}"], m[f"out1_{l}"] = np.zeros((P, 3 * nk), np.float32), np.zeros((P, nk + ns), np.float32)
            m[f"out0_{l}"][0:S, 0:nk] = out_v[l][0:S]
            m[f"out0_{l}"][S:S + V, nk:2 * nk] = out_v[l][S + V:]
            m[f"out0_{l}"][S + V:, 2 * nk:] = out_v[l][S + V:]
            m[f"out1_{l}"][0:S, nk:] = out_s[l][0:S]
            m[f"out1_{l}"][S:S + V, 0:nk] = out_v[l][S + V:]
            m[f"out1_{l}"][S + V:, nk:] = out_s[l][S:]
            m[f"out2_{l}"] = diag(out_v[l][S:S + V])
        elif l == 1:
            m["out0_1"], m["out1_1"] = np.zeros((P, ns + nk), np.float32), np.zeros((P, 3 * nk + ns), np.float32)
            m["out0_1"][S:, 0:ns] = out_s[l][0:S]
            m["out0_1"][0:S, ns:] = out_v[l][0:S]
            m["out1_1"][0:3 * V, 0:3 * nk] = diag(out_v[l][S:S + V])
            m["out1_1"][3 * V:, 3 * nk:] = out_s[l][S:]
    for key, (ss, sv, hs, hv) in skip.items():
        layer = int(key[-1])
        m[f"nv{key}"] = np.concatenate([diag(l_(layer, sv)), diag(l_(layer, hv))], 1)
        m[f"ns{key}"] = np.concatenate([l_(layer, hs), l_(layer, ss)], 1)
    m["lsa"], m["lsc"] = l_(2, "Ws_l2_a").T, l_(2, "Ws_l2_c").T
    m["lva"], m["lvc"] = l_(2, "Wv_l2_a").T, l_(2, "Wv_l2_c").T
    m["l3s"], m["l3v"] = l_(2, "Ws_l3"), l_(2, "Wv_l3")
    packed = np.zeros((P, WCOLS), np.float32)
    for name, a in m.items():
        at, rows, cols = REGIONS[name]
        assert a.shape == (rows, cols), (name, a.shape, rows, cols)
        packed[0:rows, at:at + cols] = a
    return packed


def lay_out(i):
    def padded(a, fill):
        a = np.asarray(a)
        return np.concatenate([a, np.full((NPAD - N,) + a.shape[1:], fill, a.dtype)])

    def edge_lanes(a):
        a = a.reshape(GROUPS, TILES, P, -1)
        return np.ascontiguousarray(a.transpose(2, 0, 1, 3).reshape(P, -1))

    x = np.asarray(i["x"])
    vec = x[:, S:].reshape(N, V, 3).transpose(0, 2, 1).reshape(N, 3 * V)
    out = {"x": padded(np.concatenate([vec, x[:, 0:S]], 1), 0.0)}
    for name in ("src", "dst"):
        idx = padded(i[name], N)
        out[f"{name}_lanes"] = edge_lanes(idx)
        out[f"{name}_rows"] = idx.reshape(GROUPS, GROUP)
        out[f"{name}_loads"] = idx.reshape(GROUPS // ROW_GROUPS, ROW_GROUPS * GROUP)
    out["vec3"] = edge_lanes(padded(i["edge_attr_3"], 1.0))
    out["vec4"] = edge_lanes(padded(i["edge_attr_4"], 0.0))
    for l, name in enumerate(("edge_attr_64", "edge_attr_16", "edge_attr_10", "edge_attr_64")):
        out[f"feat{l}"] = np.ascontiguousarray(padded(i[name], 0.0).T)
    attrs = np.stack([padded(i[n], 0.0)[:, 0] for n in ("node_vec1", "node_vec1_n2", "node_vec1_n3")])
    out["attrs"] = np.ascontiguousarray(attrs.reshape(3, GROUPS, P, TILES).transpose(2, 1, 0, 3).reshape(P, -1))
    out["weights"] = pack_weights(i)
    const = np.zeros((P, 3 * P + 2), np.float32)
    const[:, 0:P] = np.eye(P)
    const[:, P:2 * P] = 1.0
    const[:, 2 * P:3 * P] = np.tril(np.ones((P, P)), -1)
    const[:, 3 * P] = NPAD + np.arange(P)
    const[:, 3 * P + 1] = NPAD + P + np.arange(P)
    out["consts"] = const
    return out


def kernel(**inputs):
    import concourse.bacc as bacc
    from concourse.bass_utils import run_bass_kernel_spmd

    nc = bacc.Bacc("TRN2", target_bir_lowering=False, num_devices=1)
    arrays = {f"in_{k}": v for k, v in lay_out(inputs).items()}
    d = {k[3:]: nc.dram_tensor(k, v.shape, mybir.dt.from_np(v.dtype), kind="ExternalInput").ap()
         for k, v in arrays.items()}
    d["out"] = nc.dram_tensor("out", [NPAD, HROW], F32, kind="ExternalOutput").ap()
    build(nc, d)
    r = run_bass_kernel_spmd(nc, [arrays], core_ids=[0])
    got = r.results[0]["out"][0:N]
    vec = got[:, 0:3 * V].reshape(N, 3, V).transpose(0, 2, 1).reshape(N, 3 * V)
    return np.concatenate([got[:, 3 * V:], vec], 1)
```
